# Optimizing a Trainium2 kernel written in Bass

```python
import numpy as np
import jax
import jax.numpy as jnp

def _softmax(x, axis=-1):
    return jax.nn.softmax(x, axis=axis)

def _gelu(x):
    return jax.nn.gelu(x, approximate=True)

def _silu(x):
    return jax.nn.silu(x)

def _sigmoid(x):
    return jax.nn.sigmoid(x)

def _layernorm(x, axis=-1, eps=1e-05):
    m = jnp.mean(x, axis=axis, keepdims=True)
    v = jnp.var(x, axis=axis, keepdims=True)
    return (x - m) / jnp.sqrt(v + eps)

def _scatter_add(tgt, idx, src, axis=0):
    return tgt.at[idx].add(src)

def _segment_sum(src, seg, n):
    return jax.ops.segment_sum(src, seg, n)
kernel_name = 'mk_conv_preact_d4_conv_nchw256_r4_035449'

def setup_inputs(seed: int=0):
    np.random.seed(seed)
    _w = jnp.asarray

    def _rec_inputs():
        import jax
        import jax.numpy as jnp
        _gk = jax.random.key(seed)
        x = -0.0003929 + 0.9999 * jax.random.normal(jax.random.fold_in(_gk, 1), (16, 64, 16, 16), jnp.float32)
        return x
    x = _rec_inputs()

    def _L0_conv_setup():
        import jax, jax.numpy as jnp
        import numpy as np

        def conv1x1(x, w, b):
            return jnp.einsum('bchw,oc->bohw', x, w) + b[None, :, None, None]

        def dwconv(x, w):
            return jax.lax.conv_general_dilated(x, w, window_strides=(1, 1), padding='SAME', dimension_numbers=('NCHW', 'OIHW', 'NCHW'), feature_group_count=x.shape[1])
        key = jax.random.key(seed)
        ks = jax.random.split(key, 14)
        B, C, H, W = (16, 64, 16, 16)
        OC = C // 16
        WSCALE = 0.05
        r = lambda k, shape: jax.random.normal(k, shape, dtype=jnp.float32) * WSCALE
        return {'x': jax.random.normal(ks[0], (B, C, H, W), dtype=jnp.float32), 'conv_w': r(ks[1], (C + 4, C)), 'conv_b': r(ks[2], (C + 4,)), 'fw3': r(ks[3], (C, 1, 3, 3)), 'fw5': r(ks[4], (C, 1, 5, 5)), 'fw7': r(ks[5], (C, 1, 7, 7)), 'key_w': r(ks[6], (1, C)), 'key_b': r(ks[7], (1,)), 'v1_w': r(ks[8], (OC, C)), 'v1_b': r(ks[9], (OC,)), 'ln_w': jnp.ones((OC,), dtype=jnp.float32), 'ln_b': jnp.zeros((OC,), dtype=jnp.float32), 'v2_w': r(ks[10], (C, OC)), 'v2_b': r(ks[11], (C,))}
    _L0_conv_all = _L0_conv_setup()
    _L0_conv_in = {k: v for k, v in _L0_conv_all.items() if k in ('conv_w', 'conv_b', 'fw3', 'fw5', 'fw7', 'key_w', 'key_b', 'v1_w', 'v1_b', 'ln_w', 'ln_b', 'v2_w', 'v2_b')}
    del _L0_conv_all

    def _L1_conv_setup():
        import jax, jax.numpy as jnp
        import numpy as np
        C = 64
        G = 8
        K = 9
        DWK = 3
        OFFSET_SCALE = 1.0
        N, H, W = (8, 16, 16)
        key = jax.random.key(seed)
        ks = jax.random.split(key, 6)

        def init(k, shape, fan):
            return jax.random.normal(k, shape, jnp.float32) * fan ** (-0.5)
        return {'x': jax.random.normal(ks[0], (N, C, H, W), jnp.float32), 'dw_w': init(ks[1], (C, 1, DWK, DWK), DWK * DWK), 'dw_b': jnp.zeros((C,), jnp.float32), 'om_w': init(ks[2], (G * K * 3, C), C) * 0.01, 'om_b': jnp.zeros((G * K * 3,), jnp.float32), 'vp_w': init(ks[3], (C, C), C), 'vp_b': jnp.zeros((C,), jnp.float32), 'op_w': init(ks[4], (C, C), C)}
    _L1_conv_all = _L1_conv_setup()
    _L1_conv_in = {k: v for k, v in _L1_conv_all.items() if k in ('dw_w', 'dw_b', 'om_w', 'om_b', 'vp_w', 'vp_b', 'op_w')}
    del _L1_conv_all

    def _L2_conv_setup():
        import jax, jax.numpy as jnp
        import numpy as np
        B, C, H, W = (2, 64, 16, 16)
        EPS = 1e-08
        key = jax.random.key(seed)
        x = jax.random.normal(key, (B, C, H, W), dtype=jnp.float32)
        return {'x': x}
    _L2_conv_all = _L2_conv_setup()
    _L2_conv_in = {k: v for k, v in _L2_conv_all.items() if k in ()}
    del _L2_conv_all

    def _L3_conv_setup():
        import jax, jax.numpy as jnp
        import numpy as np
        from functools import partial
        B, C_IN, C_OUT, K, H, W = (32, 64, 64, 3, 56, 56)
        STRIDE, PAD = (1, 1)

        @jax.custom_vjp
        def sign_ste(x):
            return jnp.where(x > 0, 1.0, -1.0).astype(x.dtype)

        def _sign_fwd(x):
            return (sign_ste(x), x)

        def _sign_bwd(x, g):
            return (g * (jnp.abs(x) <= 1).astype(g.dtype),)
        sign_ste.defvjp(_sign_fwd, _sign_bwd)
        key = jax.random.key(seed)
        k_x, k_w = jax.random.split(key)
        x = jax.random.normal(k_x, (B, C_IN, H, W), dtype=jnp.float32)
        fan_in = C_IN * K * K
        bound = 1.0 / np.sqrt(fan_in)
        weight = jax.random.uniform(k_w, (C_OUT, C_IN, K, K), dtype=jnp.float32, minval=-bound, maxval=bound)
        alpha = jnp.zeros((C_IN, 1, 1), dtype=jnp.float32)
        return {'x': x, 'alpha': alpha, 'weight': weight}
    _L3_conv_all = _L3_conv_setup()
    _L3_conv_in = {k: v for k, v in _L3_conv_all.items() if k in ('alpha', 'weight')}
    del _L3_conv_all
    return {'x': x, 'L0_conv_conv_w': _L0_conv_in['conv_w'], 'L0_conv_conv_b': _L0_conv_in['conv_b'], 'L0_conv_fw3': _L0_conv_in['fw3'], 'L0_conv_fw5': _L0_conv_in['fw5'], 'L0_conv_fw7': _L0_conv_in['fw7'], 'L0_conv_key_w': _L0_conv_in['key_w'], 'L0_conv_key_b': _L0_conv_in['key_b'], 'L0_conv_v1_w': _L0_conv_in['v1_w'], 'L0_conv_v1_b': _L0_conv_in['v1_b'], 'L0_conv_ln_w': _L0_conv_in['ln_w'], 'L0_conv_ln_b': _L0_conv_in['ln_b'], 'L0_conv_v2_w': _L0_conv_in['v2_w'], 'L0_conv_v2_b': _L0_conv_in['v2_b'], 'L1_conv_dw_w': _L1_conv_in['dw_w'], 'L1_conv_dw_b': _L1_conv_in['dw_b'], 'L1_conv_om_w': _L1_conv_in['om_w'], 'L1_conv_om_b': _L1_conv_in['om_b'], 'L1_conv_vp_w': _L1_conv_in['vp_w'], 'L1_conv_vp_b': _L1_conv_in['vp_b'], 'L1_conv_op_w': _L1_conv_in['op_w'], 'L3_conv_alpha': _L3_conv_in['alpha'], 'L3_conv_weight': _L3_conv_in['weight']}

def reference(x, L0_conv_conv_w, L0_conv_conv_b, L0_conv_fw3, L0_conv_fw5, L0_conv_fw7, L0_conv_key_w, L0_conv_key_b, L0_conv_v1_w, L0_conv_v1_b, L0_conv_ln_w, L0_conv_ln_b, L0_conv_v2_w, L0_conv_v2_b, L1_conv_dw_w, L1_conv_dw_b, L1_conv_om_w, L1_conv_om_b, L1_conv_vp_w, L1_conv_vp_b, L1_conv_op_w, L3_conv_alpha, L3_conv_weight):
    import jax
    import jax.numpy as jnp

    def _L0_conv_ref(x, conv_w, conv_b, fw3, fw5, fw7, key_w, key_b, v1_w, v1_b, ln_w, ln_b, v2_w, v2_b):
        import jax, jax.numpy as jnp
        import numpy as np

        def conv1x1(x, w, b):
            return jnp.einsum('bchw,oc->bohw', x, w) + b[None, :, None, None]

        def dwconv(x, w):
            return jax.lax.conv_general_dilated(x, w, window_strides=(1, 1), padding='SAME', dimension_numbers=('NCHW', 'OIHW', 'NCHW'), feature_group_count=x.shape[1])
        B, C, H, W = x.shape
        t = conv1x1(x, conv_w, conv_b)
        ctx, gates = (t[:, :C], t[:, C:])
        ctx_all = jnp.zeros_like(ctx)
        for l, fw in enumerate((fw3, fw5, fw7)):
            ctx = jax.nn.gelu(dwconv(ctx, fw), approximate=False)
            ctx_all = ctx_all + ctx * gates[:, l:l + 1]
        ctx_global = jnp.mean(ctx, axis=(2, 3), keepdims=True)
        ctx_all = ctx_all + ctx_global * gates[:, 3:4]
        k = conv1x1(ctx_all, key_w, key_b).reshape(B, H * W)
        k = jax.nn.softmax(k, axis=1)
        q = ctx_all.reshape(B, C, H * W)
        qk = jnp.einsum('bcn,bn->bc', q, k)[:, :, None, None]
        v = conv1x1(qk, v1_w, v1_b)
        mu = jnp.mean(v, axis=(1, 2, 3), keepdims=True)
        var = jnp.var(v, axis=(1, 2, 3), keepdims=True)
        v = (v - mu) * jax.lax.rsqrt(var + 1e-05)
        v = v * ln_w[None, :, None, None] + ln_b[None, :, None, None]
        v = jax.nn.relu(v)
        v = conv1x1(v, v2_w, v2_b)
        return ctx_all + v

    def _L1_conv_ref(x, dw_w, dw_b, om_w, om_b, vp_w, vp_b, op_w):
        import jax, jax.numpy as jnp
        import numpy as np
        C = 64
        G = 8
        K = 9
        DWK = 3
        OFFSET_SCALE = 1.0
        N, H, W = (8, 16, 16)
        n, c, h, w = x.shape
        cg = c // G
        L = h * w
        xf = x.transpose(0, 2, 3, 1).reshape(n, L, c)
        value = (xf @ vp_w.T + vp_b).reshape(n, L, G, cg)
        om_in = jax.lax.conv_general_dilated(x, dw_w, (1, 1), 'SAME', feature_group_count=c, dimension_numbers=('NCHW', 'OIHW', 'NCHW')) + dw_b[None, :, None, None]
        om = om_in.transpose(0, 2, 3, 1).reshape(n, L, c) @ om_w.T + om_b
        om = om.reshape(n, h, w, G, K * 3)
        off = om[..., :2 * K].reshape(n, h, w, G, K, 2) * OFFSET_SCALE
        mask = om[..., 2 * K:]
        d = jnp.arange(-1, 2, dtype=jnp.float32)
        dy, dx = jnp.meshgrid(d, d, indexing='ij')
        base = jnp.stack([dy.ravel(), dx.ravel()], -1)
        py = jnp.arange(h, dtype=jnp.float32).reshape(1, h, 1, 1, 1) + base[:, 0].reshape(1, 1, 1, 1, K) + off[..., 0]
        px = jnp.arange(w, dtype=jnp.float32).reshape(1, 1, w, 1, 1) + base[:, 1].reshape(1, 1, 1, 1, K) + off[..., 1]
        y0 = jnp.floor(py)
        x0 = jnp.floor(px)
        ty = py - y0
        tx = px - x0
        y0i = y0.astype(jnp.int32)
        x0i = x0.astype(jnp.int32)

        def gather(yi, xi, wgt):
            valid = (yi >= 0) & (yi < h) & (xi >= 0) & (xi < w)
            idx = jnp.clip(yi, 0, h - 1) * w + jnp.clip(xi, 0, w - 1)
            idx = idx.transpose(0, 1, 2, 4, 3).reshape(n, L * K, G)[..., None]
            g = jnp.take_along_axis(value, idx, axis=1)
            g = g.reshape(n, h, w, K, G, cg).transpose(0, 1, 2, 4, 3, 5)
            return g * (wgt * valid)[..., None]
        sampled = gather(y0i, x0i, (1 - ty) * (1 - tx)) + gather(y0i, x0i + 1, (1 - ty) * tx) + gather(y0i + 1, x0i, ty * (1 - tx)) + gather(y0i + 1, x0i + 1, ty * tx)
        out = jnp.einsum('nhwgk,nhwgkc->nhwgc', mask, sampled)
        out = out.reshape(n, L, c) @ op_w.T
        return out.reshape(n, h, w, c).transpose(0, 3, 1, 2)

    def _L2_conv_ref(x):
        import jax, jax.numpy as jnp
        import numpy as np
        B, C, H, W = (2, 64, 16, 16)
        EPS = 1e-08
        Bs, Cs, Hs, Ws = x.shape
        N = Bs * Hs * Ws
        X = x.reshape(Cs, N).T
        b, h, w = jnp.meshgrid(jnp.arange(Bs), jnp.arange(Hs), jnp.arange(Ws), indexing='ij')
        cb, ch, cw = (b.ravel(), h.ravel(), w.ravel())
        dist = jnp.abs(cb[:, None] - cb[None, :]) + jnp.abs(ch[:, None] - ch[None, :]) + jnp.abs(cw[:, None] - cw[None, :])
        A = (dist == 1).astype(X.dtype) + jnp.eye(N, dtype=X.dtype)
        nrm = jnp.maximum(jnp.sqrt(jnp.sum(X * X, axis=1)), EPS)
        sim = X @ X.T / (nrm[:, None] * nrm[None, :])
        m = (A + sim) * 0.5
        d = jnp.exp(jnp.diagonal(m) - jax.nn.logsumexp(m, axis=1))
        out = jax.nn.relu(X * d[:, None])
        return out.reshape(Bs, Cs, Hs, Ws)

    def _L3_conv_ref(x, alpha, weight):
        import jax, jax.numpy as jnp
        import numpy as np
        from functools import partial
        B, C_IN, C_OUT, K, H, W = (32, 64, 64, 3, 56, 56)
        STRIDE, PAD = (1, 1)

        @jax.custom_vjp
        def sign_ste(x):
            return jnp.where(x > 0, 1.0, -1.0).astype(x.dtype)

        def _sign_fwd(x):
            return (sign_ste(x), x)

        def _sign_bwd(x, g):
            return (g * (jnp.abs(x) <= 1).astype(g.dtype),)
        sign_ste.defvjp(_sign_fwd, _sign_bwd)
        a_bin = sign_ste(x - alpha[None])
        w_bin = sign_ste(weight)
        out = jax.lax.conv_general_dilated(a_bin, w_bin, window_strides=(STRIDE, STRIDE), padding=((PAD, PAD), (PAD, PAD)), dimension_numbers=('NCHW', 'OIHW', 'NCHW'))
        return out

    def _gn(v, G=32, eps=1e-05):
        B_, C_, H_, W_ = v.shape
        g = v.reshape(B_, G, C_ // G, H_, W_)
        m = jnp.mean(g, axis=(2, 3, 4), keepdims=True)
        s = jnp.var(g, axis=(2, 3, 4), keepdims=True)
        return ((g - m) / jnp.sqrt(s + eps)).reshape(v.shape)

    def _ln_c(v, eps=1e-06):
        m = jnp.mean(v, axis=1, keepdims=True)
        s = jnp.var(v, axis=1, keepdims=True)
        return (v - m) / jnp.sqrt(s + eps)

    def _ln_t(v, eps=1e-05):
        m = jnp.mean(v, axis=-1, keepdims=True)
        s = jnp.var(v, axis=-1, keepdims=True)
        return (v - m) / jnp.sqrt(s + eps)

    def _to_tokens(v):
        B_, C_, H_, W_ = v.shape
        return v.reshape(B_, C_, H_ * W_).transpose(0, 2, 1)

    def _from_tokens(t, like):
        B_, C_, H_, W_ = like.shape
        return t.transpose(0, 2, 1).reshape(B_, C_, H_, W_)
    x = x + _L0_conv_ref(_gn(x), L0_conv_conv_w, L0_conv_conv_b, L0_conv_fw3, L0_conv_fw5, L0_conv_fw7, L0_conv_key_w, L0_conv_key_b, L0_conv_v1_w, L0_conv_v1_b, L0_conv_ln_w, L0_conv_ln_b, L0_conv_v2_w, L0_conv_v2_b)
    x = x + _L1_conv_ref(_gn(x), L1_conv_dw_w, L1_conv_dw_b, L1_conv_om_w, L1_conv_om_b, L1_conv_vp_w, L1_conv_vp_b, L1_conv_op_w)
    x = x + _L2_conv_ref(_gn(x))
    x = x + _L3_conv_ref(_gn(x), L3_conv_alpha, L3_conv_weight)
    return x

_drawn_inputs = setup_inputs


def setup_inputs(seed=0):
    import zlib

    import numpy as np

    out = dict(_drawn_inputs(seed))
    spreads = {'L0_conv_ln_w': (1.0, 0.2),
     'L0_conv_ln_b': (0.0, 0.1),
     'L1_conv_dw_b': (0.0, 0.1),
     'L1_conv_om_b': (0.0, 0.1),
     'L1_conv_vp_b': (0.0, 0.1),
     'L3_conv_alpha': (0.0, 0.1)}
    factors = {'L0_conv_fw7': 4.393, 'L0_conv_key_w': 53.319, 'L0_conv_v1_w': 2.883}
    for name, (base, spread) in spreads.items():
        noise = np.random.default_rng([zlib.crc32(name.encode()), seed]).standard_normal(out[name].shape)
        drawn = base * np.exp(spread * noise) if base else spread * noise
        out[name] = jnp.asarray(drawn.astype(out[name].dtype))
    for name, factor in factors.items():
        out[name] = (out[name] * factor).astype(out[name].dtype)
    return out
```

```python
from contextlib import ExitStack

import concourse.bass as bass
from concourse import mybir

F32 = mybir.dt.float32
F16 = mybir.dt.float16
BF16 = mybir.dt.bfloat16
I32 = mybir.dt.int32
ALU = mybir.AluOpType
ACT = mybir.ActivationFunctionType
AX = mybir.AxisListType

B, C, HW, PX = 16, 64, 16, 256
P = 128
FULL = B * C * PX // P
NQ, N4 = 4, 4
G, C4, C2 = 8, 4, 2
TAPS = 9
MAPS = 27
NODE_BLOCKS = 32
REACH = 16
ARENA = 34816
SPLIT = 256.0
GN_EPS = 1e-5

SX_V1, SX_V2B, SX_DWB, SX_KEY, SX_N = 0, 32, 40, 48, 56


def bass_preact_convs(nc, x, toep3, toep5, toep7, toepd, pw0, pw1, pw2, bias_n, small_x, key_b,
                      row_n, v2_w, alpha, sign_w, out):
    scratch_hat = nc.dram_tensor("scratch_hat", (B * C * PX,), F32, kind="Internal").ap()
    scratch_x2 = nc.dram_tensor("scratch_x2", (B * C * PX,), F32, kind="Internal").ap()
    scratch_x3 = nc.dram_tensor("scratch_x3", (B * C * PX,), F32, kind="Internal").ap()

    ctx = ExitStack()
    with ctx:
        def sb(name, cols, dt=F32):
            return ctx.enter_context(nc.sbuf_tensor(name, [P, cols], dt))[:, :]

        def view(t, col, dims, p0=0, n=P):
            row = t.ap[0][0]
            return bass.AP(t.tensor, t.offset + p0 * row + col, [[row, n]] + [list(d) for d in dims])

        def dram(t, off, dims):
            return bass.AP(t.tensor, t.offset + off, [list(d) for d in dims])

        sems = {}

        def sem(name):
            if name not in sems:
                sems[name] = ctx.enter_context(nc.semaphore(name))
            return sems[name]

        xs = sb("xs", FULL)
        ident = sb("ident", P)
        fold4 = sb("fold4", N4)
        fold16 = sb("fold16", HW)
        mean256 = sb("mean256", P)
        ones = sb("ones", P)
        pair_mean = sb("pair_mean", P)
        eighth = sb("eighth", 1)
        xcol = sb("xcol", 1)
        valid = sb("valid", 5)
        nvalid = sb("nvalid", 5)
        iota_x = sb("iota_x", HW)
        scr16 = sb("scr16", HW)
        adj = sb("adj", 3 * P)
        adj16 = sb("adj16", 6 * P, F16)
        adj_last = sb("adj_last", 2 * P, F16)
        ident16 = sb("ident16", P, F16)
        identS = sb("identS", P, F16)
        raw0, raw1, raw2 = sb("raw0", 192), sb("raw1", 640), sb("raw2", 128)
        k1 = sb("k1", 2560)
        k2 = sb("k2", 512)
        sN = sb("sN", 13)
        sX = sb("sX", SX_N)
        keyb = sb("keyb", 1)
        rowN = sb("rowN", 12)
        v2raw = sb("v2raw", 64)
        alphaT = sb("alphaT", 1)
        minus_one, half, eps = sb("minus_one", 1), sb("half", 1), sb("eps", 1)
        ytile = sb("ytile", 2 * PX)
        rot1 = sb("rot1", P)
        stats = sb("stats", 8 * 6)
        mv = sb("mv", 16)
        rstd = sb("rstd", 8)

        arena = sb("arena", ARENA)

        def cut(lo, n):
            assert lo + n <= ARENA
            return arena[:, lo:lo + n]

        wt3, wt5, wt7 = cut(0, 3072), cut(3072, 5120), cut(8192, 7168)
        wtd = cut(30976, 3072)
        k0 = cut(34048, 768)
        xh = cut(15360, FULL)
        tN, tX = cut(17408, FULL), cut(19456, FULL)
        gN, gX = cut(21504, 1024), cut(28928, FULL)
        v2k, keyk = cut(21504, G * P), cut(15360, G * P)
        ctxs = [cut(22528, FULL), cut(24576, FULL), cut(26624, FULL)]
        ctx_all = cut(17408, FULL)
        tmp = cut(19456, FULL)
        tmpg = cut(28672, PX)
        small = sb("small", 1200)
        R3 = small[:, 0:128]
        kS, kC, kE = small[:, 128:384], small[:, 384:640], small[:, 640:896]
        kmax, Ey, Rq = small[:, 896:912], small[:, 912:928], small[:, 928:1056]
        vadd = small[:, 1056:1184]
        sm = sb("sm", 64)
        gmax, diag, vrow, vT = sm[:, 0:1], sm[:, 1:17], sm[:, 17:21], sm[:, 21:37]
        vst, vmv, vrs, rden = sm[:, 37:43], sm[:, 43:45], sm[:, 45:46], sm[:, 46:47]
        over, flagf = sm[:, 47:49], sm[:, 49:50]
        oversum = sm[:, 50:51]
        flag = sb("flag", 1, I32)

        omX = cut(0, 32 * PX)
        vsh = [cut(8192 + b * 2560, 2560) for b in range(5)]
        hx = cut(20992, 3 * TAPS * PX)
        hy = cut(27904, 3 * TAPS * PX)
        xh1, xX, dwX = cut(20992, FULL), cut(23040, FULL), cut(25088, FULL)
        turns = sb("turns", 3 * FULL)
        dN = turns[:, 0:FULL]
        omN = [turns[:, FULL:2 * FULL], turns[:, 2 * FULL:3 * FULL]]
        nmask = turns[:, 0:TAPS * PX]
        ring = [turns[:, c:c + 1024] for c in (2304, 3328, 4352, 0)]
        A = sb("A", 5 * PX)
        fold = [cut(0, TAPS * PX), cut(TAPS * PX, TAPS * PX)]
        oN = dN

        X64 = cut(0, 4096)
        XT, xx = cut(4096, 2048), cut(6144, 2048)
        sq = cut(8192, 2048)
        hm = cut(10240, 4096).bitcast(F16)
        wraw, wsgn = cut(12400, TAPS * P), cut(13600, 576).bitcast(BF16)
        HM = cut(14336, 2048).bitcast(F16)
        HH = cut(16384, 3072).bitcast(F16)
        MM = cut(19456, 3072).bitcast(F16)
        colacc = cut(22528, 48 * P)
        E = [cut(28672, 2048), cut(30720, 2048), cut(32768, 2048)]
        x2R = omN[0]
        xh2 = dN
        n2, rs = small[:, 0:32], small[:, 32:64]
        rowsum, row16, Ssum, dexp = small[:, 64:96], small[:, 96:128], small[:, 128:160], small[:, 160:192]
        rsS, simii = small[:, 192:224], small[:, 224:256]
        o2, x3R = cut(0, 2048), cut(2048, 2048)

        x3N = cut(4096, 2048)
        sgn = cut(6144, 2048)
        apad = cut(8192, 1296).bitcast(BF16)
        yout = cut(10240, 2048)
        pstat = small[:, 256:272]
        pavg = small[:, 272:288]
        pvar = small[:, 288:296]

        ps = ctx.enter_context(nc.psum_tensor("ps", [P, 4096], F32))[:, :]

        def bank(b, n=512):
            return ps[:, b * 512:b * 512 + n]

        def turned(q, which):
            return bank((3 * q + which) % 8).bitcast(F16)

        free_turned = [[("HHMM", 1)], [("HM", 1)], [("HHMM", 2)], [("HHMM", 3)]]
        conv_order = [(l, i - l) for i in range(G + 2) for l in range(3) if 0 <= i - l < G]

        def to_rows_in(t, nq):
            return view(t, nq * 512, [(HW, HW), (PX, C2), (1, HW)])

        def cols(t, base, slot, nq):
            return view(t, base + nq, [(HW, HW), (slot, 8), (NQ, N4)])

        W = TAPS * PX
        Vd = cut(8192, 4096)
        acc, term = cut(15872, FULL), cut(18432, FULL)
        hxS, hyS, prS = hx[:, 0:W], hy[:, 0:W], hy[:, W:2 * W]
        xprime, wrapped = sb("xprime", 1), sb("wrapped", 1)

        def slow_vector(dve):
            def settle():
                dve.drain()

            dve.wait_ge(sem("iota_ready"), 2)
            for d in range(3):
                px = view(omX, (TAPS + d) * PX, [(3 * PX, 3), (1, PX)])
                dve.tensor_scalar(px, px, xcol[:, 0:1], float(d - 1), ALU.add, ALU.add)
                py = view(omX, 3 * d * PX, [(PX, 3), (1, PX)])
                dve.scalar_tensor_tensor(out=py, in0=py, scalar=float(d - 1), in1=view(ytile, 0, [(0, 3), (1, PX)]),
                                         op0=ALU.add, op1=ALU.add)
            PY, PXc, mask = omX[:, 0:W], omX[:, W:2 * W], omX[:, 2 * W:3 * W]
            dve.tensor_copy(xprime, xcol)
            dve.memset(acc, 0.0)
            for rows in range(2):
                dve.tensor_copy(view(Vd, rows * PX, [(2 * PX, 8), (1, PX)]),
                                view(vsh[2], 2 * HW, [(320, 8), (1, PX)]))
            settle()
            with dve.Fori(0, HW) as r:
                dve.tensor_scalar(hxS, PXc, xprime[:, 0:1], None, ALU.subtract)
                settle()
                dve.scalar_tensor_tensor(out=hxS, in0=hxS, scalar=-1.0, in1=hxS, op0=ALU.mult, op1=ALU.min)
                settle()
                dve.tensor_scalar(hxS, hxS, 1.0, 0.0, ALU.add, ALU.max)
                dve.tensor_scalar(wrapped, xprime, float(HW - 1), -float(HW), ALU.is_ge, ALU.mult)
                settle()
                dve.scalar_tensor_tensor(out=xprime, in0=xprime, scalar=1.0, in1=wrapped, op0=ALU.add, op1=ALU.add)
                with dve.Fori(0, HW) as s:
                    ys = ytile[:, bass.ds(s * HW, PX)]
                    for k in range(TAPS):
                        dve.tensor_tensor(out=hyS[:, k * PX:(k + 1) * PX], in0=PY[:, k * PX:(k + 1) * PX], in1=ys,
                                          op=ALU.subtract)
                    settle()
                    dve.scalar_tensor_tensor(out=hyS, in0=hyS, scalar=-1.0, in1=hyS, op0=ALU.mult, op1=ALU.min)
                    settle()
                    dve.tensor_scalar(hyS, hyS, 1.0, 0.0, ALU.add, ALU.max)
                    settle()
                    dve.tensor_tensor(out=hyS, in0=hyS, in1=mask, op=ALU.mult)
                    settle()
                    dve.tensor_tensor(out=prS, in0=hyS, in1=hxS, op=ALU.mult)
                    settle()
                    dve.tensor_reduce(A[:, 0:PX], view(prS, 0, [(1, PX), (PX, TAPS)]), AX.X, ALU.add)
                    settle()
                    for ch in range(8):
                        dve.tensor_tensor(out=term[:, ch * PX:(ch + 1) * PX], in0=Vd[:, bass.ds(s * HW + ch * 2 * PX, PX)],
                                          in1=A[:, 0:PX], op=ALU.mult)
                    settle()
                    dve.tensor_tensor(out=acc, in0=acc, in1=term, op=ALU.add)
                    settle()
                dve.memset(scr16, 0.0).then_inc(sem("slow_used"), 1)
                dve.wait_ge(sem("slow_turned"), r + 1)
                for rows in range(2):
                    dve.tensor_copy(view(Vd, rows * PX, [(2 * PX, 8), (1, PX)]), view(ps, 0, [(PX, 8), (1, PX)]))
                settle()
                dve.memset(scr16, 0.0).then_inc(sem("slow_copied"), 1)
            dve.wait_ge(sem("slow_copied"), HW)
            dve.tensor_copy(ps[:, 0:FULL], acc).then_inc(sem("window_sum"), 1)

        def slow_tensor(pe):
            with pe.Fori(0, HW) as r:
                pe.wait_ge(sem("slow_used"), r + 1)
                for q in range(4):
                    ins = pe.matmul(bank(q), rot1, view(Vd, q * 4 * PX, [(2 * PX, 2), (1, PX)]), start=True, stop=True)
                ins.then_inc(sem("slow_turned"), 1)
            pe.wait_ge(sem("slow_turned"), HW)

        block = ctx.enter_context(nc.Block())

        def nat(t, c4):
            return dram(t, c4 * 512, [(2048, 8), (65536, 4), (16384, 4), (1, 512)])

        def quad(t, c4):
            return view(t, 0, [(512, 4), (1, 512)], 32 * c4, 32)

        def toeplitz(eng, wt, src, k, done):
            w = 8 * k
            for c8 in range(8):
                eng.dma_start(view(wt, c8 * 16 * w, [(1, 16 * w)], 16 * c8, 16),
                              dram(src, c8 * 256 * w, [(16 * w, 16), (1, 16 * w)])).then_inc(sem(done), 16)

        @block.sync
        def _(sp):
            for c4 in range(C4):
                sp.dma_start(quad(xs, c4), nat(x, c4)).then_inc(sem("x_in"), 16)
            sp.dma_start(raw0, dram(pw0, 0, [(192, 32), (0, 4), (1, 192)])).then_inc(sem("raw0_in"), 16)
            sp.dma_start(sN, dram(bias_n, 0, [(13, 32), (0, 4), (1, 13)])).then_inc(sem("bias_in"), 16)
            sp.wait_ge(sem("wt3_zero"), 1)
            toeplitz(sp, wt3, toep3, 3, "wt3_in")
            sp.wait_ge(sem("wt5_zero"), 1)
            toeplitz(sp, wt5, toep5, 5, "wt5_in")
            sp.wait_ge(sem("wt7_zero"), 1)
            toeplitz(sp, wt7, toep7, 7, "wt7_in")
            sp.wait_ge(sem("wtd_zero"), 1)
            toeplitz(sp, wtd, toepd, 3, "wtd_in")
            sp.dma_start(alphaT[:, :], dram(alpha, 0, [(0, 2), (1, 64)])).then_inc(sem("l3_in"), 16)
            for b in (0, 1, 3, 4):
                s = b - 2
                sp.wait_ge(sem("v0_ready"), 4)
                sp.wait_ge(sem("vsh_zero"), 5)
                lo, n = max(0, -s), P - abs(s)
                sp.dma_start(view(vsh[b], 0, [(1, 2560)], lo, n),
                             view(vsh[2], 0, [(1, 2560)], lo + s, n)).then_inc(sem("vsh_in"), 16)
            sp.wait_ge(sem("l3_in"), 16)
            sp.wait_ge(sem("x2_ready"), 4)
            for c4 in range(C4):
                sp.dma_start(nat(scratch_x2, c4), quad(xs, c4)).then_inc(sem("x2_out"), 16)
            sp.wait_ge(sem("x2_out"), 64)
            sp.dma_start(x2R, dram(scratch_x2, 0, [(64, P), (8192, 32), (1, 64)])).then_inc(sem("x2R_in"), 16)
            sp.wait_ge(sem("wraw_zero"), 1)
            for b2 in range(2):
                sp.dma_start(view(wraw, b2 * 64, [(P, TAPS), (1, 64)], 64 * b2, 64),
                             dram(sign_w, 0, [(576, 64), (64, TAPS), (1, 64)])).then_inc(sem("l3_in"), 16)
            sp.wait_ge(sem("x3_ready"), 1)
            sp.dma_start(dram(scratch_x3, 0, [(64, P), (8192, 32), (1, 64)]), x3R).then_inc(sem("x3_out"), 16)
            sp.wait_ge(sem("x3_out"), 16)
            for h in range(2):
                sp.dma_start(view(x3N, h * 1024, [(PX, 4), (1, PX)]),
                             dram(scratch_x3, h * 131072, [(PX, P), (32768, 4), (1, PX)])).then_inc(sem(f"x3N_in{h}"), 16)
            for q in range(4):
                sp.wait_ge(sem("y_ready"), q + 1)
                sp.dma_start(dram(out, q * 65536, [(PX, P), (32768, 2), (1, PX)]),
                             view(yout, q * 512, [(PX, 2), (1, PX)])).then_inc(sem("y_out"), 16)
            sp.wait_ge(sem("y_out"), 64)

        @block.gpsimd
        def _(pool):
            done = [0]

            def link(ins):
                ins.then_inc(sem("pool_step"), 1)
                done[0] += 1
                pool.wait_ge(sem("pool_step"), done[0])

            def diagonal(t, col, dims, pattern, base, mult, fill):
                v = view(t, col, dims)
                link(pool.affine_select(out=v, in_=v, compare_op=ALU.not_equal, fill=fill, base=base,
                                        pattern=pattern, channel_multiplier=mult))

            link(pool.memset(ident, 0.0))
            v = ident
            pool.affine_select(out=v, in_=v, compare_op=ALU.not_equal, fill=1.0, base=0,
                               pattern=[[-1, P]], channel_multiplier=1).then_inc(sem("ident_ready"), 1)
            pool.memset(wt5, 0.0).then_inc(sem("wt5_zero"), 1)
            pool.memset(wt7, 0.0).then_inc(sem("wt7_zero"), 1)
            pool.iota(iota_x, pattern=[[1, HW]], base=0, channel_multiplier=0,
                      allow_small_or_imprecise_dtypes=True).then_inc(sem("iota_ready"), 1)
            for t, w, value in ((mean256, 16, 1.0 / 256), (pair_mean, 2, 0.5)):
                link(pool.memset(t, value))
                v = view(t, 0, [(w, P // w), (1, w)])
                link(pool.affine_select(out=v, in_=v, compare_op=ALU.is_ge, fill=0.0, base=0,
                                        pattern=[[-w, P // w], [0, w]], channel_multiplier=1))
                last = pool.affine_select(out=v, in_=v, compare_op=ALU.is_ge, fill=0.0, base=w - 1,
                                          pattern=[[w, P // w], [0, w]], channel_multiplier=-1)
                last.then_inc(sem("means_ready"), 1)
                pool.wait_ge(sem("means_ready"), 1 if w == 16 else 2)
            pool.memset(wtd, 0.0).then_inc(sem("wtd_zero"), 1)
            pool.wait_ge(sem("fold_ready"), 2)
            pool.wait_ge(sem("smallx_in"), 16)
            pool.wait_ge(sem("l0_pw"), 6)
            pool.tensor_tensor(out=view(keyk, 0, [(P, 8), (16, 8), (1, 16)]), in0=view(fold16, 0, [(0, 8), (0, 8), (1, 16)]),
                               in1=view(sX, SX_KEY, [(1, 8), (0, 8), (0, 16)]), op=ALU.mult).then_inc(sem("keyk_ready"), 1)
            pool.wait_ge(sem("small_in"), 48)
            pool.wait_ge(sem("g_turned"), 4)
            pool.tensor_copy(view(v2k, 0, [(16, 64), (1, 16)], 0, 4),
                             view(v2raw, 0, [(1, 64), (0, 16)], 0, 4)).then_inc(sem("v2k_ready"), 1)
            pool.wait_ge(sem("raw12_in"), 32)
            pool.tensor_tensor(out=view(k1, 0, [(4, 640), (1, 4)]), in0=view(raw1, 0, [(1, 640), (0, 4)]),
                               in1=view(fold4, 0, [(0, 640), (1, 4)]), op=ALU.mult).then_inc(sem("k1_ready"), 1)
            pool.tensor_tensor(out=view(k2, 0, [(4, 128), (1, 4)]), in0=view(raw2, 0, [(1, 128), (0, 4)]),
                               in1=view(fold4, 0, [(0, 128), (1, 4)]), op=ALU.mult).then_inc(sem("k2_ready"), 1)
            for t, w, base in ((rot1[:, :], 15, -1), (rot1[:, 15:], 1, 0)):
                if w == 15:
                    link(pool.memset(rot1, 0.0))
                v = view(rot1, 15 - w if w == 1 else 0, [(16, 8), (1, w)]) if w == 15 else view(rot1, 15, [(16, 8), (1, 1)])
                link(pool.affine_select(out=v, in_=v, compare_op=ALU.not_equal, fill=1.0, base=base,
                                        pattern=[[-16, 8], [-1, w]], channel_multiplier=1))
            pool.iota(ytile, pattern=[[0, 2], [1, HW], [0, HW]], base=0, channel_multiplier=0,
                      allow_small_or_imprecise_dtypes=True).then_inc(sem("iota_ready"), 1)
            link(pool.memset(adj, 0.0))
            for d in (0, 16, -16):
                diagonal(adj, 0, [(1, P)], [[-1, P]], d, 1, SPLIT)
            diagonal(adj, 0, [(16, 8), (1, 15)], [[-16, 8], [-1, 15]], -1, 1, SPLIT)
            diagonal(adj, 1, [(16, 8), (1, 15)], [[-16, 8], [-1, 15]], 0, 1, SPLIT)
            diagonal(adj, P, [(1, P)], [[-1, P]], -112, 1, SPLIT)
            diagonal(adj, 2 * P, [(1, P)], [[-1, P]], 0, 1, SPLIT)
            for t, c, s, n in ((adj16, 0, 0, 3 * P), (adj16, 3 * P, 0, P), (adj16, 5 * P, 2 * P, P),
                               (adj_last, 0, 0, 2 * P), (identS, 0, 2 * P, P)):
                link(pool.tensor_copy(t[:, c:c + n], adj[:, s:s + n]))
            link(pool.memset(adj16[:, 4 * P:5 * P], 0.0))
            pool.tensor_copy(ident16, ident).then_inc(sem("graph_ready"), 1)
            pool.wait_ge(sem("l0_done"), 1)
            for b in range(5):
                pool.memset(vsh[b], 0.0).then_inc(sem("vsh_zero"), 1)
            pool.wait_ge(sem("window_done"), 1)
            pool.memset(colacc, 0.0).then_inc(sem("colacc_zero"), 1)
            pool.wait_ge(sem("turn_done"), 12)
            pool.memset(wraw, 0.0).then_inc(sem("wraw_zero"), 1)

        @block.scalar
        def _(act):
            act.dma_start(sX, dram(small_x, 0, [(SX_N, 8), (0, 16), (1, SX_N)])).then_inc(sem("smallx_in"), 16)
            act.dma_start(keyb, dram(key_b, 0, [(0, P), (1, 1)])).then_inc(sem("small_in"), 16)
            act.dma_start(rowN[0:16, :], dram(row_n, 0, [(0, 16), (1, 12)])).then_inc(sem("small_in"), 16)
            act.dma_start(v2raw[0:4, :], dram(v2_w, 0, [(64, 4), (1, 64)])).then_inc(sem("small_in"), 16)
            act.dma_start(raw1, dram(pw1, 0, [(640, 32), (0, 4), (1, 640)])).then_inc(sem("raw12_in"), 16)
            act.dma_start(raw2, dram(pw2, 0, [(128, 32), (0, 4), (1, 128)])).then_inc(sem("raw12_in"), 16)
            roots = [0]

            def root(dst, src, add_eps=True):
                roots[0] += 1
                act.wait_ge(sem("root_asked"), roots[0])
                act.activation(dst, src, ACT.Sqrt, bias=eps[0:dst.shape[0], :] if add_eps else 0.0).then_inc(sem("root_given"), 1)

            act.wait_ge(sem("ones_ready"), 5)
            root(rstd[:, 0:4], view(mv, 1, [(2, 4)]))
            act.wait_ge(sem("bias_in"), 16)
            for h in range(2):
                for s in range(3):
                    act.wait_ge(sem("l0_pw"), 3 * h + s + 1)
                    o = view(tN, h * 1024 + s * PX, [(512, 2), (1, PX)]) if s < 2 else \
                        view(gN, h * 512, [(PX, 2), (1, PX)])
                    act.activation(o, view(bank(3 * h + s), 0, [(PX, 2), (1, PX)]), ACT.Identity,
                                   bias=sN[:, s:s + 1]).then_inc(sem("l0_pw_bias"), 1)
            for m, (l, g) in enumerate(conv_order):
                act.wait_ge(sem("conv_done"), m + 1)
                act.activation(ctxs[l][:, g * PX:(g + 1) * PX], bank(m % 8, PX), ACT.Gelu).then_inc(sem("gelu"), 1)
            act.wait_ge(sem("key_centred"), 1)
            act.activation(kE, kC, ACT.Exp).then_inc(sem("key_exp"), 1)
            root(vrs[0:16, :], vmv[0:16, 1:2])

            root(rstd[:, 0:4], view(mv, 1, [(2, 4)]))
            for g in range(G):
                act.wait_ge(sem("dw_done"), g - g % 2 + 2)
                act.activation(dwX[:, g * PX:(g + 1) * PX], view(bank(g // 2), (g % 2) * PX, [(1, PX)]),
                               ACT.Identity, bias=sX[:, SX_DWB + g:SX_DWB + g + 1]).then_inc(sem("dw_bias"), 1)
            for s in range(2):
                for h in range(2):
                    act.wait_ge(sem("value_done"), 2 * s + h + 1)
                    act.activation(view(omN[1], h * 1024 + s * PX, [(512, 2), (1, PX)]),
                                   view(bank(4 + 2 * s + h), 0, [(PX, 2), (1, PX)]),
                                   ACT.Identity, bias=sN[:, 11 + s:12 + s]).then_inc(sem("value_bias"), 1)
            for js in range(4):
                if js == 1:
                    act.wait_ge(sem("v0_ready"), 4)
                elif js >= 2:
                    act.wait_ge(sem("maps_turned"), 4 * (js - 1))
                for s in range(2):
                    for h in range(2):
                        act.wait_ge(sem("maps_done"), 4 * js + 2 * s + h + 1)
                        act.activation(view(omN[js % 2], h * 1024 + s * PX, [(512, 2), (1, PX)]),
                                       view(bank(4 * (js % 2) + 2 * s + h), 0, [(PX, 2), (1, PX)]),
                                       ACT.Identity, bias=sN[:, 3 + 2 * js + s:4 + 2 * js + s]).then_inc(sem("maps_bias"), 1)
            act.wait_ge(sem("maps_turned"), 12)
            act.wait_ge(sem("value_done"), 4)
            act.wait_ge(sem("valid_ready"), 2)
            offx = omX[:, TAPS * PX:2 * TAPS * PX]
            offy = omX[:, 0:TAPS * PX]
            W = TAPS * PX
            act.activation(hx[:, W:2 * W], offx, ACT.Abs).then_inc(sem("absx"), 1)
            act.activation(hy[:, W:2 * W], offy, ACT.Abs).then_inc(sem("absy"), 1)
            act.wait_ge(sem("absx"), 1)
            act.activation(hx[:, 2 * W:3 * W], hx[:, W:2 * W], ACT.Relu, bias=minus_one[:, :],
                           accum_out=over[:, 0:1]).then_inc(sem("over"), 1)
            act.wait_ge(sem("absy"), 1)
            act.activation(hy[:, 0:W], hy[:, W:2 * W], ACT.Relu, bias=minus_one[:, :],
                           accum_out=over[:, 1:2]).then_inc(sem("over"), 1)
            act.wait_ge(sem("over"), 2)
            for dx in range(3):
                def taps(t, a):
                    return view(t, a * W + dx * PX, [(3 * PX, 3), (1, PX)])
                src = view(omX, (TAPS + dx) * PX, [(3 * PX, 3), (1, PX)])
                act.activation(taps(hx, 0), src, ACT.Relu, scale=nvalid[:, dx:dx + 1]).then_inc(sem("hats_x"), 1)
                act.activation(taps(hx, 1), taps(hx, 1), ACT.Relu, scale=nvalid[:, dx + 1:dx + 2],
                               bias=valid[:, dx + 1:dx + 2]).then_inc(sem("hats_x"), 1)
                act.activation(taps(hx, 2), src, ACT.Relu, scale=valid[:, dx + 2:dx + 3]).then_inc(sem("hats_x"), 1)
            act.wait_ge(sem("maps_turned"), 16)
            act.activation(nmask, omX[:, 2 * W:3 * W], ACT.Copy, scale=-1.0).then_inc(sem("nmask"), 1)

            root(rstd[:, 0:4], view(mv, 1, [(2, 4)]))
            act.wait_ge(sem("xhat2"), 4)
            for c4 in range(C4):
                act.dma_start(nat(scratch_hat, c4), quad(xh2, c4)).then_inc(sem("hat_out"), 16)
            act.wait_ge(sem("hat_out"), 64)
            for h in range(2):
                act.dma_start(view(X64, h * 2048, [(1, 2048)], 0, 64),
                              dram(scratch_hat, h * 2048, [(4096, 64), (1, 2048)])).then_inc(sem(f"X64_in{h}"), 16)
            for q in range(4):
                act.wait_ge(sem("xt_done"), q + 1)
                act.activation(XT[:, q * 512:(q + 1) * 512], bank(q), ACT.Copy).then_inc(sem("xt"), 1)
                act.wait_ge(sem("xt"), q + 1)
                act.activation(sq[:, q * 512:(q + 1) * 512], XT[:, q * 512:(q + 1) * 512], ACT.Square).then_inc(sem("sq"), 1)
            root(rs, n2, add_eps=False)
            for q in range(4):
                act.wait_ge(sem("xx"), q + 1)
                act.activation(view(hm, q * 2048 + 64, [(256, 8), (1, 64)]), view(xx, q * 512, [(64, 8), (1, 64)]),
                               ACT.Copy).then_inc(sem("h_copy"), 1)
                act.wait_ge(sem("m_half"), q + 1)
                act.activation(view(hm, q * 2048 + 192, [(256, 8), (1, 64)]), view(hm, q * 2048 + 128, [(256, 8), (1, 64)]),
                               ACT.Copy).then_inc(sem("m_copy"), 1)
            for q in range(4):
                act.wait_ge(sem("turn_done"), 3 * q + 2)
                act.activation(HM[:, q * 1024:(q + 1) * 1024], turned(q, 1), ACT.Copy).then_inc(sem("HM"), 1)
            for r in range(2):
                act.wait_ge(sem("far_done"), r + 1)
                act.activation(E[r], ps[:, r * 2048:(r + 1) * 2048], ACT.Exp, scale=0.5 / SPLIT ** 2).then_inc(sem("far_exp"), 1)
            for i in range(NODE_BLOCKS):
                act.wait_ge(sem("span_done"), i + 1)
                if i < 3:
                    act.wait_ge(sem("far_sum"), min(i + 1, 2))
                if i >= 3:
                    act.wait_ge(sem("span_added"), i - 2)
                act.activation(E[i % 3], ps[:, (i % 2) * 2048:(i % 2 + 1) * 2048], ACT.Exp, scale=0.5 / SPLIT ** 2,
                               accum_out=rowsum[:, i:i + 1]).then_inc(sem("span_exp"), 1)
            act.wait_ge(sem("simii"), 1)
            act.activation(dexp, simii, ACT.Exp, scale=0.5, bias=half[:, :]).then_inc(sem("dexp"), 1)
            root(rstd, pvar)

        @block.vector
        def _(dve):
            done = [0]

            def link(ins):
                ins.then_inc(sem("dve_step"), 1)
                done[0] += 1
                dve.wait_ge(sem("dve_step"), done[0])

            last, roots = [None], [0]

            def inverse_root(t, least=None):
                roots[0] += 1
                last[0].then_inc(sem("root_asked"), 1)
                dve.wait_ge(sem("root_given"), roots[0])
                if least is not None:
                    link(dve.tensor_scalar(t, t, least, None, ALU.max))
                link(dve.reciprocal(t, t))

            def group_norm(dst, ready, before=None):
                for q in range(NQ):
                    if q == 0 and before is not None:
                        before()
                    ins = dve.bn_stats(stats[:, 6 * q:6 * q + 6], xs[:, q * 512:(q + 1) * 512])
                    if q == NQ - 1:
                        link(ins)
                for q in range(NQ):
                    ins = dve.bn_aggr(mv[:, 2 * q:2 * q + 2], stats[:, 6 * q:6 * q + 6])
                last[0] = ins
                inverse_root(rstd[:, 0:4])
                for q in range(NQ):
                    dve.tensor_scalar(dst[:, q * 512:(q + 1) * 512], xs[:, q * 512:(q + 1) * 512], mv[:, 2 * q:2 * q + 1],
                                      rstd[:, q:q + 1], ALU.subtract, ALU.mult).then_inc(sem(ready), 1)

            dve.memset(wt3, 0.0).then_inc(sem("wt3_zero"), 1)
            dve.memset(minus_one, -1.0).then_inc(sem("ones_ready"), 1)
            dve.memset(eps, GN_EPS).then_inc(sem("ones_ready"), 1)
            dve.memset(half, 0.5).then_inc(sem("ones_ready"), 1)
            dve.memset(ones, 1.0).then_inc(sem("ones_ready"), 1)
            dve.memset(eighth, 0.125).then_inc(sem("ones_ready"), 1)
            dve.wait_ge(sem("ident_ready"), 1)
            dve.tensor_reduce(fold4, view(ident, 0, [(1, 4), (4, 32)]), AX.X, ALU.add).then_inc(sem("fold_ready"), 1)
            dve.tensor_reduce(fold16, view(ident, 0, [(1, 16), (16, 8)]), AX.X, ALU.add).then_inc(sem("fold_ready"), 1)
            dve.wait_ge(sem("fold_ready"), 2)
            dve.wait_ge(sem("raw0_in"), 16)
            dve.tensor_tensor(out=view(k0, 0, [(4, 192), (1, 4)]), in0=view(raw0, 0, [(1, 192), (0, 4)]),
                              in1=view(fold4, 0, [(0, 192), (1, 4)]), op=ALU.mult).then_inc(sem("k0_ready"), 1)
            group_norm(xh, "xhat0", lambda: dve.wait_ge(sem("x_in"), 64))
            dve.wait_ge(sem("iota_ready"), 1)
            link(dve.tensor_tensor(out=scr16, in0=fold16, in1=iota_x, op=ALU.mult))
            link(dve.tensor_reduce(xcol, scr16, AX.X, ALU.add))
            for b in range(5):
                s = b - 2
                dve.tensor_scalar(valid[:, b:b + 1], xcol, float(-s if s < 0 else HW - 1 - s), None,
                                  ALU.is_ge if s < 0 else ALU.is_le)
            link(dve.memset(scr16, 0.0))
            dve.tensor_scalar(nvalid, valid, -1.0, None, ALU.mult).then_inc(sem("valid_ready"), 2)

            for h in range(2):
                dve.wait_ge(sem("l0_pw_bias"), 3 * h + 2)
                for nq in (2 * h, 2 * h + 1):
                    dve.transpose(cols(tX, 0, PX, nq), to_rows_in(tN, nq)).then_inc(sem("t_turned"), 1)
            dve.wait_ge(sem("l0_pw_bias"), 6)
            for nq in range(NQ):
                dve.transpose(cols(gX, 0, PX, nq), view(gN, nq * PX, [(HW, HW), (0, C2), (1, HW)])).then_inc(sem("g_turned"), 1)
            dve.wait_ge(sem("g_turned"), 4)
            dve.wait_ge(sem("t_turned"), 4)
            for m, (l, g) in enumerate(conv_order):
                sl = slice(g * PX, (g + 1) * PX)
                gate = gX[:, l * PX:(l + 1) * PX]
                dve.wait_ge(sem("gelu"), m + 1)
                if l == 0:
                    link(dve.tensor_tensor(out=ctx_all[:, sl], in0=ctxs[0][:, sl], in1=gate, op=ALU.mult))
                else:
                    link(dve.tensor_tensor(out=tmpg[:, 0:PX], in0=ctxs[l][:, sl], in1=gate, op=ALU.mult))
                    link(dve.tensor_tensor(out=ctx_all[:, sl], in0=ctx_all[:, sl], in1=tmpg[:, 0:PX], op=ALU.add))
                if l == 2:
                    dve.tensor_reduce(R3[:, g * HW:(g + 1) * HW], view(ctxs[2], g * PX, [(1, HW), (HW, HW)]),
                                      AX.X, ALU.add).then_inc(sem("rows3"), 1)
            dve.wait_ge(sem("glob_done"), 1)
            link(dve.tensor_tensor(out=view(tmp, 0, [(PX, 8), (HW, HW), (1, HW)]),
                                   in0=view(bank(0), 0, [(HW, 8), (0, HW), (1, HW)]),
                                   in1=view(gX, 3 * PX, [(0, 8), (HW, HW), (1, HW)]), op=ALU.mult))
            dve.tensor_tensor(out=ctx_all, in0=ctx_all, in1=tmp, op=ALU.add).then_inc(sem("ctx_all"), 1)
            dve.wait_ge(sem("key_done"), 1)
            dve.wait_ge(sem("small_in"), 48)
            link(dve.tensor_scalar(kS, bank(1, PX), keyb[:, 0:1], None, ALU.add))
            dve.tensor_reduce(kmax, view(kS, 0, [(1, HW), (HW, HW)]), AX.X, ALU.max).then_inc(sem("kmax"), 1)
            dve.wait_ge(sem("kmax_turned"), 1)
            link(dve.tensor_reduce(gmax[0:16, :], view(bank(2), 0, [(1, P)], 0, 16), AX.X, ALU.max))
            dve.tensor_scalar(diag[0:16, :], ident[0:16, 0:16], gmax[0:16, 0:1], None, ALU.mult).then_inc(sem("max_diag"), 1)
            dve.wait_ge(sem("max_spread"), 1)
            dve.tensor_tensor(out=view(kC, 0, [(HW, HW), (1, HW)]), in0=view(kS, 0, [(HW, HW), (1, HW)]),
                              in1=view(bank(3), 0, [(0, HW), (1, HW)]), op=ALU.subtract).then_inc(sem("key_centred"), 1)
            dve.wait_ge(sem("key_exp"), 1)
            dve.wait_ge(sem("ctx_all"), 1)
            link(dve.tensor_tensor(out=view(tmp, 0, [(PX, 8), (1, PX)]), in0=view(ctx_all, 0, [(PX, 8), (1, PX)]),
                                   in1=view(kE, 0, [(0, 8), (1, PX)]), op=ALU.mult))
            dve.tensor_reduce(Ey, view(kE, 0, [(1, HW), (HW, HW)]), AX.X, ALU.add).then_inc(sem("qk_rows"), 1)
            dve.tensor_reduce(view(Rq, 0, [(HW, 8), (1, HW)]), view(tmp, 0, [(PX, 8), (1, HW), (HW, HW)]),
                              AX.X, ALU.add).then_inc(sem("qk_rows"), 1)
            dve.wait_ge(sem("v1_done"), 1)
            link(dve.reciprocal(rden[0:16, :], view(bank(2), 256, [(1, 1)], 0, 16)))
            link(dve.scalar_tensor_tensor(out=vrow[0:16, :], in0=view(bank(2), 128, [(1, 4)], 0, 16),
                                          scalar=rden[0:16, 0:1], in1=rowN[0:16, 0:4], op0=ALU.mult, op1=ALU.add))
            link(dve.bn_stats(vst[0:16, :], vrow[0:16, :]))
            last[0] = dve.bn_aggr(vmv[0:16, :], vst[0:16, :])
            inverse_root(vrs[0:16, :])
            link(dve.tensor_scalar(vrow[0:16, :], vrow[0:16, :], vmv[0:16, 0:1], vrs[0:16, 0:1], ALU.subtract, ALU.mult))
            link(dve.tensor_tensor(out=vrow[0:16, :], in0=vrow[0:16, :], in1=rowN[0:16, 4:8], op=ALU.mult))
            link(dve.tensor_tensor(out=vrow[0:16, :], in0=vrow[0:16, :], in1=rowN[0:16, 8:12], op=ALU.add))
            dve.tensor_scalar(vrow[0:16, :], vrow[0:16, :], 0.0, None, ALU.max).then_inc(sem("v1_relu"), 1)
            dve.wait_ge(sem("v1_turned"), 1)
            dve.tensor_copy(vT[0:4, :], view(bank(2), 320, [(1, HW)], 0, 4)).then_inc(sem("vT"), 1)
            dve.wait_ge(sem("v2_done"), 1)
            link(dve.tensor_tensor(out=view(vadd, 0, [(HW, 8), (1, HW)]), in0=view(bank(3), 128, [(HW, 8), (1, HW)]),
                                   in1=view(sX, SX_V2B, [(1, 8), (0, HW)]), op=ALU.add))
            link(dve.tensor_tensor(out=view(tmp, 0, [(PX, 8), (HW, HW), (1, HW)]),
                                   in0=view(ctx_all, 0, [(PX, 8), (HW, HW), (1, HW)]),
                                   in1=view(vadd, 0, [(HW, 8), (0, HW), (1, HW)]), op=ALU.add))
            for nq in range(NQ):
                ins = dve.transpose(to_rows_in(ctxs[0], nq), cols(tmp, 0, PX, nq))
            link(ins)
            dve.tensor_tensor(out=xs, in0=xs, in1=ctxs[0], op=ALU.add).then_inc(sem("l0_done"), 1)

            dve.wait_ge(sem("l0_done"), 1)
            group_norm(xh1, "xhat1")
            dve.wait_ge(sem("xhat1"), 4)
            for nq in range(NQ):
                dve.transpose(cols(xX, 0, PX, nq), to_rows_in(xh1, nq)).then_inc(sem("xX_turned"), 1)
            dve.wait_ge(sem("dw_bias"), G)
            for nq in range(NQ):
                dve.transpose(to_rows_in(dN, nq), cols(dwX, 0, PX, nq)).then_inc(sem("dN_ready"), 1)
            dve.wait_ge(sem("value_bias"), 4)
            dve.wait_ge(sem("vsh_zero"), 5)
            for nq in range(NQ):
                dve.transpose(cols(vsh[2], 2 * HW, 20 * HW, nq), to_rows_in(omN[1], nq)).then_inc(sem("v0_ready"), 1)
            for js in range(4):
                dve.wait_ge(sem("maps_bias"), 4 * js + 4)
                for nq in range(NQ):
                    dve.transpose(cols(omX, 8 * js * PX, PX, nq), to_rows_in(omN[js % 2], nq)).then_inc(sem("maps_turned"), 1)
            W = TAPS * PX
            dve.wait_ge(sem("over"), 2)
            dve.tensor_tensor(out=oversum, in0=over[:, 0:1], in1=over[:, 1:2], op=ALU.add).then_inc(sem("over_rows"), 1)
            dve.wait_ge(sem("over_all"), 1)
            link(dve.tensor_scalar(flagf[0:1, :], bank(0)[0:1, 0:1], 0.0, None, ALU.is_gt))
            dve.tensor_copy(flag[0:1, :], flagf[0:1, :]).then_inc(sem("flag"), 1)
            dve.wait_ge(sem("flag"), 1)
            far = dve.value_load(flag[0:1, 0:1], min_val=0, max_val=1)
            dve.wait_ge(sem("maps_turned"), 16)
            dve.wait_ge(sem("nmask"), 1)
            dve.wait_ge(sem("hats_x"), 9)
            dve.wait_ge(sem("vsh_in"), 64)
            offy, offx, mask = omX[:, 0:W], omX[:, W:2 * W], omX[:, 2 * W:3 * W]
            base = done[0]
            with dve.If(far == 0):
                dve.scalar_tensor_tensor(out=hy[:, 0:W], in0=offy, scalar=0.0, in1=nmask, op0=ALU.min, op1=ALU.mult).then_inc(sem("hats_y"), 1)
                dve.scalar_tensor_tensor(out=hy[:, W:2 * W], in0=hy[:, W:2 * W], scalar=-1.0, in1=nmask, op0=ALU.add, op1=ALU.mult).then_inc(sem("hats_y"), 1)
                dve.scalar_tensor_tensor(out=hy[:, 2 * W:3 * W], in0=offy, scalar=0.0, in1=mask, op0=ALU.max, op1=ALU.mult).then_inc(sem("hats_y"), 1)
                dve.wait_ge(sem("hats_y"), 3)
                m = 0
                for by in range(5):
                    first = True
                    for dy in range(3):
                        ay = by - dy
                        if not 0 <= ay < 3:
                            continue
                        link(dve.tensor_tensor(out=view(fold[0 if first else 1], 0, [(3 * PX, 3), (PX, 3), (1, PX)]),
                                               in0=view(hy, ay * W + dy * 3 * PX, [(PX, 3), (0, 3), (1, PX)]),
                                               in1=view(hx, dy * 3 * PX, [(PX, 3), (W, 3), (1, PX)]), op=ALU.mult))
                        if not first:
                            link(dve.tensor_tensor(out=fold[0], in0=fold[0], in1=fold[1], op=ALU.add))
                        first = False
                    f, a = fold[0], 0
                    dve.tensor_copy(view(A, a, [(4 * PX, 2), (1, PX)]), view(f, 0, [(8 * PX, 2), (1, PX)]))
                    dve.tensor_tensor(out=view(A, a + PX, [(2 * PX, 2), (1, PX)]), in0=view(f, PX, [(4 * PX, 2), (1, PX)]),
                                      in1=view(f, 3 * PX, [(4 * PX, 2), (1, PX)]), op=ALU.add)
                    link(dve.tensor_tensor(out=view(A, a + 2 * PX, [(1, PX)]), in0=view(f, 2 * PX, [(1, PX)]),
                                           in1=view(f, 4 * PX, [(1, PX)]), op=ALU.add))
                    link(dve.tensor_tensor(out=view(A, a + 2 * PX, [(1, PX)]), in0=view(A, a + 2 * PX, [(1, PX)]),
                                           in1=view(f, 6 * PX, [(1, PX)]), op=ALU.add))
                    for bx in range(5):
                        for hh in range(2):
                            if m >= 4:
                                dve.wait_ge(sem("window_added"), m - 3)
                            dve.tensor_tensor(out=view(ring[m % 4], 0, [(PX, 4), (1, PX)]),
                                              in0=view(vsh[bx], hh * 4 * 320 + by * HW, [(320, 4), (1, PX)]),
                                              in1=view(A, a + bx * PX, [(0, 4), (1, PX)]), op=ALU.mult).then_inc(sem("window_prod"), 1)
                            m += 1
                dve.wait_ge(sem("window_added"), 50)
                dve.memset(scr16, 0.0).then_inc(sem("window_sum"), 1)
            with dve.Else():
                slow_vector(dve)
            dve.wait_ge(sem("window_sum"), 1)
            for nq in range(NQ):
                dve.transpose(to_rows_in(oN, nq), cols(ps, 0, PX, nq)).then_inc(sem("window_turned"), 1)
            dve.wait_ge(sem("window_turned"), 4)
            dve.memset(scr16, 0.0).then_inc(sem("window_done"), 1)
            for h in range(2):
                for s in range(2):
                    dve.wait_ge(sem("op_done"), 2 * h + s + 1)
                    v = view(xs, h * 1024 + s * PX, [(512, 2), (1, PX)])
                    dve.tensor_tensor(out=v, in0=v, in1=view(bank(4 + 2 * h + s), 0, [(PX, 2), (1, PX)]),
                                      op=ALU.add).then_inc(sem("x2_ready"), 1)

            dve.wait_ge(sem("x2_ready"), 4)
            group_norm(xh2, "xhat2")
            dve.wait_ge(sem("sq"), 4)
            last[0] = dve.tensor_reduce(n2, view(sq, 0, [(64, 32), (1, 64)]), AX.X, ALU.add)
            inverse_root(rs, 1e-8)
            link(dve.tensor_scalar(rsS, rs, SPLIT, None, ALU.mult))
            link(dve.tensor_tensor(out=simii, in0=n2, in1=rs, op=ALU.mult))
            dve.tensor_tensor(out=simii, in0=simii, in1=rs, op=ALU.mult).then_inc(sem("simii"), 1)
            for q in range(4):
                dve.tensor_tensor(out=view(xx, q * 512, [(64, 8), (1, 64)]), in0=view(XT, q * 512, [(64, 8), (1, 64)]),
                                  in1=view(rsS, q * 8, [(1, 8), (0, 64)]), op=ALU.mult).then_inc(sem("xx"), 1)
                dve.wait_ge(sem("xx"), q + 1)
                dve.tensor_copy(view(hm, q * 2048, [(256, 8), (1, 64)]),
                                view(xx, q * 512, [(64, 8), (1, 64)])).then_inc(sem("h_half"), 1)
                dve.wait_ge(sem("h_half"), q + 1)
                dve.tensor_tensor(out=view(hm, q * 2048 + 128, [(256, 8), (1, 64)]),
                                  in0=view(xx, q * 512, [(64, 8), (1, 64)]),
                                  in1=view(hm, q * 2048, [(256, 8), (1, 64)]), op=ALU.subtract).then_inc(sem("m_half"), 1)
            for q in range(4):
                for t, (dst, which) in enumerate(((HH, 0), (MM, 2))):
                    dve.wait_ge(sem("turn_done"), 3 * q + which + 1)
                    dve.tensor_copy(dst[:, q * 1024:(q + 1) * 1024], turned(q, which)).then_inc(sem("HHMM"), 1)
            dve.wait_ge(sem("HHMM"), 8)
            dve.tensor_copy(HH[:, 4096:6144], HH[:, 0:2048]).then_inc(sem("HHMM"), 1)
            dve.tensor_copy(MM[:, 4096:6144], MM[:, 0:2048]).then_inc(sem("HHMM"), 1)
            for r in range(2):
                dve.wait_ge(sem("far_exp"), r + 1)
                dve.tensor_reduce(row16[:, 16 * r:16 * r + 16], view(E[r], 0, [(P, 16), (1, P)]), AX.X,
                                  ALU.add).then_inc(sem("far_sum"), 1)
            dve.wait_ge(sem("colacc_zero"), 1)
            for i in range(NODE_BLOCKS):
                dve.wait_ge(sem("span_exp"), i + 1)
                if i:
                    dve.wait_ge(sem("span_added"), i)
                cc = colacc[:, (i + 1) * P:(i + REACH) * P]
                dve.tensor_tensor(out=cc, in0=cc, in1=E[i % 3][:, P:REACH * P], op=ALU.add).then_inc(sem("span_added"), 1)
            dve.wait_ge(sem("span_added"), NODE_BLOCKS)
            dve.tensor_tensor(out=colacc[:, 0:2048], in0=colacc[:, 0:2048], in1=colacc[:, 4096:6144],
                              op=ALU.add).then_inc(sem("col_folded"), 1)
            dve.wait_ge(sem("col_done"), 1)
            link(dve.tensor_tensor(out=Ssum, in0=rowsum, in1=row16, op=ALU.add))
            link(dve.tensor_tensor(out=Ssum, in0=Ssum, in1=bank(0, 32), op=ALU.add))
            link(dve.reciprocal(Ssum, Ssum))
            dve.wait_ge(sem("dexp"), 1)
            link(dve.tensor_tensor(out=Ssum, in0=Ssum, in1=dexp, op=ALU.mult))
            link(dve.tensor_tensor(out=view(o2, 0, [(64, 32), (1, 64)]), in0=view(XT, 0, [(64, 32), (1, 64)]),
                                   in1=view(Ssum, 0, [(1, 32), (0, 64)]), op=ALU.mult))
            dve.wait_ge(sem("x2R_in"), 16)
            dve.scalar_tensor_tensor(out=x3R, in0=o2, scalar=0.0, in1=x2R, op0=ALU.max, op1=ALU.add).then_inc(sem("x3_ready"), 1)

            dve.wait_ge(sem("l3_in"), 48)
            link(dve.tensor_scalar(wraw, wraw, 0.0, 2.0, ALU.is_gt, ALU.mult))
            for b2 in range(2):
                dve.tensor_scalar(view(wsgn, 64 * b2, [(P, TAPS), (1, 64)], 64 * b2, 64),
                                  view(wraw, 64 * b2, [(P, TAPS), (1, 64)], 64 * b2, 64), 1.0, None,
                                  ALU.subtract).then_inc(sem("wsgn"), 1)
                dve.memset(view(wsgn, 64 * (1 - b2), [(P, TAPS), (1, 64)], 64 * b2, 64), 0.0).then_inc(sem("wsgn"), 1)
            dve.memset(apad, 0.0).then_inc(sem("apad_zero"), 1)
            for b in range(8):
                dve.wait_ge(sem(f"x3N_in{b // 4}"), 16)
                ins = dve.bn_stats(stats[:, 6 * b:6 * b + 6], x3N[:, b * PX:(b + 1) * PX])
            link(ins)
            for b in range(8):
                ins = dve.bn_aggr(mv[:, 2 * b:2 * b + 2], stats[:, 6 * b:6 * b + 6])
            link(ins)
            dve.tensor_copy(pstat[:, 0:8], view(mv, 0, [(2, 8)]))
            link(dve.tensor_tensor(out=pstat[:, 8:16], in0=view(mv, 0, [(2, 8)]), in1=view(mv, 0, [(2, 8)]), op=ALU.mult))
            dve.tensor_tensor(out=pstat[:, 8:16], in0=pstat[:, 8:16], in1=view(mv, 1, [(2, 8)]),
                              op=ALU.add).then_inc(sem("pstat"), 1)
            dve.wait_ge(sem("pair_done"), 1)
            link(dve.tensor_copy(pavg, bank(1, 16)))
            link(dve.tensor_tensor(out=pvar, in0=pavg[:, 0:8], in1=pavg[:, 0:8], op=ALU.mult))
            last[0] = dve.tensor_tensor(out=pvar, in0=pavg[:, 8:16], in1=pvar, op=ALU.subtract)
            inverse_root(rstd)
            for b in range(8):
                ins = dve.tensor_scalar(sgn[:, b * PX:(b + 1) * PX], x3N[:, b * PX:(b + 1) * PX], pavg[:, b:b + 1],
                                        rstd[:, b:b + 1], ALU.subtract, ALU.mult)
            link(ins)
            link(dve.tensor_scalar(sgn, sgn, alphaT[:, 0:1], 2.0, ALU.is_gt, ALU.mult))
            for b in range(8):
                dve.tensor_scalar(view(apad, b * 324 + 19, [(18, 16), (1, 16)]), view(sgn, b * PX, [(16, 16), (1, 16)]),
                                  1.0, None, ALU.subtract).then_inc(sem("apad"), 1)
            for q in range(4):
                dve.wait_ge(sem("l3_done"), q + 1)
                dve.tensor_tensor(out=yout[:, q * 512:(q + 1) * 512], in0=x3N[:, q * 512:(q + 1) * 512],
                                  in1=bank(2 + q), op=ALU.add).then_inc(sem("y_ready"), 1)

        @block.tensor
        def _(pe):
            def pointwise(dst, w, nset, s, src, h, ready):
                for c2 in range(C2):
                    ins = pe.matmul(dst, w[:, (c2 * nset + s) * P:(c2 * nset + s + 1) * P],
                                    view(src, h * 1024 + c2 * PX, [(512, 2), (1, PX)]), start=(c2 == 0), stop=(c2 == 1))
                ins.then_inc(sem(ready), 1)

            def depthwise(dst, wt, k, src, g, ready):
                r = k // 2
                rows = [0] + [d for d in range(-r, r + 1) if d]
                for n, dy in enumerate(rows):
                    y0, y1 = max(0, -dy), HW - max(0, dy)
                    ins = pe.matmul(view(dst, y0 * HW, [(1, (y1 - y0) * HW)]), view(wt, g * k + dy + r, [(8 * k, P)]),
                                    view(src, g * PX + (y0 + dy) * HW, [(1, (y1 - y0) * HW)]),
                                    start=(n == 0), stop=(n == k - 1))
                ins.then_inc(sem(ready), 1)

            pe.wait_ge(sem("k0_ready"), 1)
            for h in range(2):
                pe.wait_ge(sem("xhat0"), 2 * h + 2)
                for s in range(3):
                    pointwise(bank(3 * h + s), k0, 3, s, xh, h, "l0_pw")
            pe.wait_ge(sem("t_turned"), 4)
            pe.wait_ge(sem("l0_pw_bias"), 6)
            for m, (l, g) in enumerate(conv_order):
                k = (3, 5, 7)[l]
                if g == 0:
                    pe.wait_ge(sem(("wt3_in", "wt5_in", "wt7_in")[l]), 128)
                need = 0 if m < 8 else m - 7
                if l:
                    need = max(need, conv_order.index((l - 1, g)) + 1)
                if need:
                    pe.wait_ge(sem("gelu"), need)
                depthwise(bank(m % 8, PX), (wt3, wt5, wt7)[l], k, (tX, ctxs[0], ctxs[1])[l], g, "conv_done")
            pe.wait_ge(sem("rows3"), G)
            pe.wait_ge(sem("gelu"), 24)
            pe.wait_ge(sem("means_ready"), 2)
            pe.matmul(bank(0, P), mean256, R3, start=True, stop=True).then_inc(sem("glob_done"), 1)
            pe.wait_ge(sem("ctx_all"), 1)
            pe.wait_ge(sem("keyk_ready"), 1)
            for g in range(G):
                ins = pe.matmul(bank(1, PX), keyk[:, g * P:(g + 1) * P], ctx_all[:, g * PX:(g + 1) * PX],
                                start=(g == 0), stop=(g == G - 1))
            ins.then_inc(sem("key_done"), 1)
            pe.wait_ge(sem("kmax"), 1)
            pe.transpose(view(bank(2), 0, [(1, P)], 0, 16), kmax, ident).then_inc(sem("kmax_turned"), 1)
            pe.wait_ge(sem("max_diag"), 1)
            pe.wait_ge(sem("ones_ready"), 5)
            pe.matmul(bank(3, 16), ones[0:16, :], diag[0:16, :], start=True, stop=True).then_inc(sem("max_spread"), 1)
            pe.wait_ge(sem("qk_rows"), 2)
            for g in range(G):
                pe.matmul(view(bank(2), 128, [(1, 4)], 0, 16), Rq[:, g * HW:(g + 1) * HW],
                          sX[:, SX_V1 + 4 * g:SX_V1 + 4 * g + 4], start=(g == 0), stop=(g == G - 1))
            pe.matmul(view(bank(2), 256, [(1, 1)], 0, 16), Ey, eighth, start=True, stop=True).then_inc(sem("v1_done"), 1)
            pe.wait_ge(sem("v1_relu"), 1)
            pe.transpose(view(bank(2), 320, [(1, HW)], 0, 4), vrow[0:16, :], ident[0:16, 0:16]).then_inc(sem("v1_turned"), 1)
            pe.wait_ge(sem("vT"), 1)
            pe.wait_ge(sem("v2k_ready"), 1)
            for g in range(G):
                ins = pe.matmul(view(bank(3), 128 + g * HW, [(1, HW)]), v2k[0:4, g * P:(g + 1) * P], vT[0:4, :],
                                start=True, stop=True)
            ins.then_inc(sem("v2_done"), 1)

            pe.wait_ge(sem("xX_turned"), 4)
            pe.wait_ge(sem("wtd_in"), 128)
            for g in range(G):
                depthwise(view(bank(g // 2), (g % 2) * PX, [(1, PX)]), wtd, 3, xX, g, "dw_done")
            pe.wait_ge(sem("k1_ready"), 1)
            for s in range(2):
                for h in range(2):
                    pointwise(bank(4 + 2 * s + h), k1, 10, 8 + s, xh1, h, "value_done")
            pe.wait_ge(sem("dN_ready"), 4)
            pe.wait_ge(sem("dw_bias"), G)
            for js in range(4):
                for s in range(2):
                    for h in range(2):
                        if js == 1:
                            pe.wait_ge(sem("value_bias"), 2 * s + h + 1)
                        elif js > 1:
                            pe.wait_ge(sem("maps_bias"), 4 * (js - 2) + 2 * s + h + 1)
                        pointwise(bank(4 * (js % 2) + 2 * s + h), k1, 10, 2 * js + s, dN, h, "maps_done")
            pe.wait_ge(sem("over_rows"), 1)
            pe.wait_ge(sem("maps_bias"), 16)
            pe.matmul(bank(0)[0:1, 0:1], oversum, ones[:, 0:1], start=True, stop=True).then_inc(sem("over_all"), 1)
            pe.wait_ge(sem("flag"), 1)
            far = pe.value_load(flag[0:1, 0:1], min_val=0, max_val=1)
            with pe.If(far == 0):
                for m in range(50):
                    pe.wait_ge(sem("window_prod"), m + 1)
                    for q in range(2):
                        ins = pe.matmul(bank(2 * (m % 2) + q), ident, view(ring[m % 4], 512 * q, [(1, 512)]),
                                        start=(m < 2), stop=(m >= 48))
                    ins.then_inc(sem("window_added"), 1)
            with pe.Else():
                slow_tensor(pe)
            pe.wait_ge(sem("window_turned"), 4)
            pe.wait_ge(sem("k2_ready"), 1)
            for h in range(2):
                for s in range(2):
                    pointwise(bank(4 + 2 * h + s), k2, 2, s, oN, h, "op_done")

            for q in range(4):
                pe.wait_ge(sem(f"X64_in{q // 2}"), 16)
                for j in range(8):
                    i = 8 * q + j
                    ins = pe.transpose(view(bank(q), 64 * j, [(1, 64)]), X64[0:64, i * P:(i + 1) * P], ident[0:64, 0:64])
                ins.then_inc(sem("xt_done"), 1)
            pe.wait_ge(sem("graph_ready"), 1)
            pe.wait_ge(sem("xt"), 4)
            pe.wait_ge(sem("x2_ready"), 4)
            for q in range(4):
                pe.wait_ge(sem("h_half"), q + 1)
                pe.wait_ge(sem("m_copy"), q + 1)
                pe.wait_ge(sem("h_copy"), q + 1)
                for which in range(3):
                    t = 3 * q + which
                    if t >= 8:
                        for name, n in free_turned[t - 8]:
                            pe.wait_ge(sem(name), n)
                    for j in range(8):
                        ins = pe.transpose(view(turned(q, which), P * j, [(1, P)]),
                                           view(hm, (8 * q + j) * 256 + 64 * which, [(1, P)]), ident16)
                    ins.then_inc(sem("turn_done"), 1)
            pe.wait_ge(sem("HM"), 4)
            pe.wait_ge(sem("HHMM"), 10)

            def half_products(dst, i, col, n, stop=True):
                w = HM[:, bass.ts(i, P)] if not isinstance(i, int) else HM[:, i * P:(i + 1) * P]
                pe.matmul(dst, w, HH[:, col:col + n], start=True, stop=False)
                return pe.matmul(dst, w, MM[:, col:col + n], start=False, stop=stop)

            for r in range(2):
                for i in range(16 * r, 16 * r + 16):
                    ins = half_products(view(ps, r * 2048 + (i - 16 * r) * P, [(1, P)]), i, (i + 16) * P, P)
                ins.then_inc(sem("far_done"), 1)
            for i in range(NODE_BLOCKS):
                if i < 2:
                    pe.wait_ge(sem("far_exp"), i + 1)
                else:
                    pe.wait_ge(sem("span_exp"), i - 1)
                b0 = (i % 2) * 4
                for q in range(4):
                    ins = half_products(bank(b0 + q), i, i * P + 512 * q, 512, stop=(q > 0))
                    if q == 0:
                        e = adj16[:, (i % 2) * 3 * P:(i % 2) * 3 * P + 3 * P] if i < 30 else \
                            (adj_last if i == 30 else adj16[:, 3 * P:4 * P])
                        n = e.ap[1][1]
                        ins = pe.matmul(bank(b0, n), identS, e, start=False, stop=True)
                ins.then_inc(sem("span_done"), 1)
            pe.wait_ge(sem("col_folded"), 1)
            pe.wait_ge(sem("span_exp"), NODE_BLOCKS)
            for i in range(NODE_BLOCKS):
                ins = pe.matmul(view(bank(0), i, [(1, 1)]), colacc[:, i * P:(i + 1) * P], ones[:, 0:1], start=True, stop=True)
            ins.then_inc(sem("col_done"), 1)

            pe.wait_ge(sem("pstat"), 1)
            pe.matmul(bank(1, 16), pair_mean, pstat, start=True, stop=True).then_inc(sem("pair_done"), 1)
            pe.wait_ge(sem("wsgn"), 4)
            pe.wait_ge(sem("apad_zero"), 1)
            for q in range(4):
                pe.wait_ge(sem("apad"), 2 * q + 2)
                for t in range(TAPS):
                    ky, kx = divmod(t, 3)
                    ins = pe.matmul(bank(2 + q), wsgn[:, t * P:(t + 1) * P],
                                    view(apad, 2 * q * 324 + ky * 18 + kx, [(324, 2), (18, 16), (1, 16)]),
                                    start=(t == 0), stop=(t == TAPS - 1))
                ins.then_inc(sem("l3_done"), 1)



def kernel(**inputs):
    import numpy as np
    import concourse.bacc as bacc
    from concourse.bass_utils import run_bass_kernel_spmd as run

    a = {k: np.asarray(v) for k, v in inputs.items()}
    arrays = lay_out(np, a)
    nc = bacc.Bacc("TRN2", target_bir_lowering=False, num_devices=1)
    args = [nc.dram_tensor(f"in_{n}", v.shape, mybir.dt.from_np(v.dtype), kind="ExternalInput").ap()
            for n, v in arrays.items()]
    args.append(nc.dram_tensor("out_0", (B * C * PX,), F32, kind="ExternalOutput").ap())
    bass_preact_convs(nc, *args)
    r = run(nc, [{f"in_{n}": v for n, v in arrays.items()}], core_ids=[0])
    return r.results[0]["out_0"].reshape(B, C, HW, HW)


def lay_out(np, a):
    f = np.float32

    def toeplitz(ws):
        k = ws.shape[-1]
        r = k // 2
        t = np.zeros((8, HW, HW, 8, k), f)
        w = ws.reshape(8, 8, k, k).transpose(1, 0, 2, 3)
        for x in range(HW):
            for x1 in range(max(0, x - r), min(HW, x + r + 1)):
                t[:, x1, x] = w[..., x1 - x + r]
        return t

    def rows(w):
        return w.reshape(-1, 8, 4, 2).transpose(2, 1, 3, 0).reshape(32, 2, -1)

    def outs(v):
        return v.reshape(v.shape[:-1] + (8, 4, 2)).transpose(tuple(range(v.ndim - 1)) + (v.ndim + 1, v.ndim, v.ndim - 1)) \
                .reshape(v.shape[:-1] + (2, 32))

    def gates(v):
        g = np.zeros(v.shape[:-1] + (4, 8), f)
        g[..., 0:4] = v[..., None, :]
        return g.reshape(v.shape[:-1] + (1, 32))

    def groups(v, n):
        m = -(-n // 8) * 8
        t = np.zeros(v.shape[:-2] + (8, m), f)
        t[..., :n] = v
        t = t.reshape(v.shape[:-2] + (4, 2, m // 8, 8))
        d = v.ndim - 2
        return t.transpose(tuple(range(d)) + (d + 2, d + 1, d, d + 3)).reshape(v.shape[:-2] + (m // 8 * 2, 32))

    def maps(v):
        v = v.reshape(v.shape[:-1] + (8, 27))
        return np.concatenate([v[..., 0:18:2], v[..., 1:18:2], v[..., 18:27]], axis=-1)

    w0, b0 = rows(a["L0_conv_conv_w"]), a["L0_conv_conv_b"]
    pw0 = np.concatenate([outs(w0[..., :64]), gates(w0[..., 64:])], axis=2)
    om, vp = rows(a["L1_conv_om_w"]), rows(a["L1_conv_vp_w"])
    pw1 = np.concatenate([groups(maps(om), 27), groups(vp.reshape(32, 2, 8, 8), 8)], axis=2)
    op = a["L1_conv_op_w"].reshape(64, 4, 2, 8).transpose(1, 3, 2, 0).reshape(32, 2, 64)
    bias = np.concatenate([outs(b0[:64]), gates(b0[64:]), groups(maps(a["L1_conv_om_b"]), 27),
                           groups(a["L1_conv_vp_b"].reshape(8, 8), 8)], axis=0)
    small = np.concatenate([a["L0_conv_v1_w"].reshape(4, 8, 8).transpose(2, 1, 0).reshape(8, 32),
                            a["L0_conv_v2_b"].reshape(8, 8).T, a["L1_conv_dw_b"].reshape(8, 8).T,
                            a["L0_conv_key_w"].reshape(8, 8).T], axis=1)
    out = {
        "x": a["x"].reshape(-1), "toep3": toeplitz(a["L0_conv_fw3"]), "toep5": toeplitz(a["L0_conv_fw5"]),
        "toep7": toeplitz(a["L0_conv_fw7"]), "toepd": toeplitz(a["L1_conv_dw_w"]),
        "pw0": pw0, "pw1": pw1, "pw2": outs(op), "bias_n": bias.T, "small_x": small, "key_b": a["L0_conv_key_b"],
        "row_n": np.concatenate([a["L0_conv_v1_b"], a["L0_conv_ln_w"], a["L0_conv_ln_b"]]),
        "v2_w": a["L0_conv_v2_w"].T, "alpha": a["L3_conv_alpha"].reshape(-1),
        "sign_w": a["L3_conv_weight"].transpose(1, 2, 3, 0),
    }
    return {k: np.ascontiguousarray(v).reshape(-1) for k, v in out.items()}
```

```python
from contextlib import ExitStack

import concourse.bass as bass
from concourse import mybir

F32 = mybir.dt.float32
F16 = mybir.dt.float16
BF16 = mybir.dt.bfloat16
I32 = mybir.dt.int32
ALU = mybir.AluOpType
ACT = mybir.ActivationFunctionType
AX = mybir.AxisListType

B, C, HW, PX = 16, 64, 16, 256
P = 128
FULL = B * C * PX // P
NQ, N4 = 4, 4
G, C4, C2 = 8, 4, 2
TAPS = 9
MAPS = 27
NODE_BLOCKS = 32
REACH = 16
ARENA = 34816
SPLIT = 256.0
GN_EPS = 1e-5

SX_V1, SX_V2B, SX_DWB, SX_KEY, SX_N = 0, 32, 40, 48, 56


def bass_preact_convs(nc, x, toep3, toep5, toep7, toepd, pw0, pw1, pw2, bias_n, small_x, key_b,
                      row_n, v2_w, alpha, sign_w, out):
    scratch_hat = nc.dram_tensor("scratch_hat", (B * C * PX,), F32, kind="Internal").ap()
    scratch_x2 = nc.dram_tensor("scratch_x2", (B * C * PX,), F32, kind="Internal").ap()
    scratch_x3 = nc.dram_tensor("scratch_x3", (B * C * PX,), F32, kind="Internal").ap()

    ctx = ExitStack()
    with ctx:
        def sb(name, cols, dt=F32):
            return ctx.enter_context(nc.sbuf_tensor(name, [P, cols], dt))[:, :]

        def view(t, col, dims, p0=0, n=P):
            row = t.ap[0][0]
            return bass.AP(t.tensor, t.offset + p0 * row + col, [[row, n]] + [list(d) for d in dims])

        def dram(t, off, dims):
            return bass.AP(t.tensor, t.offset + off, [list(d) for d in dims])

        sems = {}

        def sem(name):
            if name not in sems:
                sems[name] = ctx.enter_context(nc.semaphore(name))
            return sems[name]

        xs = sb("xs", FULL)
        ident = sb("ident", P)
        fold4 = sb("fold4", N4)
        fold16 = sb("fold16", HW)
        mean256 = sb("mean256", P)
        ones = sb("ones", P)
        pair_mean = sb("pair_mean", P)
        eighth = sb("eighth", 1)
        xcol = sb("xcol", 1)
        valid = sb("valid", 5)
        nvalid = sb("nvalid", 5)
        iota_x = sb("iota_x", HW)
        scr16 = sb("scr16", HW)
        adj = sb("adj", 3 * P)
        adj16 = sb("adj16", 6 * P, F16)
        adj_last = sb("adj_last", 2 * P, F16)
        ident16 = sb("ident16", P, F16)
        identS = sb("identS", P, F16)
        raw0, raw1, raw2 = sb("raw0", 192), sb("raw1", 640), sb("raw2", 128)
        k1 = sb("k1", 2560)
        k2 = sb("k2", 512)
        sN = sb("sN", 13)
        sX = sb("sX", SX_N)
        keyb = sb("keyb", 1)
        rowN = sb("rowN", 12)
        v2raw = sb("v2raw", 64)
        alphaT = sb("alphaT", 1)
        minus_one, half, eps = sb("minus_one", 1), sb("half", 1), sb("eps", 1)
        ytile = sb("ytile", 2 * PX)
        rot1 = sb("rot1", P)
        stats = sb("stats", 8 * 6)
        mv = sb("mv", 16)
        rstd = sb("rstd", 8)

        arena = sb("arena", ARENA)

        def cut(lo, n):
            assert lo + n <= ARENA
            return arena[:, lo:lo + n]

        wt3, wt5, wt7 = cut(0, 3072), cut(3072, 5120), cut(8192, 7168)
        wtd = cut(30976, 3072)
        k0 = cut(34048, 768)
        xh = cut(15360, FULL)
        tN, tX = cut(17408, FULL), cut(19456, FULL)
        gN, gX = cut(21504, 1024), cut(28928, FULL)
        v2k, keyk = cut(21504, G * P), cut(15360, G * P)
        ctxs = [cut(22528, FULL), cut(24576, FULL), cut(26624, FULL)]
        ctx_all = cut(17408, FULL)
        tmp = cut(19456, FULL)
        tmpg = cut(28672, PX)
        small = sb("small", 1200)
        R3 = small[:, 0:128]
        kS, kC, kE = small[:, 128:384], small[:, 384:640], small[:, 640:896]
        kmax, Ey, Rq = small[:, 896:912], small[:, 912:928], small[:, 928:1056]
        vadd = small[:, 1056:1184]
        sm = sb("sm", 64)
        gmax, diag, vrow, vT = sm[:, 0:1], sm[:, 1:17], sm[:, 17:21], sm[:, 21:37]
        vst, vmv, vrs, rden = sm[:, 37:43], sm[:, 43:45], sm[:, 45:46], sm[:, 46:47]
        over, flagf = sm[:, 47:49], sm[:, 49:50]
        oversum = sm[:, 50:51]
        flag = sb("flag", 1, I32)

        omX = cut(0, 32 * PX)
        vsh = [cut(8192 + b * 2560, 2560) for b in range(5)]
        hx = cut(20992, 3 * TAPS * PX)
        hy = cut(27904, 3 * TAPS * PX)
        xh1, xX, dwX = cut(20992, FULL), cut(23040, FULL), cut(25088, FULL)
        turns = sb("turns", 3 * FULL)
        dN = turns[:, 0:FULL]
        omN = [turns[:, FULL:2 * FULL], turns[:, 2 * FULL:3 * FULL]]
        ring = [turns[:, c * 1024:(c + 1) * 1024] for c in range(6)] + [cut(4608 + c * 1024, 1024) for c in range(3)]
        RING = len(ring)
        A = sb("A", 5 * PX)
        fold = [cut(0, TAPS * PX), cut(TAPS * PX, TAPS * PX)]
        oN = dN

        X64 = cut(0, 4096)
        XT, xx = cut(4096, 2048), cut(6144, 2048)
        sq = cut(8192, 2048)
        hm = cut(10240, 4096).bitcast(F16)
        wraw, wsgn = cut(12400, TAPS * P), cut(13600, 576).bitcast(BF16)
        HM = cut(14336, 2048).bitcast(F16)
        HH = cut(16384, 3072).bitcast(F16)
        MM = cut(19456, 3072).bitcast(F16)
        colacc = cut(22528, 48 * P)
        E = [cut(28672, 2048), cut(30720, 2048), cut(32768, 2048), cut(6144, 2048)]
        x2R = omN[0]
        xh2 = dN
        n2, rs = small[:, 0:32], small[:, 32:64]
        rowsum, row16, Ssum, dexp = small[:, 64:96], small[:, 96:128], small[:, 128:160], small[:, 160:192]
        rsS, simii = small[:, 192:224], small[:, 224:256]
        colsum = small[:, 300:332]
        o2, x3R = cut(0, 2048), cut(2048, 2048)

        x3N = cut(4096, 2048)
        sgn = cut(6144, 2048)
        apad = cut(8192, 1296).bitcast(BF16)
        yout = cut(10240, 2048)
        pstat = small[:, 256:272]
        pavg = small[:, 272:288]
        pvar = small[:, 288:296]

        ps = ctx.enter_context(nc.psum_tensor("ps", [P, 4096], F32))[:, :]

        def bank(b, n=512):
            return ps[:, b * 512:b * 512 + n]

        def turned(q, which):
            return bank((3 * q + which) % 8).bitcast(F16)

        free_turned = [[("HHMM", 1)], [("HM", 1)], [("HHMM", 2)], [("HHMM", 3)]]
        conv_order = [(l, i - l) for i in range(G + 2) for l in range(3) if 0 <= i - l < G]

        def to_rows_in(t, nq):
            return view(t, nq * 512, [(HW, HW), (PX, C2), (1, HW)])

        def cols(t, base, slot, nq):
            return view(t, base + nq, [(HW, HW), (slot, 8), (NQ, N4)])

        W = TAPS * PX
        Vd = cut(8192, 4096)
        acc, term = cut(15872, FULL), cut(18432, FULL)
        hxS, hyS, prS = hx[:, 0:W], hy[:, 0:W], hy[:, W:2 * W]
        xprime, wrapped = sb("xprime", 1), sb("wrapped", 1)

        def slow_vector(dve):
            def settle():
                dve.drain()

            dve.wait_ge(sem("iota_ready"), 2)
            for d in range(3):
                px = view(omX, (TAPS + d) * PX, [(3 * PX, 3), (1, PX)])
                dve.tensor_scalar(px, px, xcol[:, 0:1], float(d - 1), ALU.add, ALU.add)
                py = view(omX, 3 * d * PX, [(PX, 3), (1, PX)])
                dve.scalar_tensor_tensor(out=py, in0=py, scalar=float(d - 1), in1=view(ytile, 0, [(0, 3), (1, PX)]),
                                         op0=ALU.add, op1=ALU.add)
            PY, PXc, mask = omX[:, 0:W], omX[:, W:2 * W], omX[:, 2 * W:3 * W]
            dve.tensor_copy(xprime, xcol)
            dve.memset(acc, 0.0)
            for rows in range(2):
                dve.tensor_copy(view(Vd, rows * PX, [(2 * PX, 8), (1, PX)]),
                                view(vsh[2], 2 * HW, [(320, 8), (1, PX)]))
            settle()
            with dve.Fori(0, HW) as r:
                dve.tensor_scalar(hxS, PXc, xprime[:, 0:1], None, ALU.subtract)
                settle()
                dve.scalar_tensor_tensor(out=hxS, in0=hxS, scalar=-1.0, in1=hxS, op0=ALU.mult, op1=ALU.min)
                settle()
                dve.tensor_scalar(hxS, hxS, 1.0, 0.0, ALU.add, ALU.max)
                dve.tensor_scalar(wrapped, xprime, float(HW - 1), -float(HW), ALU.is_ge, ALU.mult)
                settle()
                dve.scalar_tensor_tensor(out=xprime, in0=xprime, scalar=1.0, in1=wrapped, op0=ALU.add, op1=ALU.add)
                with dve.Fori(0, HW) as s:
                    ys = ytile[:, bass.ds(s * HW, PX)]
                    for k in range(TAPS):
                        dve.tensor_tensor(out=hyS[:, k * PX:(k + 1) * PX], in0=PY[:, k * PX:(k + 1) * PX], in1=ys,
                                          op=ALU.subtract)
                    settle()
                    dve.scalar_tensor_tensor(out=hyS, in0=hyS, scalar=-1.0, in1=hyS, op0=ALU.mult, op1=ALU.min)
                    settle()
                    dve.tensor_scalar(hyS, hyS, 1.0, 0.0, ALU.add, ALU.max)
                    settle()
                    dve.tensor_tensor(out=hyS, in0=hyS, in1=mask, op=ALU.mult)
                    settle()
                    dve.tensor_tensor(out=prS, in0=hyS, in1=hxS, op=ALU.mult)
                    settle()
                    dve.tensor_reduce(A[:, 0:PX], view(prS, 0, [(1, PX), (PX, TAPS)]), AX.X, ALU.add)
                    settle()
                    for ch in range(8):
                        dve.tensor_tensor(out=term[:, ch * PX:(ch + 1) * PX], in0=Vd[:, bass.ds(s * HW + ch * 2 * PX, PX)],
                                          in1=A[:, 0:PX], op=ALU.mult)
                    settle()
                    dve.tensor_tensor(out=acc, in0=acc, in1=term, op=ALU.add)
                    settle()
                dve.memset(scr16, 0.0).then_inc(sem("slow_used"), 1)
                dve.wait_ge(sem("slow_turned"), r + 1)
                for rows in range(2):
                    dve.tensor_copy(view(Vd, rows * PX, [(2 * PX, 8), (1, PX)]), view(ps, 0, [(PX, 8), (1, PX)]))
                settle()
                dve.memset(scr16, 0.0).then_inc(sem("slow_copied"), 1)
            dve.wait_ge(sem("slow_copied"), HW)
            dve.tensor_copy(ps[:, 0:FULL], acc).then_inc(sem("window_sum"), 1)

        def slow_tensor(pe):
            with pe.Fori(0, HW) as r:
                pe.wait_ge(sem("slow_used"), r + 1)
                for q in range(4):
                    ins = pe.matmul(bank(q), rot1, view(Vd, q * 4 * PX, [(2 * PX, 2), (1, PX)]), start=True, stop=True)
                ins.then_inc(sem("slow_turned"), 1)
            pe.wait_ge(sem("slow_turned"), HW)

        block = ctx.enter_context(nc.Block())

        def nat(t, c4):
            return dram(t, c4 * 512, [(2048, 8), (65536, 4), (16384, 4), (1, 512)])

        def quad(t, c4):
            return view(t, 0, [(512, 4), (1, 512)], 32 * c4, 32)

        def toeplitz(eng, wt, src, k, done):
            w = 8 * k
            for c8 in range(8):
                eng.dma_start(view(wt, c8 * 16 * w, [(1, 16 * w)], 16 * c8, 16),
                              dram(src, c8 * 256 * w, [(16 * w, 16), (1, 16 * w)])).then_inc(sem(done), 16)

        @block.sync
        def _(sp):
            for c4 in range(C4):
                sp.dma_start(quad(xs, c4), nat(x, c4)).then_inc(sem("x_in"), 16)
            sp.dma_start(raw0, dram(pw0, 0, [(192, 32), (0, 4), (1, 192)])).then_inc(sem("raw0_in"), 16)
            sp.dma_start(sN, dram(bias_n, 0, [(13, 32), (0, 4), (1, 13)])).then_inc(sem("bias_in"), 16)
            sp.wait_ge(sem("wt3_zero"), 1)
            toeplitz(sp, wt3, toep3, 3, "wt3_in")
            sp.wait_ge(sem("wt5_zero"), 1)
            toeplitz(sp, wt5, toep5, 5, "wt5_in")
            sp.wait_ge(sem("wt7_zero"), 1)
            toeplitz(sp, wt7, toep7, 7, "wt7_in")
            sp.wait_ge(sem("wtd_zero"), 1)
            toeplitz(sp, wtd, toepd, 3, "wtd_in")
            sp.dma_start(alphaT[:, :], dram(alpha, 0, [(0, 2), (1, 64)])).then_inc(sem("l3_in"), 16)
            for b in (0, 1, 3, 4):
                s = b - 2
                sp.wait_ge(sem("v0_ready"), 4)
                sp.wait_ge(sem("vsh_zero"), 5)
                lo, n = max(0, -s), P - abs(s)
                sp.dma_start(view(vsh[b], 0, [(1, 2560)], lo, n),
                             view(vsh[2], 0, [(1, 2560)], lo + s, n)).then_inc(sem("vsh_in"), 16)
            sp.wait_ge(sem("l3_in"), 16)
            sp.wait_ge(sem("x2_ready"), 4)
            for c4 in range(C4):
                sp.dma_start(nat(scratch_x2, c4), quad(xs, c4)).then_inc(sem("x2_out"), 16)
            sp.wait_ge(sem("x2_out"), 64)
            sp.wait_ge(sem("X64_in0"), 16)
            sp.wait_ge(sem("X64_in1"), 16)
            sp.dma_start(x2R, dram(scratch_x2, 0, [(64, P), (8192, 32), (1, 64)])).then_inc(sem("x2R_in"), 16)
            sp.wait_ge(sem("wraw_zero"), 1)
            for b2 in range(2):
                sp.dma_start(view(wraw, b2 * 64, [(P, TAPS), (1, 64)], 64 * b2, 64),
                             dram(sign_w, 0, [(576, 64), (64, TAPS), (1, 64)])).then_inc(sem("l3_in"), 16)
            for h in range(2):
                sp.wait_ge(sem("x3_ready"), h + 1)
                sp.dma_start(dram(scratch_x3, h * 131072, [(64, P), (8192, 16), (1, 64)]),
                             x3R[:, h * 1024:(h + 1) * 1024]).then_inc(sem(f"x3_out{h}"), 16)
            for q in range(4):
                sp.wait_ge(sem("y_ready"), q + 1)
                sp.dma_start(dram(out, q * 65536, [(PX, P), (32768, 2), (1, PX)]),
                             view(yout, q * 512, [(PX, 2), (1, PX)])).then_inc(sem("y_out"), 16)
            sp.wait_ge(sem("y_out"), 64)

        @block.gpsimd
        def _(pool):
            done = [0]

            def link(ins):
                ins.then_inc(sem("pool_step"), 1)
                done[0] += 1
                pool.wait_ge(sem("pool_step"), done[0])

            def diagonal(t, col, dims, pattern, base, mult, fill):
                v = view(t, col, dims)
                link(pool.affine_select(out=v, in_=v, compare_op=ALU.not_equal, fill=fill, base=base,
                                        pattern=pattern, channel_multiplier=mult))

            link(pool.memset(ident, 0.0))
            v = ident
            pool.affine_select(out=v, in_=v, compare_op=ALU.not_equal, fill=1.0, base=0,
                               pattern=[[-1, P]], channel_multiplier=1).then_inc(sem("ident_ready"), 1)
            pool.memset(wt5, 0.0).then_inc(sem("wt5_zero"), 1)
            pool.memset(wt7, 0.0).then_inc(sem("wt7_zero"), 1)
            pool.iota(iota_x, pattern=[[1, HW]], base=0, channel_multiplier=0,
                      allow_small_or_imprecise_dtypes=True).then_inc(sem("iota_ready"), 1)
            for t, w, value in ((mean256, 16, 1.0 / 256), (pair_mean, 2, 0.5)):
                link(pool.memset(t, value))
                v = view(t, 0, [(w, P // w), (1, w)])
                link(pool.affine_select(out=v, in_=v, compare_op=ALU.is_ge, fill=0.0, base=0,
                                        pattern=[[-w, P // w], [0, w]], channel_multiplier=1))
                last = pool.affine_select(out=v, in_=v, compare_op=ALU.is_ge, fill=0.0, base=w - 1,
                                          pattern=[[w, P // w], [0, w]], channel_multiplier=-1)
                last.then_inc(sem("means_ready"), 1)
                pool.wait_ge(sem("means_ready"), 1 if w == 16 else 2)
            pool.memset(wtd, 0.0).then_inc(sem("wtd_zero"), 1)
            pool.wait_ge(sem("fold_ready"), 2)
            pool.wait_ge(sem("smallx_in"), 16)
            pool.wait_ge(sem("l0_pw"), 6)
            pool.tensor_tensor(out=view(keyk, 0, [(P, 8), (16, 8), (1, 16)]), in0=view(fold16, 0, [(0, 8), (0, 8), (1, 16)]),
                               in1=view(sX, SX_KEY, [(1, 8), (0, 8), (0, 16)]), op=ALU.mult).then_inc(sem("keyk_ready"), 1)
            pool.wait_ge(sem("small_in"), 48)
            pool.wait_ge(sem("g_turned"), 4)
            pool.tensor_copy(view(v2k, 0, [(16, 64), (1, 16)], 0, 4),
                             view(v2raw, 0, [(1, 64), (0, 16)], 0, 4)).then_inc(sem("v2k_ready"), 1)
            pool.wait_ge(sem("raw12_in"), 32)
            pool.tensor_tensor(out=view(k1, 0, [(4, 640), (1, 4)]), in0=view(raw1, 0, [(1, 640), (0, 4)]),
                               in1=view(fold4, 0, [(0, 640), (1, 4)]), op=ALU.mult).then_inc(sem("k1_ready"), 1)
            pool.tensor_tensor(out=view(k2, 0, [(4, 128), (1, 4)]), in0=view(raw2, 0, [(1, 128), (0, 4)]),
                               in1=view(fold4, 0, [(0, 128), (1, 4)]), op=ALU.mult).then_inc(sem("k2_ready"), 1)
            for t, w, base in ((rot1[:, :], 15, -1), (rot1[:, 15:], 1, 0)):
                if w == 15:
                    link(pool.memset(rot1, 0.0))
                v = view(rot1, 15 - w if w == 1 else 0, [(16, 8), (1, w)]) if w == 15 else view(rot1, 15, [(16, 8), (1, 1)])
                link(pool.affine_select(out=v, in_=v, compare_op=ALU.not_equal, fill=1.0, base=base,
                                        pattern=[[-16, 8], [-1, w]], channel_multiplier=1))
            pool.iota(ytile, pattern=[[0, 2], [1, HW], [0, HW]], base=0, channel_multiplier=0,
                      allow_small_or_imprecise_dtypes=True).then_inc(sem("iota_ready"), 1)
            link(pool.memset(adj, 0.0))
            for d in (0, 16, -16):
                diagonal(adj, 0, [(1, P)], [[-1, P]], d, 1, SPLIT)
            diagonal(adj, 0, [(16, 8), (1, 15)], [[-16, 8], [-1, 15]], -1, 1, SPLIT)
            diagonal(adj, 1, [(16, 8), (1, 15)], [[-16, 8], [-1, 15]], 0, 1, SPLIT)
            diagonal(adj, P, [(1, P)], [[-1, P]], -112, 1, SPLIT)
            diagonal(adj, 2 * P, [(1, P)], [[-1, P]], 0, 1, SPLIT)
            for t, c, s, n in ((adj16, 0, 0, 3 * P), (adj16, 3 * P, 0, P), (adj16, 5 * P, 2 * P, P),
                               (adj_last, 0, 0, 2 * P), (identS, 0, 2 * P, P)):
                link(pool.tensor_copy(t[:, c:c + n], adj[:, s:s + n]))
            link(pool.memset(adj16[:, 4 * P:5 * P], 0.0))
            pool.tensor_copy(ident16, ident).then_inc(sem("graph_ready"), 1)
            pool.wait_ge(sem("l0_done"), 1)
            for b in range(5):
                pool.memset(vsh[b], 0.0).then_inc(sem("vsh_zero"), 1)
            pool.wait_ge(sem("window_done"), 1)
            pool.memset(colacc[:, 0:REACH * P], 0.0).then_inc(sem("col_near"), 1)
            pool.memset(colacc[:, REACH * P:48 * P], 0.0).then_inc(sem("col_far"), 1)
            pool.wait_ge(sem("turn_done"), 12)
            pool.memset(wraw, 0.0).then_inc(sem("wraw_zero"), 1)
            pool.wait_ge(sem("l3_in"), 48)
            link(pool.tensor_scalar(wraw, wraw, 0.0, 2.0, ALU.is_gt, ALU.mult))
            for b2 in range(2):
                link(pool.memset(view(wsgn, 64 * (1 - b2), [(P, TAPS), (1, 64)], 64 * b2, 64), 0.0))
                pool.tensor_scalar(view(wsgn, 64 * b2, [(P, TAPS), (1, 64)], 64 * b2, 64),
                                   view(wraw, 64 * b2, [(P, TAPS), (1, 64)], 64 * b2, 64), 1.0, None,
                                   ALU.subtract).then_inc(sem("wsgn"), 1)
            pool.wait_ge(sem("wsgn"), 2)
            pool.memset(apad, 0.0).then_inc(sem("apad_zero"), 1)

        @block.scalar
        def _(act):
            act.dma_start(sX, dram(small_x, 0, [(SX_N, 8), (0, 16), (1, SX_N)])).then_inc(sem("smallx_in"), 16)
            act.dma_start(keyb, dram(key_b, 0, [(0, P), (1, 1)])).then_inc(sem("small_in"), 16)
            act.dma_start(rowN[0:16, :], dram(row_n, 0, [(0, 16), (1, 12)])).then_inc(sem("small_in"), 16)
            act.dma_start(v2raw[0:4, :], dram(v2_w, 0, [(64, 4), (1, 64)])).then_inc(sem("small_in"), 16)
            act.dma_start(raw1, dram(pw1, 0, [(640, 32), (0, 4), (1, 640)])).then_inc(sem("raw12_in"), 16)
            act.dma_start(raw2, dram(pw2, 0, [(128, 32), (0, 4), (1, 128)])).then_inc(sem("raw12_in"), 16)
            roots = [0]

            def root(dst, src, add_eps=True):
                roots[0] += 1
                act.wait_ge(sem("root_asked"), roots[0])
                act.activation(dst, src, ACT.Sqrt, bias=eps[0:dst.shape[0], :] if add_eps else 0.0).then_inc(sem("root_given"), 1)

            act.wait_ge(sem("ones_ready"), 5)
            root(rstd[:, 0:4], view(mv, 1, [(2, 4)]))
            act.wait_ge(sem("bias_in"), 16)
            for h in range(2):
                for s in range(3):
                    act.wait_ge(sem("l0_pw"), 3 * h + s + 1)
                    o = view(tN, h * 1024 + s * PX, [(512, 2), (1, PX)]) if s < 2 else \
                        view(gN, h * 512, [(PX, 2), (1, PX)])
                    act.activation(o, view(bank(3 * h + s), 0, [(PX, 2), (1, PX)]), ACT.Identity,
                                   bias=sN[:, s:s + 1]).then_inc(sem("l0_pw_bias"), 1)
            for m, (l, g) in enumerate(conv_order):
                act.wait_ge(sem("conv_done"), m + 1)
                act.activation(ctxs[l][:, g * PX:(g + 1) * PX], bank(m % 8, PX), ACT.Gelu).then_inc(sem("gelu"), 1)
            act.wait_ge(sem("key_centred"), 1)
            act.activation(kE, kC, ACT.Exp).then_inc(sem("key_exp"), 1)
            root(vrs[0:16, :], vmv[0:16, 1:2])

            root(rstd[:, 0:4], view(mv, 1, [(2, 4)]))
            for g in range(G):
                act.wait_ge(sem("dw_done"), g - g % 2 + 2)
                act.activation(dwX[:, g * PX:(g + 1) * PX], view(bank(g // 2), (g % 2) * PX, [(1, PX)]),
                               ACT.Identity, bias=sX[:, SX_DWB + g:SX_DWB + g + 1]).then_inc(sem("dw_bias"), 1)
            for s in range(2):
                for h in range(2):
                    act.wait_ge(sem("value_done"), 2 * s + h + 1)
                    act.activation(view(omN[1], h * 1024 + s * PX, [(512, 2), (1, PX)]),
                                   view(bank(4 + 2 * s + h), 0, [(PX, 2), (1, PX)]),
                                   ACT.Identity, bias=sN[:, 11 + s:12 + s]).then_inc(sem("value_bias"), 1)
            W = TAPS * PX
            for js in range(4):
                if js >= 2:
                    t, c, mine = ((hy, 0, "absy"), (hx, W, "absx"))[js - 2]
                    act.wait_ge(sem("maps_turned"), 4 * js)
                    if js == 3:
                        act.wait_ge(sem("value_done"), 4)
                    act.activation(t[:, W:2 * W], omX[:, c:c + W], ACT.Abs).then_inc(sem(mine), 1)
                    act.wait_ge(sem(mine), 1)
                    act.activation(t[:, 0:W], t[:, W:2 * W], ACT.Relu, bias=minus_one[:, :],
                                   accum_out=over[:, js - 2:js - 1]).then_inc(sem("over"), 1)
                if js == 1:
                    act.wait_ge(sem("v0_ready"), 4)
                elif js >= 2:
                    act.wait_ge(sem("maps_turned"), 4 * (js - 1))
                for s in range(2):
                    for h in range(2):
                        act.wait_ge(sem("maps_done"), 4 * js + 2 * s + h + 1)
                        act.activation(view(omN[js % 2], h * 1024 + s * PX, [(512, 2), (1, PX)]),
                                       view(bank(4 * (js % 2) + 2 * s + h), 0, [(PX, 2), (1, PX)]),
                                       ACT.Identity, bias=sN[:, 3 + 2 * js + s:4 + 2 * js + s]).then_inc(sem("maps_bias"), 1)

            root(rstd[:, 0:4], view(mv, 1, [(2, 4)]))
            act.wait_ge(sem("xhat2"), 4)
            for c4 in range(C4):
                act.dma_start(nat(scratch_hat, c4), quad(xh2, c4)).then_inc(sem("hat_out"), 16)
            act.wait_ge(sem("hat_out"), 64)
            for h in range(2):
                act.dma_start(view(X64, h * 2048, [(1, 2048)], 0, 64),
                              dram(scratch_hat, h * 2048, [(4096, 64), (1, 2048)])).then_inc(sem(f"X64_in{h}"), 16)
            for q in range(4):
                act.wait_ge(sem("xt_done"), q + 1)
                act.activation(XT[:, q * 512:(q + 1) * 512], bank(q), ACT.Copy).then_inc(sem("xt"), 1)
                act.wait_ge(sem("xt"), q + 1)
                act.activation(sq[:, q * 512:(q + 1) * 512], XT[:, q * 512:(q + 1) * 512], ACT.Square).then_inc(sem("sq"), 1)
            root(rs, n2, add_eps=False)
            for q in range(4):
                act.wait_ge(sem("xx"), q + 1)
                act.activation(view(hm, q * 2048 + 64, [(256, 8), (1, 64)]), view(xx, q * 512, [(64, 8), (1, 64)]),
                               ACT.Copy).then_inc(sem("h_copy"), 1)
                act.wait_ge(sem("m_half"), q + 1)
                act.activation(view(hm, q * 2048 + 192, [(256, 8), (1, 64)]), view(hm, q * 2048 + 128, [(256, 8), (1, 64)]),
                               ACT.Copy).then_inc(sem("m_copy"), 1)
            for q in range(4):
                act.wait_ge(sem("turn_done"), 3 * q + 2)
                act.activation(HM[:, q * 1024:(q + 1) * 1024], turned(q, 1), ACT.Copy).then_inc(sem("HM"), 1)
            for r in range(2):
                act.wait_ge(sem("far_done"), r + 1)
                act.activation(E[r], ps[:, r * 2048:(r + 1) * 2048], ACT.Exp, scale=0.5 / SPLIT ** 2).then_inc(sem("exp_done"), 1)

            def span_exp(i, k):
                act.wait_ge(sem("span_done"), i + 1)
                act.activation(E[(k + 2) % 4], ps[:, (k % 2) * 2048:(k % 2 + 1) * 2048], ACT.Exp, scale=0.5 / SPLIT ** 2,
                               accum_out=rowsum[:, bass.ds(i, 1)]).then_inc(sem("exp_done"), 1)

            for i in range(4):
                if i >= 2:
                    act.wait_ge(sem("far_sum"), i - 1)
                span_exp(i, i)
            with act.Fori(1, NODE_BLOCKS // 4 - 1) as it:
                for k in range(4):
                    act.wait_ge(sem("col_near"), 4 * it + k - 2)
                    span_exp(4 * it + k, k)
            for i in range(NODE_BLOCKS - 4, NODE_BLOCKS):
                act.wait_ge(sem("col_near"), i - 2)
                span_exp(i, i % 4)
            act.wait_ge(sem("simii"), 1)
            act.activation(dexp, simii, ACT.Exp, scale=0.5, bias=half[:, :]).then_inc(sem("dexp"), 1)
            for h in range(2):
                act.wait_ge(sem(f"x3_out{h}"), 16)
                act.dma_start(view(x3N, h * 1024, [(PX, 4), (1, PX)]),
                              dram(scratch_x3, h * 131072, [(PX, P), (32768, 4), (1, PX)])).then_inc(sem(f"x3N_in{h}"), 16)
            for h in range(2):
                root(rstd[:, 4 * h:4 * h + 4], pvar[:, 4 * h:4 * h + 4])

        @block.vector
        def _(dve):
            done = [0]

            def link(ins):
                ins.then_inc(sem("dve_step"), 1)
                done[0] += 1
                dve.wait_ge(sem("dve_step"), done[0])

            last, roots = [None], [0]

            def inverse_root(t, least=None):
                roots[0] += 1
                last[0].then_inc(sem("root_asked"), 1)
                dve.wait_ge(sem("root_given"), roots[0])
                if least is not None:
                    link(dve.tensor_scalar(t, t, least, None, ALU.max))
                link(dve.reciprocal(t, t))

            def group_norm(dst, ready, before=None):
                for q in range(NQ):
                    if q == 0 and before is not None:
                        before()
                    ins = dve.bn_stats(stats[:, 6 * q:6 * q + 6], xs[:, q * 512:(q + 1) * 512])
                    if q == NQ - 1:
                        link(ins)
                for q in range(NQ):
                    ins = dve.bn_aggr(mv[:, 2 * q:2 * q + 2], stats[:, 6 * q:6 * q + 6])
                last[0] = ins
                inverse_root(rstd[:, 0:4])
                for q in range(NQ):
                    dve.tensor_scalar(dst[:, q * 512:(q + 1) * 512], xs[:, q * 512:(q + 1) * 512], mv[:, 2 * q:2 * q + 1],
                                      rstd[:, q:q + 1], ALU.subtract, ALU.mult).then_inc(sem(ready), 1)

            dve.memset(wt3, 0.0).then_inc(sem("wt3_zero"), 1)
            dve.memset(minus_one, -1.0).then_inc(sem("ones_ready"), 1)
            dve.memset(eps, GN_EPS).then_inc(sem("ones_ready"), 1)
            dve.memset(half, 0.5).then_inc(sem("ones_ready"), 1)
            dve.memset(ones, 1.0).then_inc(sem("ones_ready"), 1)
            dve.memset(eighth, 0.125).then_inc(sem("ones_ready"), 1)
            dve.wait_ge(sem("ident_ready"), 1)
            dve.tensor_reduce(fold4, view(ident, 0, [(1, 4), (4, 32)]), AX.X, ALU.add).then_inc(sem("fold_ready"), 1)
            dve.tensor_reduce(fold16, view(ident, 0, [(1, 16), (16, 8)]), AX.X, ALU.add).then_inc(sem("fold_ready"), 1)
            dve.wait_ge(sem("fold_ready"), 2)
            dve.wait_ge(sem("raw0_in"), 16)
            dve.tensor_tensor(out=view(k0, 0, [(4, 192), (1, 4)]), in0=view(raw0, 0, [(1, 192), (0, 4)]),
                              in1=view(fold4, 0, [(0, 192), (1, 4)]), op=ALU.mult).then_inc(sem("k0_ready"), 1)
            group_norm(xh, "xhat0", lambda: dve.wait_ge(sem("x_in"), 64))
            dve.wait_ge(sem("iota_ready"), 1)
            link(dve.tensor_tensor(out=scr16, in0=fold16, in1=iota_x, op=ALU.mult))
            link(dve.tensor_reduce(xcol, scr16, AX.X, ALU.add))
            for b in range(5):
                s = b - 2
                dve.tensor_scalar(valid[:, b:b + 1], xcol, float(-s if s < 0 else HW - 1 - s), None,
                                  ALU.is_ge if s < 0 else ALU.is_le)
            link(dve.memset(scr16, 0.0))
            dve.tensor_scalar(nvalid, valid, -1.0, None, ALU.mult).then_inc(sem("valid_ready"), 2)

            for h in range(2):
                dve.wait_ge(sem("l0_pw_bias"), 3 * h + 2)
                for nq in (2 * h, 2 * h + 1):
                    dve.transpose(cols(tX, 0, PX, nq), to_rows_in(tN, nq)).then_inc(sem("t_turned"), 1)
            dve.wait_ge(sem("l0_pw_bias"), 6)
            for nq in range(NQ):
                dve.transpose(cols(gX, 0, PX, nq), view(gN, nq * PX, [(HW, HW), (0, C2), (1, HW)])).then_inc(sem("g_turned"), 1)
            dve.wait_ge(sem("g_turned"), 4)
            dve.wait_ge(sem("t_turned"), 4)
            for m, (l, g) in enumerate(conv_order):
                sl = slice(g * PX, (g + 1) * PX)
                gate = gX[:, l * PX:(l + 1) * PX]
                dve.wait_ge(sem("gelu"), m + 1)
                if l == 0:
                    link(dve.tensor_tensor(out=ctx_all[:, sl], in0=ctxs[0][:, sl], in1=gate, op=ALU.mult))
                else:
                    link(dve.tensor_tensor(out=tmpg[:, 0:PX], in0=ctxs[l][:, sl], in1=gate, op=ALU.mult))
                    link(dve.tensor_tensor(out=ctx_all[:, sl], in0=ctx_all[:, sl], in1=tmpg[:, 0:PX], op=ALU.add))
                if l == 2:
                    dve.tensor_reduce(R3[:, g * HW:(g + 1) * HW], view(ctxs[2], g * PX, [(1, HW), (HW, HW)]),
                                      AX.X, ALU.add).then_inc(sem("rows3"), 1)
            dve.wait_ge(sem("glob_done"), 1)
            link(dve.tensor_tensor(out=view(tmp, 0, [(PX, 8), (HW, HW), (1, HW)]),
                                   in0=view(bank(0), 0, [(HW, 8), (0, HW), (1, HW)]),
                                   in1=view(gX, 3 * PX, [(0, 8), (HW, HW), (1, HW)]), op=ALU.mult))
            dve.tensor_tensor(out=ctx_all, in0=ctx_all, in1=tmp, op=ALU.add).then_inc(sem("ctx_all"), 1)
            dve.wait_ge(sem("key_done"), 1)
            dve.wait_ge(sem("small_in"), 48)
            link(dve.tensor_scalar(kS, bank(1, PX), keyb[:, 0:1], None, ALU.add))
            dve.tensor_reduce(kmax, view(kS, 0, [(1, HW), (HW, HW)]), AX.X, ALU.max).then_inc(sem("kmax"), 1)
            dve.wait_ge(sem("kmax_turned"), 1)
            link(dve.tensor_reduce(gmax[0:16, :], view(bank(2), 0, [(1, P)], 0, 16), AX.X, ALU.max))
            dve.tensor_scalar(diag[0:16, :], ident[0:16, 0:16], gmax[0:16, 0:1], None, ALU.mult).then_inc(sem("max_diag"), 1)
            dve.wait_ge(sem("max_spread"), 1)
            dve.tensor_tensor(out=view(kC, 0, [(HW, HW), (1, HW)]), in0=view(kS, 0, [(HW, HW), (1, HW)]),
                              in1=view(bank(3), 0, [(0, HW), (1, HW)]), op=ALU.subtract).then_inc(sem("key_centred"), 1)
            dve.wait_ge(sem("key_exp"), 1)
            dve.wait_ge(sem("ctx_all"), 1)
            link(dve.tensor_tensor(out=view(tmp, 0, [(PX, 8), (1, PX)]), in0=view(ctx_all, 0, [(PX, 8), (1, PX)]),
                                   in1=view(kE, 0, [(0, 8), (1, PX)]), op=ALU.mult))
            dve.tensor_reduce(Ey, view(kE, 0, [(1, HW), (HW, HW)]), AX.X, ALU.add).then_inc(sem("qk_rows"), 1)
            dve.tensor_reduce(view(Rq, 0, [(HW, 8), (1, HW)]), view(tmp, 0, [(PX, 8), (1, HW), (HW, HW)]),
                              AX.X, ALU.add).then_inc(sem("qk_rows"), 1)
            dve.wait_ge(sem("v1_done"), 1)
            link(dve.reciprocal(rden[0:16, :], view(bank(2), 256, [(1, 1)], 0, 16)))
            link(dve.scalar_tensor_tensor(out=vrow[0:16, :], in0=view(bank(2), 128, [(1, 4)], 0, 16),
                                          scalar=rden[0:16, 0:1], in1=rowN[0:16, 0:4], op0=ALU.mult, op1=ALU.add))
            link(dve.bn_stats(vst[0:16, :], vrow[0:16, :]))
            last[0] = dve.bn_aggr(vmv[0:16, :], vst[0:16, :])
            inverse_root(vrs[0:16, :])
            link(dve.tensor_scalar(vrow[0:16, :], vrow[0:16, :], vmv[0:16, 0:1], vrs[0:16, 0:1], ALU.subtract, ALU.mult))
            link(dve.tensor_tensor(out=vrow[0:16, :], in0=vrow[0:16, :], in1=rowN[0:16, 4:8], op=ALU.mult))
            link(dve.tensor_tensor(out=vrow[0:16, :], in0=vrow[0:16, :], in1=rowN[0:16, 8:12], op=ALU.add))
            dve.tensor_scalar(vrow[0:16, :], vrow[0:16, :], 0.0, None, ALU.max).then_inc(sem("v1_relu"), 1)
            dve.wait_ge(sem("v1_turned"), 1)
            dve.tensor_copy(vT[0:4, :], view(bank(2), 320, [(1, HW)], 0, 4)).then_inc(sem("vT"), 1)
            dve.wait_ge(sem("v2_done"), 1)
            link(dve.tensor_tensor(out=view(vadd, 0, [(HW, 8), (1, HW)]), in0=view(bank(3), 128, [(HW, 8), (1, HW)]),
                                   in1=view(sX, SX_V2B, [(1, 8), (0, HW)]), op=ALU.add))
            link(dve.tensor_tensor(out=view(tmp, 0, [(PX, 8), (HW, HW), (1, HW)]),
                                   in0=view(ctx_all, 0, [(PX, 8), (HW, HW), (1, HW)]),
                                   in1=view(vadd, 0, [(HW, 8), (0, HW), (1, HW)]), op=ALU.add))
            for nq in range(NQ):
                ins = dve.transpose(to_rows_in(ctxs[0], nq), cols(tmp, 0, PX, nq))
            link(ins)
            dve.tensor_tensor(out=xs, in0=xs, in1=ctxs[0], op=ALU.add).then_inc(sem("l0_done"), 1)

            dve.wait_ge(sem("l0_done"), 1)
            group_norm(xh1, "xhat1")
            dve.wait_ge(sem("xhat1"), 4)
            for nq in range(NQ):
                dve.transpose(cols(xX, 0, PX, nq), to_rows_in(xh1, nq)).then_inc(sem("xX_turned"), 1)
            dve.wait_ge(sem("dw_bias"), G)
            for nq in range(NQ):
                dve.transpose(to_rows_in(dN, nq), cols(dwX, 0, PX, nq)).then_inc(sem("dN_ready"), 1)
            dve.wait_ge(sem("value_bias"), 4)
            dve.wait_ge(sem("vsh_zero"), 5)
            for nq in range(NQ):
                dve.transpose(cols(vsh[2], 2 * HW, 20 * HW, nq), to_rows_in(omN[1], nq)).then_inc(sem("v0_ready"), 1)
            W = TAPS * PX
            offy, offx, mask = omX[:, 0:W], omX[:, W:2 * W], omX[:, 2 * W:3 * W]

            def turn_maps(js):
                dve.wait_ge(sem("maps_bias"), 4 * js + 4)
                for nq in range(NQ):
                    dve.transpose(cols(omX, 8 * js * PX, PX, nq), to_rows_in(omN[js % 2], nq)).then_inc(sem("maps_turned"), 1)

            turn_maps(0)
            turn_maps(1)
            dve.wait_ge(sem("maps_turned"), 8)
            dve.tensor_scalar(hy[:, 2 * W:3 * W], offy, 0.0, None, ALU.max)
            dve.wait_ge(sem("over"), 1)
            dve.tensor_scalar(hy[:, 0:W], offy, 0.0, -1.0, ALU.min, ALU.mult)
            dve.tensor_scalar(hy[:, W:2 * W], hy[:, W:2 * W], -1.0, 1.0, ALU.mult, ALU.add).then_inc(sem("hats_y"), 1)
            turn_maps(2)
            dve.wait_ge(sem("maps_turned"), 12)
            dve.wait_ge(sem("over"), 2)
            dve.tensor_tensor(out=oversum, in0=over[:, 0:1], in1=over[:, 1:2], op=ALU.add).then_inc(sem("over_rows"), 1)
            for dx in range(3):
                def taps(t, a):
                    return view(t, a * W + dx * PX, [(3 * PX, 3), (1, PX)])
                src = view(omX, (TAPS + dx) * PX, [(3 * PX, 3), (1, PX)])
                dve.tensor_scalar(taps(hx, 0), src, 0.0, nvalid[:, dx:dx + 1], ALU.min, ALU.mult)
                dve.tensor_scalar(taps(hx, 1), taps(hx, 1), nvalid[:, dx + 1:dx + 2], valid[:, dx + 1:dx + 2],
                                  ALU.mult, ALU.add)
                dve.tensor_scalar(taps(hx, 2), src, 0.0, valid[:, dx + 2:dx + 3], ALU.max, ALU.mult).then_inc(sem("hats_x"), 1)
            dve.wait_ge(sem("over_all"), 1)
            link(dve.tensor_scalar(flagf[0:1, :], bank(4)[0:1, 0:1], 0.0, None, ALU.is_gt))
            dve.tensor_copy(flag[0:1, :], flagf[0:1, :]).then_inc(sem("flag"), 1)
            dve.wait_ge(sem("flag"), 1)
            far = dve.value_load(flag[0:1, 0:1], min_val=0, max_val=1)
            dve.wait_ge(sem("hats_x"), 3)
            dve.wait_ge(sem("hats_y"), 1)
            with dve.If(far == 0):
                for k, n in ((0, 6), (6, 3)):
                    if k:
                        turn_maps(3)
                        dve.wait_ge(sem("maps_turned"), 16)
                    for a in range(3):
                        v = hy[:, a * W + k * PX:a * W + (k + n) * PX]
                        dve.tensor_tensor(out=v, in0=v, in1=mask[:, k * PX:(k + n) * PX], op=ALU.mult).then_inc(sem("masked"), 1)
                dve.wait_ge(sem("masked"), 6)
                dve.wait_ge(sem("vsh_in"), 64)
                dve.wait_ge(sem("maps_done"), 16)
                m = 0
                for by in range(5):
                    first = True
                    for dy in range(3):
                        ay = by - dy
                        if not 0 <= ay < 3:
                            continue
                        link(dve.tensor_tensor(out=view(fold[0 if first else 1], 0, [(3 * PX, 3), (PX, 3), (1, PX)]),
                                               in0=view(hy, ay * W + dy * 3 * PX, [(PX, 3), (0, 3), (1, PX)]),
                                               in1=view(hx, dy * 3 * PX, [(PX, 3), (W, 3), (1, PX)]), op=ALU.mult))
                        if not first:
                            link(dve.tensor_tensor(out=fold[0], in0=fold[0], in1=fold[1], op=ALU.add))
                        first = False
                    f, a = fold[0], 0
                    dve.tensor_copy(view(A, a, [(4 * PX, 2), (1, PX)]), view(f, 0, [(8 * PX, 2), (1, PX)]))
                    dve.tensor_tensor(out=view(A, a + PX, [(2 * PX, 2), (1, PX)]), in0=view(f, PX, [(4 * PX, 2), (1, PX)]),
                                      in1=view(f, 3 * PX, [(4 * PX, 2), (1, PX)]), op=ALU.add)
                    link(dve.tensor_tensor(out=view(A, a + 2 * PX, [(1, PX)]), in0=view(f, 2 * PX, [(1, PX)]),
                                           in1=view(f, 4 * PX, [(1, PX)]), op=ALU.add))
                    link(dve.tensor_tensor(out=view(A, a + 2 * PX, [(1, PX)]), in0=view(A, a + 2 * PX, [(1, PX)]),
                                           in1=view(f, 6 * PX, [(1, PX)]), op=ALU.add))
                    for bx in range(5):
                        for hh in range(2):
                            if m >= RING:
                                dve.wait_ge(sem("window_added"), m - RING + 1)
                            dve.tensor_tensor(out=view(ring[m % RING], 0, [(PX, 4), (1, PX)]),
                                              in0=view(vsh[bx], hh * 4 * 320 + by * HW, [(320, 4), (1, PX)]),
                                              in1=view(A, a + bx * PX, [(0, 4), (1, PX)]), op=ALU.mult).then_inc(sem("window_prod"), 1)
                            m += 1
                dve.wait_ge(sem("window_added"), 50)
                dve.memset(scr16, 0.0).then_inc(sem("window_sum"), 1)
            with dve.Else():
                turn_maps(3)
                dve.wait_ge(sem("maps_turned"), 16)
                dve.wait_ge(sem("vsh_in"), 64)
                slow_vector(dve)
            dve.wait_ge(sem("window_sum"), 1)
            for nq in range(NQ):
                dve.transpose(to_rows_in(oN, nq), cols(ps, 0, PX, nq)).then_inc(sem("window_turned"), 1)
            dve.wait_ge(sem("window_turned"), 4)
            dve.memset(scr16, 0.0).then_inc(sem("window_done"), 1)
            for h in range(2):
                for s in range(2):
                    dve.wait_ge(sem("op_done"), 2 * h + s + 1)
                    v = view(xs, h * 1024 + s * PX, [(512, 2), (1, PX)])
                    dve.tensor_tensor(out=v, in0=v, in1=view(bank(4 + 2 * h + s), 0, [(PX, 2), (1, PX)]),
                                      op=ALU.add).then_inc(sem("x2_ready"), 1)

            dve.wait_ge(sem("x2_ready"), 4)
            group_norm(xh2, "xhat2")
            for q in range(4):
                dve.wait_ge(sem("sq"), q + 1)
                last[0] = dve.tensor_reduce(n2[:, 8 * q:8 * q + 8], view(sq, q * 512, [(64, 8), (1, 64)]), AX.X, ALU.add)
            inverse_root(rs, 1e-8)
            link(dve.tensor_scalar(rsS, rs, SPLIT, None, ALU.mult))
            link(dve.tensor_tensor(out=simii, in0=n2, in1=rs, op=ALU.mult))
            dve.tensor_tensor(out=simii, in0=simii, in1=rs, op=ALU.mult).then_inc(sem("simii"), 1)
            for q in range(4):
                dve.tensor_tensor(out=view(xx, q * 512, [(64, 8), (1, 64)]), in0=view(XT, q * 512, [(64, 8), (1, 64)]),
                                  in1=view(rsS, q * 8, [(1, 8), (0, 64)]), op=ALU.mult).then_inc(sem("xx"), 1)
                dve.wait_ge(sem("xx"), q + 1)
                dve.tensor_copy(view(hm, q * 2048, [(256, 8), (1, 64)]),
                                view(xx, q * 512, [(64, 8), (1, 64)])).then_inc(sem("h_half"), 1)
                dve.wait_ge(sem("h_half"), q + 1)
                dve.tensor_tensor(out=view(hm, q * 2048 + 128, [(256, 8), (1, 64)]),
                                  in0=view(xx, q * 512, [(64, 8), (1, 64)]),
                                  in1=view(hm, q * 2048, [(256, 8), (1, 64)]), op=ALU.subtract).then_inc(sem("m_half"), 1)
            for q in range(4):
                for t, (dst, which) in enumerate(((HH, 0), (MM, 2))):
                    dve.wait_ge(sem("turn_done"), 3 * q + which + 1)
                    dve.tensor_copy(dst[:, q * 1024:(q + 1) * 1024], turned(q, which)).then_inc(sem("HHMM"), 1)
            dve.wait_ge(sem("HHMM"), 8)
            dve.tensor_copy(HH[:, 4096:6144], HH[:, 0:2048]).then_inc(sem("HHMM"), 1)
            dve.tensor_copy(MM[:, 4096:6144], MM[:, 0:2048]).then_inc(sem("HHMM"), 1)
            for r in range(2):
                dve.wait_ge(sem("exp_done"), r + 1)
                dve.tensor_reduce(row16[:, 16 * r:16 * r + 16], view(E[r], 0, [(P, 16), (1, P)]), AX.X,
                                  ALU.add).then_inc(sem("far_sum"), 1)

            def add_span(i, k):
                dve.wait_ge(sem("exp_done"), i + 3)
                for name, lo, hi in (("col_far", 8, REACH), ("col_near", 1, 8)):
                    dve.wait_ge(sem(name), i + 1)
                    cc = colacc[:, bass.ds((i + lo) * P, (hi - lo) * P)]
                    dve.tensor_tensor(out=cc, in0=cc, in1=E[(k + 2) % 4][:, lo * P:hi * P], op=ALU.add).then_inc(sem(name), 1)

            with dve.Fori(0, NODE_BLOCKS // 4) as it:
                for k in range(4):
                    add_span(4 * it + k, k)
            dve.wait_ge(sem("col_far"), NODE_BLOCKS + 1)
            dve.wait_ge(sem("col_near"), NODE_BLOCKS + 1)
            dve.tensor_tensor(out=colacc[:, 0:2048], in0=colacc[:, 0:2048], in1=colacc[:, 4096:6144],
                              op=ALU.add).then_inc(sem("col_folded"), 1)
            for h in (1, 0):
                dve.wait_ge(sem("col_turned"), 2 - h)
                ins = dve.tensor_reduce(colsum[:, 16 * h:16 * h + 16], view(ps, (1 - h) * 2048, [(P, 16), (1, P)]), AX.X, ALU.add)
            link(ins)
            link(dve.tensor_tensor(out=Ssum, in0=rowsum, in1=row16, op=ALU.add))
            link(dve.tensor_tensor(out=Ssum, in0=Ssum, in1=colsum, op=ALU.add))
            link(dve.reciprocal(Ssum, Ssum))
            dve.wait_ge(sem("dexp"), 1)
            link(dve.tensor_tensor(out=Ssum, in0=Ssum, in1=dexp, op=ALU.mult))
            dve.wait_ge(sem("x2R_in"), 16)
            for h in range(2):
                c = h * 1024
                link(dve.tensor_tensor(out=view(o2, c, [(64, 16), (1, 64)]), in0=view(XT, c, [(64, 16), (1, 64)]),
                                       in1=view(Ssum, 16 * h, [(1, 16), (0, 64)]), op=ALU.mult))
                dve.scalar_tensor_tensor(out=x3R[:, c:c + 1024], in0=o2[:, c:c + 1024], scalar=0.0, in1=x2R[:, c:c + 1024],
                                         op0=ALU.max, op1=ALU.add).then_inc(sem("x3_ready"), 1)

            dve.wait_ge(sem("apad_zero"), 1)
            for h in range(2):
                dve.wait_ge(sem(f"x3N_in{h}"), 16)
                pst, pav, pvr, rsd = (t[:, 8 * h:8 * h + 8] if t is pstat or t is pavg else t[:, 4 * h:4 * h + 4]
                                      for t in (pstat, pavg, pvar, rstd))
                for b in range(4 * h, 4 * h + 4):
                    ins = dve.bn_stats(stats[:, 6 * b:6 * b + 6], x3N[:, b * PX:(b + 1) * PX])
                link(ins)
                for b in range(4 * h, 4 * h + 4):
                    ins = dve.bn_aggr(mv[:, 2 * b:2 * b + 2], stats[:, 6 * b:6 * b + 6])
                link(ins)
                means, variances = view(mv, 8 * h, [(2, 4)]), view(mv, 8 * h + 1, [(2, 4)])
                dve.tensor_copy(pst[:, 0:4], means)
                link(dve.tensor_tensor(out=pst[:, 4:8], in0=means, in1=means, op=ALU.mult))
                dve.tensor_tensor(out=pst[:, 4:8], in0=pst[:, 4:8], in1=variances, op=ALU.add).then_inc(sem("pstat"), 1)
                dve.wait_ge(sem("pair_done"), h + 1)
                link(dve.tensor_copy(pav, bank(h, 8)))
                link(dve.tensor_tensor(out=pvr, in0=pav[:, 0:4], in1=pav[:, 0:4], op=ALU.mult))
                last[0] = dve.tensor_tensor(out=pvr, in0=pav[:, 4:8], in1=pvr, op=ALU.subtract)
                inverse_root(rsd)
                for b in range(4):
                    v = slice((4 * h + b) * PX, (4 * h + b + 1) * PX)
                    ins = dve.tensor_scalar(sgn[:, v], x3N[:, v], pav[:, b:b + 1], rsd[:, b:b + 1], ALU.subtract, ALU.mult)
                link(ins)
                v = sgn[:, h * 1024:(h + 1) * 1024]
                link(dve.tensor_scalar(v, v, alphaT[:, 0:1], 2.0, ALU.is_gt, ALU.mult))
                dve.tensor_scalar(view(apad, h * 4 * 324 + 19, [(324, 4), (18, 16), (1, 16)]),
                                  view(sgn, h * 1024, [(PX, 4), (16, 16), (1, 16)]), 1.0, None,
                                  ALU.subtract).then_inc(sem("apad"), 1)
            for q in range(4):
                dve.wait_ge(sem("l3_done"), q + 1)
                dve.tensor_tensor(out=yout[:, q * 512:(q + 1) * 512], in0=x3N[:, q * 512:(q + 1) * 512],
                                  in1=bank(2 + q), op=ALU.add).then_inc(sem("y_ready"), 1)

        @block.tensor
        def _(pe):
            def pointwise(dst, w, nset, s, src, h, ready):
                for c2 in range(C2):
                    ins = pe.matmul(dst, w[:, (c2 * nset + s) * P:(c2 * nset + s + 1) * P],
                                    view(src, h * 1024 + c2 * PX, [(512, 2), (1, PX)]), start=(c2 == 0), stop=(c2 == 1))
                ins.then_inc(sem(ready), 1)

            def depthwise(dst, wt, k, src, g, ready):
                r = k // 2
                rows = [0] + [d for d in range(-r, r + 1) if d]
                for n, dy in enumerate(rows):
                    y0, y1 = max(0, -dy), HW - max(0, dy)
                    ins = pe.matmul(view(dst, y0 * HW, [(1, (y1 - y0) * HW)]), view(wt, g * k + dy + r, [(8 * k, P)]),
                                    view(src, g * PX + (y0 + dy) * HW, [(1, (y1 - y0) * HW)]),
                                    start=(n == 0), stop=(n == k - 1))
                ins.then_inc(sem(ready), 1)

            pe.wait_ge(sem("k0_ready"), 1)
            for h in range(2):
                pe.wait_ge(sem("xhat0"), 2 * h + 2)
                for s in range(3):
                    pointwise(bank(3 * h + s), k0, 3, s, xh, h, "l0_pw")
            pe.wait_ge(sem("t_turned"), 4)
            pe.wait_ge(sem("l0_pw_bias"), 6)
            for m, (l, g) in enumerate(conv_order):
                k = (3, 5, 7)[l]
                if g == 0:
                    pe.wait_ge(sem(("wt3_in", "wt5_in", "wt7_in")[l]), 128)
                need = 0 if m < 8 else m - 7
                if l:
                    need = max(need, conv_order.index((l - 1, g)) + 1)
                if need:
                    pe.wait_ge(sem("gelu"), need)
                depthwise(bank(m % 8, PX), (wt3, wt5, wt7)[l], k, (tX, ctxs[0], ctxs[1])[l], g, "conv_done")
            pe.wait_ge(sem("rows3"), G)
            pe.wait_ge(sem("gelu"), 24)
            pe.wait_ge(sem("means_ready"), 2)
            pe.matmul(bank(0, P), mean256, R3, start=True, stop=True).then_inc(sem("glob_done"), 1)
            pe.wait_ge(sem("ctx_all"), 1)
            pe.wait_ge(sem("keyk_ready"), 1)
            for g in range(G):
                ins = pe.matmul(bank(1, PX), keyk[:, g * P:(g + 1) * P], ctx_all[:, g * PX:(g + 1) * PX],
                                start=(g == 0), stop=(g == G - 1))
            ins.then_inc(sem("key_done"), 1)
            pe.wait_ge(sem("kmax"), 1)
            pe.transpose(view(bank(2), 0, [(1, P)], 0, 16), kmax, ident).then_inc(sem("kmax_turned"), 1)
            pe.wait_ge(sem("max_diag"), 1)
            pe.wait_ge(sem("ones_ready"), 5)
            pe.matmul(bank(3, 16), ones[0:16, :], diag[0:16, :], start=True, stop=True).then_inc(sem("max_spread"), 1)
            pe.wait_ge(sem("qk_rows"), 2)
            for g in range(G):
                pe.matmul(view(bank(2), 128, [(1, 4)], 0, 16), Rq[:, g * HW:(g + 1) * HW],
                          sX[:, SX_V1 + 4 * g:SX_V1 + 4 * g + 4], start=(g == 0), stop=(g == G - 1))
            pe.matmul(view(bank(2), 256, [(1, 1)], 0, 16), Ey, eighth, start=True, stop=True).then_inc(sem("v1_done"), 1)
            pe.wait_ge(sem("v1_relu"), 1)
            pe.transpose(view(bank(2), 320, [(1, HW)], 0, 4), vrow[0:16, :], ident[0:16, 0:16]).then_inc(sem("v1_turned"), 1)
            pe.wait_ge(sem("vT"), 1)
            pe.wait_ge(sem("v2k_ready"), 1)
            for g in range(G):
                ins = pe.matmul(view(bank(3), 128 + g * HW, [(1, HW)]), v2k[0:4, g * P:(g + 1) * P], vT[0:4, :],
                                start=True, stop=True)
            ins.then_inc(sem("v2_done"), 1)

            pe.wait_ge(sem("xX_turned"), 4)
            pe.wait_ge(sem("wtd_in"), 128)
            for g in range(G):
                depthwise(view(bank(g // 2), (g % 2) * PX, [(1, PX)]), wtd, 3, xX, g, "dw_done")
            pe.wait_ge(sem("k1_ready"), 1)
            for s in range(2):
                for h in range(2):
                    pointwise(bank(4 + 2 * s + h), k1, 10, 8 + s, xh1, h, "value_done")
            pe.wait_ge(sem("dN_ready"), 4)
            pe.wait_ge(sem("dw_bias"), G)
            def size_of_offsets():
                pe.wait_ge(sem("over_rows"), 1)
                pe.matmul(bank(4)[0:1, 0:1], oversum, ones[:, 0:1], start=True, stop=True).then_inc(sem("over_all"), 1)

            for js in range(4):
                for s in range(2):
                    for h in range(2):
                        if js == 1:
                            pe.wait_ge(sem("value_bias"), 2 * s + h + 1)
                        elif js > 1:
                            pe.wait_ge(sem("maps_bias"), 4 * (js - 2) + 2 * s + h + 1)
                        pointwise(bank(4 * (js % 2) + 2 * s + h), k1, 10, 2 * js + s, dN, h, "maps_done")
            pe.wait_ge(sem("maps_bias"), 13)
            size_of_offsets()
            pe.wait_ge(sem("flag"), 1)
            far = pe.value_load(flag[0:1, 0:1], min_val=0, max_val=1)
            with pe.If(far == 0):
                for m in range(50):
                    pe.wait_ge(sem("window_prod"), m + 1)
                    for q in range(2):
                        ins = pe.matmul(bank(2 * (m % 2) + q), ident, view(ring[m % RING], 512 * q, [(1, 512)]),
                                        start=(m < 2), stop=(m >= 48))
                    ins.then_inc(sem("window_added"), 1)
            with pe.Else():
                slow_tensor(pe)
            pe.wait_ge(sem("window_turned"), 4)
            pe.wait_ge(sem("k2_ready"), 1)
            for h in range(2):
                for s in range(2):
                    pointwise(bank(4 + 2 * h + s), k2, 2, s, oN, h, "op_done")

            for q in range(4):
                pe.wait_ge(sem(f"X64_in{q // 2}"), 16)
                for j in range(8):
                    i = 8 * q + j
                    ins = pe.transpose(view(bank(q), 64 * j, [(1, 64)]), X64[0:64, i * P:(i + 1) * P], ident[0:64, 0:64])
                ins.then_inc(sem("xt_done"), 1)
            pe.wait_ge(sem("graph_ready"), 1)
            pe.wait_ge(sem("xt"), 4)
            pe.wait_ge(sem("x2_ready"), 4)
            for q in range(4):
                pe.wait_ge(sem("h_half"), q + 1)
                pe.wait_ge(sem("m_copy"), q + 1)
                pe.wait_ge(sem("h_copy"), q + 1)
                for which in range(3):
                    t = 3 * q + which
                    if t >= 8:
                        for name, n in free_turned[t - 8]:
                            pe.wait_ge(sem(name), n)
                    for j in range(8):
                        ins = pe.transpose(view(turned(q, which), P * j, [(1, P)]),
                                           view(hm, (8 * q + j) * 256 + 64 * which, [(1, P)]), ident16)
                    ins.then_inc(sem("turn_done"), 1)
            pe.wait_ge(sem("HM"), 4)
            pe.wait_ge(sem("HHMM"), 10)

            def half_products(dst, i, col, n, stop=True):
                w = HM[:, bass.ts(i, P)] if not isinstance(i, int) else HM[:, i * P:(i + 1) * P]
                pe.matmul(dst, w, HH[:, col:col + n], start=True, stop=False)
                return pe.matmul(dst, w, MM[:, col:col + n], start=False, stop=stop)

            for r in range(2):
                for i in range(16 * r, 16 * r + 16):
                    ins = half_products(view(ps, r * 2048 + (i - 16 * r) * P, [(1, P)]), i, (i + 16) * P, P)
                ins.then_inc(sem("far_done"), 1)

            def span(i, k, edges):
                pe.wait_ge(sem("exp_done"), i + 1)
                b0 = (k % 2) * 4
                w = HM[:, bass.ds(i * P, P)]
                for q in range(4):
                    for t, m in enumerate((HH, MM)):
                        ins = pe.matmul(bank(b0 + q), w, m[:, bass.ds(i * P + 512 * q, 512)], start=(t == 0),
                                        stop=(t == 1 and q > 0))
                    if q == 0:
                        ins = pe.matmul(bank(b0, edges.ap[1][1]), identS, edges, start=False, stop=True)
                ins.then_inc(sem("span_done"), 1)

            even, odd = adj16[:, 0:3 * P], adj16[:, 3 * P:6 * P]
            with pe.Fori(0, NODE_BLOCKS // 4 - 1) as it:
                for k in range(4):
                    span(4 * it + k, k, (even, odd)[k % 2])
            for k, edges in enumerate((even, odd, adj_last, adj16[:, 3 * P:4 * P])):
                span(NODE_BLOCKS - 4 + k, k, edges)
            pe.wait_ge(sem("col_far"), NODE_BLOCKS + 1)
            pe.wait_ge(sem("col_near"), NODE_BLOCKS + 1)
            pe.wait_ge(sem("exp_done"), NODE_BLOCKS + 2)
            for h in (1, 0):
                if h == 0:
                    pe.wait_ge(sem("col_folded"), 1)
                for i in range(16):
                    ins = pe.transpose(view(ps, (1 - h) * 2048 + i * P, [(1, P)]), colacc[:, (16 * h + i) * P:(16 * h + i + 1) * P],
                                       ident)
                ins.then_inc(sem("col_turned"), 1)

            def pair_means(h):
                pe.wait_ge(sem("pstat"), h + 1)
                pe.matmul(bank(h, 8), pair_mean, pstat[:, 8 * h:8 * h + 8], start=True, stop=True).then_inc(sem("pair_done"), 1)

            pair_means(0)
            pe.wait_ge(sem("wsgn"), 2)
            for q in range(4):
                if q == 2:
                    pair_means(1)
                pe.wait_ge(sem("apad"), q // 2 + 1)
                for t in range(TAPS):
                    ky, kx = divmod(t, 3)
                    ins = pe.matmul(bank(2 + q), wsgn[:, t * P:(t + 1) * P],
                                    view(apad, 2 * q * 324 + ky * 18 + kx, [(324, 2), (18, 16), (1, 16)]),
                                    start=(t == 0), stop=(t == TAPS - 1))
                ins.then_inc(sem("l3_done"), 1)


def kernel(**inputs):
    import numpy as np
    import concourse.bacc as bacc
    from concourse.bass_utils import run_bass_kernel_spmd as run

    a = {k: np.asarray(v) for k, v in inputs.items()}
    arrays = lay_out(np, a)
    nc = bacc.Bacc("TRN2", target_bir_lowering=False, num_devices=1)
    args = [nc.dram_tensor(f"in_{n}", v.shape, mybir.dt.from_np(v.dtype), kind="ExternalInput").ap()
            for n, v in arrays.items()]
    args.append(nc.dram_tensor("out_0", (B * C * PX,), F32, kind="ExternalOutput").ap())
    bass_preact_convs(nc, *args)
    r = run(nc, [{f"in_{n}": v for n, v in arrays.items()}], core_ids=[0])
    return r.results[0]["out_0"].reshape(B, C, HW, HW)


def lay_out(np, a):
    f = np.float32

    def toeplitz(ws):
        k = ws.shape[-1]
        r = k // 2
        t = np.zeros((8, HW, HW, 8, k), f)
        w = ws.reshape(8, 8, k, k).transpose(1, 0, 2, 3)
        for x in range(HW):
            for x1 in range(max(0, x - r), min(HW, x + r + 1)):
                t[:, x1, x] = w[..., x1 - x + r]
        return t

    def rows(w):
        return w.reshape(-1, 8, 4, 2).transpose(2, 1, 3, 0).reshape(32, 2, -1)

    def outs(v):
        return v.reshape(v.shape[:-1] + (8, 4, 2)).transpose(tuple(range(v.ndim - 1)) + (v.ndim + 1, v.ndim, v.ndim - 1)) \
                .reshape(v.shape[:-1] + (2, 32))

    def gates(v):
        g = np.zeros(v.shape[:-1] + (4, 8), f)
        g[..., 0:4] = v[..., None, :]
        return g.reshape(v.shape[:-1] + (1, 32))

    def groups(v, n):
        m = -(-n // 8) * 8
        t = np.zeros(v.shape[:-2] + (8, m), f)
        t[..., :n] = v
        t = t.reshape(v.shape[:-2] + (4, 2, m // 8, 8))
        d = v.ndim - 2
        return t.transpose(tuple(range(d)) + (d + 2, d + 1, d, d + 3)).reshape(v.shape[:-2] + (m // 8 * 2, 32))

    def maps(v):
        v = v.reshape(v.shape[:-1] + (8, 27))
        return np.concatenate([v[..., 0:18:2], v[..., 1:18:2], v[..., 18:27]], axis=-1)

    w0, b0 = rows(a["L0_conv_conv_w"]), a["L0_conv_conv_b"]
    pw0 = np.concatenate([outs(w0[..., :64]), gates(w0[..., 64:])], axis=2)
    om, vp = rows(a["L1_conv_om_w"]), rows(a["L1_conv_vp_w"])
    pw1 = np.concatenate([groups(maps(om), 27), groups(vp.reshape(32, 2, 8, 8), 8)], axis=2)
    op = a["L1_conv_op_w"].reshape(64, 4, 2, 8).transpose(1, 3, 2, 0).reshape(32, 2, 64)
    bias = np.concatenate([outs(b0[:64]), gates(b0[64:]), groups(maps(a["L1_conv_om_b"]), 27),
                           groups(a["L1_conv_vp_b"].reshape(8, 8), 8)], axis=0)
    small = np.concatenate([a["L0_conv_v1_w"].reshape(4, 8, 8).transpose(2, 1, 0).reshape(8, 32),
                            a["L0_conv_v2_b"].reshape(8, 8).T, a["L1_conv_dw_b"].reshape(8, 8).T,
                            a["L0_conv_key_w"].reshape(8, 8).T], axis=1)
    out = {
        "x": a["x"].reshape(-1), "toep3": toeplitz(a["L0_conv_fw3"]), "toep5": toeplitz(a["L0_conv_fw5"]),
        "toep7": toeplitz(a["L0_conv_fw7"]), "toepd": toeplitz(a["L1_conv_dw_w"]),
        "pw0": pw0, "pw1": pw1, "pw2": outs(op), "bias_n": bias.T, "small_x": small, "key_b": a["L0_conv_key_b"],
        "row_n": np.concatenate([a["L0_conv_v1_b"], a["L0_conv_ln_w"], a["L0_conv_ln_b"]]),
        "v2_w": a["L0_conv_v2_w"].T, "alpha": a["L3_conv_alpha"].reshape(-1),
        "sign_w": a["L3_conv_weight"].transpose(1, 2, 3, 0),
    }
    return {k: np.ascontiguousarray(v).reshape(-1) for k, v in out.items()}
```

```python
from contextlib import ExitStack

import concourse.bass as bass
from concourse import mybir

F32 = mybir.dt.float32
F16 = mybir.dt.float16
BF16 = mybir.dt.bfloat16
I32 = mybir.dt.int32
ALU = mybir.AluOpType
ACT = mybir.ActivationFunctionType
AX = mybir.AxisListType

B, C, HW, PX = 16, 64, 16, 256
P = 128
FULL = B * C * PX // P
NQ, N4 = 4, 4
G, C4, C2 = 8, 4, 2
TAPS = 9
MAPS = 27
NODE_BLOCKS = 32
REACH = 16
ARENA = 34816
SPLIT = 256.0
GN_EPS = 1e-5

SX_V1, SX_V2B, SX_DWB, SX_KEY, SX_N = 0, 32, 40, 48, 56


def bass_preact_convs(nc, x, toep3, toep5, toep7, toepd, pw0, pw1, pw2, bias_n, small_x, key_b,
                      row_n, v2_w, alpha, sign_w, out):
    scratch_hat = nc.dram_tensor("scratch_hat", (B * C * PX,), F32, kind="Internal").ap()
    scratch_x2 = nc.dram_tensor("scratch_x2", (B * C * PX,), F32, kind="Internal").ap()
    scratch_x3 = nc.dram_tensor("scratch_x3", (B * C * PX,), F32, kind="Internal").ap()

    ctx = ExitStack()
    with ctx:
        def sb(name, cols, dt=F32):
            return ctx.enter_context(nc.sbuf_tensor(name, [P, cols], dt))[:, :]

        def view(t, col, dims, p0=0, n=P):
            row = t.ap[0][0]
            return bass.AP(t.tensor, t.offset + p0 * row + col, [[row, n]] + [list(d) for d in dims])

        def dram(t, off, dims):
            return bass.AP(t.tensor, t.offset + off, [list(d) for d in dims])

        sems = {}

        def sem(name):
            if name not in sems:
                sems[name] = ctx.enter_context(nc.semaphore(name))
            return sems[name]

        xs = sb("xs", FULL)
        ident = sb("ident", P)
        fold4 = sb("fold4", N4)
        fold16 = sb("fold16", HW)
        mean256 = sb("mean256", P)
        ones = sb("ones", P)
        pair_mean = sb("pair_mean", P)
        xcol = sb("xcol", 1)
        valid = sb("valid", 5)
        nvalid = sb("nvalid", 5)
        iota_x = sb("iota_x", HW)
        scr16 = sb("scr16", HW)
        adj = sb("adj", 3 * P)
        adj16 = sb("adj16", 6 * P, F16)
        adj_last = sb("adj_last", 2 * P, F16)
        ident16 = sb("ident16", P, F16)
        identS = sb("identS", P, F16)
        raw0, raw1, raw2 = sb("raw0", 192), sb("raw1", 640), sb("raw2", 128)
        k1 = sb("k1", 2560)
        k2 = sb("k2", 512)
        sN = sb("sN", 13)
        sX = sb("sX", SX_N)
        keyb = sb("keyb", 1)
        rowN = sb("rowN", 12)
        v2raw = sb("v2raw", 8)
        alphaT = sb("alphaT", 1)
        minus_one, half, eps = sb("minus_one", 1), sb("half", 1), sb("eps", 1)
        ytile = sb("ytile", 2 * PX)
        rot1 = sb("rot1", P)
        stats = sb("stats", 8 * 6)
        mv = sb("mv", 16)
        rstd = sb("rstd", 8)

        arena = sb("arena", ARENA)

        def cut(lo, n):
            assert lo + n <= ARENA
            return arena[:, lo:lo + n]

        wt3, wt5, wt7 = cut(0, 3072), cut(3072, 5120), cut(8192, 7168)
        wtd = cut(30976, 3072)
        k0 = cut(34048, 768)
        xh = cut(15360, FULL)
        tN, tX = cut(17408, FULL), cut(19456, FULL)
        gN, gX = cut(21504, 1024), cut(28928, FULL)
        v2k, kvk = cut(22400, P), cut(15360, G * P)
        ctxs = [cut(22528, FULL), cut(24576, FULL), cut(26624, FULL)]
        SLOT = PX + HW
        ctx_all = cut(17408, G * SLOT)
        tmp = cut(19584, FULL)
        tmpg = cut(28672, PX)
        small = sb("small", 1200)
        rowsums, Fy, vwide = small[:, 0:16], small[:, 16:32], small[:, 32:64]
        kS, kC, kE = small[:, 128:384], small[:, 384:640], small[:, 640:896]
        kmax, Ey, vaddN = small[:, 896:912], small[:, 912:928], small[:, 928:1056]
        vadd, group_of = small[:, 1056:1184], small[:, 1184:1192]
        vdiag = small[:, 128:256]
        sm = sb("sm", 64)
        gmax, diag, vrow, table_out = sm[:, 0:1], sm[:, 1:17], sm[:, 17:21], sm[:, 60:61]
        vst, vmv, vrs, rden = sm[:, 37:43], sm[:, 43:45], sm[:, 45:46], sm[:, 46:47]
        over = sm[:, 51:55]
        oversum = sm[:, 50:51]
        flag = sb("flag", 1, I32)

        omX = cut(0, 32 * PX)
        vsh = [cut(8192 + b * 2560, 2560) for b in range(5)]
        hx = cut(20992, 3 * TAPS * PX)
        hy = cut(27904, 3 * TAPS * PX)
        xh1, xX, dwX = cut(20992, FULL), cut(23040, FULL), cut(25088, FULL)
        turns = sb("turns", 3 * FULL)
        dN = turns[:, 0:FULL]
        omN = [turns[:, FULL:2 * FULL], turns[:, 2 * FULL:3 * FULL]]
        ring = [turns[:, c * 1024:(c + 1) * 1024] for c in range(6)] + [cut(4608 + c * 1024, 1024) for c in range(3)]
        RING, PRODUCTS = len(ring), 48
        A = sb("A", 3 * PX)
        fold0 = turns[:, 3 * FULL - TAPS * PX:3 * FULL]
        fold = [cut(0, TAPS * PX), cut(TAPS * PX, TAPS * PX)]
        beyond = small.bitcast(BF16)
        oN = dN

        X64 = cut(0, 4096)
        XT, xx = cut(4096, 2048), cut(6144, 2048)
        sq = cut(8192, 2048)
        hm = cut(10240, 4096).bitcast(F16)
        wraw, wsgn = cut(12400, TAPS * P), cut(13600, 576).bitcast(BF16)
        HM = cut(14336, 2048).bitcast(F16)
        HH = cut(16384, 3072).bitcast(F16)
        MM = cut(19456, 3072).bitcast(F16)
        colacc = cut(22528, 48 * P)
        E = [cut(28672, 2048), cut(30720, 2048), cut(32768, 2048), cut(6144, 2048)]
        x2R = omN[0]
        xh2 = dN
        n2, rs = small[:, 0:32], small[:, 32:64]
        rowsum, row16, Ssum, dexp = small[:, 64:96], small[:, 96:128], small[:, 128:160], small[:, 160:192]
        rsS, simii = small[:, 192:224], small[:, 224:256]
        colsum = small[:, 300:332]
        o2, x3R = cut(0, 2048), cut(2048, 2048)

        x3N = cut(4096, 2048)
        sgn = cut(6144, 2048)
        apad = cut(8192, 1296).bitcast(BF16)
        yout = cut(10240, 2048)
        pstat = small[:, 256:272]
        pavg = small[:, 272:288]
        pvar = small[:, 288:296]

        ps = ctx.enter_context(nc.psum_tensor("ps", [P, 4096], F32))[:, :]

        def bank(b, n=512):
            return ps[:, b * 512:b * 512 + n]

        def turned(q, which):
            return bank((3 * q + which) % 8).bitcast(F16)

        free_turned = [[("HHMM", 1)], [("HM", 1)], [("HHMM", 2)], [("HHMM", 3)]]
        CONV_BANKS = 7
        pw_order = [(0, 0), (0, 1), (1, 0), (1, 1), (0, 2), (1, 2)]
        conv_order = [(l, i - l) for i in range(G + 2) for l in range(3) if 0 <= i - l < G]

        def ctx_sums(m):
            return sum(l > 0 for l, g in conv_order[:m + 1])

        def to_rows_in(t, nq):
            return view(t, nq * 512, [(HW, HW), (PX, C2), (1, HW)])

        def cols(t, base, slot, nq):
            return view(t, base + nq, [(HW, HW), (slot, 8), (NQ, N4)])

        W = TAPS * PX
        Vd = cut(8192, 4096)
        acc, term = cut(15872, FULL), cut(18432, FULL)
        hxS, hyS, prS = hx[:, 0:W], hy[:, 0:W], hy[:, W:2 * W]
        xprime, wrapped = sb("xprime", 1), sb("wrapped", 1)

        def slow_vector(dve):
            def settle():
                dve.drain()

            dve.wait_ge(sem("iota_ready"), 2)
            for d in range(3):
                px = view(omX, (2 * TAPS + d) * PX, [(3 * PX, 3), (1, PX)])
                dve.tensor_scalar(px, px, xcol[:, 0:1], float(d - 1), ALU.add, ALU.add)
                py = view(omX, 3 * d * PX, [(PX, 3), (1, PX)])
                dve.scalar_tensor_tensor(out=py, in0=py, scalar=float(d - 1), in1=view(ytile, 0, [(0, 3), (1, PX)]),
                                         op0=ALU.add, op1=ALU.add)
            PY, mask, PXc = omX[:, 0:W], omX[:, W:2 * W], omX[:, 2 * W:3 * W]
            dve.tensor_copy(xprime, xcol)
            dve.memset(acc, 0.0)
            for rows in range(2):
                dve.tensor_copy(view(Vd, rows * PX, [(2 * PX, 8), (1, PX)]),
                                view(vsh[2], 2 * HW, [(320, 8), (1, PX)]))
            settle()
            with dve.Fori(0, HW) as r:
                dve.tensor_scalar(hxS, PXc, xprime[:, 0:1], None, ALU.subtract)
                settle()
                dve.scalar_tensor_tensor(out=hxS, in0=hxS, scalar=-1.0, in1=hxS, op0=ALU.mult, op1=ALU.min)
                settle()
                dve.tensor_scalar(hxS, hxS, 1.0, 0.0, ALU.add, ALU.max)
                dve.tensor_scalar(wrapped, xprime, float(HW - 1), -float(HW), ALU.is_ge, ALU.mult)
                settle()
                dve.scalar_tensor_tensor(out=xprime, in0=xprime, scalar=1.0, in1=wrapped, op0=ALU.add, op1=ALU.add)
                with dve.Fori(0, HW) as s:
                    ys = ytile[:, bass.ds(s * HW, PX)]
                    for k in range(TAPS):
                        dve.tensor_tensor(out=hyS[:, k * PX:(k + 1) * PX], in0=PY[:, k * PX:(k + 1) * PX], in1=ys,
                                          op=ALU.subtract)
                    settle()
                    dve.scalar_tensor_tensor(out=hyS, in0=hyS, scalar=-1.0, in1=hyS, op0=ALU.mult, op1=ALU.min)
                    settle()
                    dve.tensor_scalar(hyS, hyS, 1.0, 0.0, ALU.add, ALU.max)
                    settle()
                    dve.tensor_tensor(out=hyS, in0=hyS, in1=mask, op=ALU.mult)
                    settle()
                    dve.tensor_tensor(out=prS, in0=hyS, in1=hxS, op=ALU.mult)
                    settle()
                    dve.tensor_reduce(A[:, 0:PX], view(prS, 0, [(1, PX), (PX, TAPS)]), AX.X, ALU.add)
                    settle()
                    for ch in range(8):
                        dve.tensor_tensor(out=term[:, ch * PX:(ch + 1) * PX], in0=Vd[:, bass.ds(s * HW + ch * 2 * PX, PX)],
                                          in1=A[:, 0:PX], op=ALU.mult)
                    settle()
                    dve.tensor_tensor(out=acc, in0=acc, in1=term, op=ALU.add)
                    settle()
                dve.memset(scr16, 0.0).then_inc(sem("slow_used"), 1)
                dve.wait_ge(sem("slow_turned"), r + 1)
                for rows in range(2):
                    dve.tensor_copy(view(Vd, rows * PX, [(2 * PX, 8), (1, PX)]), view(ps, 0, [(PX, 8), (1, PX)]))
                settle()
                dve.memset(scr16, 0.0).then_inc(sem("slow_copied"), 1)
            dve.wait_ge(sem("slow_copied"), HW)
            dve.tensor_copy(ps[:, 0:FULL], acc).then_inc(sem("window_sum"), 1)

        def slow_tensor(pe):
            with pe.Fori(0, HW) as r:
                pe.wait_ge(sem("slow_used"), r + 1)
                for q in range(4):
                    ins = pe.matmul(bank(q), rot1, view(Vd, q * 4 * PX, [(2 * PX, 2), (1, PX)]), start=True, stop=True)
                ins.then_inc(sem("slow_turned"), 1)
            pe.wait_ge(sem("slow_turned"), HW)

        block = ctx.enter_context(nc.Block())

        def nat(t, c4):
            return dram(t, c4 * 512, [(2048, 8), (65536, 4), (16384, 4), (1, 512)])

        def quad(t, c4):
            return view(t, 0, [(512, 4), (1, 512)], 32 * c4, 32)

        def toeplitz(eng, wt, src, k, done):
            w = 8 * k
            for c8 in range(8):
                eng.dma_start(view(wt, c8 * 16 * w, [(1, 16 * w)], 16 * c8, 16),
                              dram(src, c8 * 256 * w, [(16 * w, 16), (1, 16 * w)])).then_inc(sem(done), 16)

        @block.sync
        def _(sp):
            for c4 in range(C4):
                sp.dma_start(quad(xs, c4), nat(x, c4)).then_inc(sem("x_in"), 16)
            sp.dma_start(sN, dram(bias_n, 0, [(13, 32), (0, 4), (1, 13)])).then_inc(sem("bias_in"), 16)
            sp.wait_ge(sem("wt3_zero"), 1)
            toeplitz(sp, wt3, toep3, 3, "wt3_in")
            sp.wait_ge(sem("wt5_zero"), 1)
            toeplitz(sp, wt5, toep5, 5, "wt5_in")
            sp.wait_ge(sem("wt7_zero"), 1)
            toeplitz(sp, wt7, toep7, 7, "wt7_in")
            sp.wait_ge(sem("wtd_zero"), 1)
            toeplitz(sp, wtd, toepd, 3, "wtd_in")
            sp.dma_start(alphaT[:, :], dram(alpha, 0, [(0, 2), (1, 64)])).then_inc(sem("l3_in"), 16)
            for b in (0, 1, 3, 4):
                s = b - 2
                sp.wait_ge(sem("v0_ready"), 4)
                sp.wait_ge(sem("vsh_zero"), 5)
                lo, n = max(0, -s), P - abs(s)
                sp.dma_start(view(vsh[b], 0, [(1, 2560)], lo, n),
                             view(vsh[2], 0, [(1, 2560)], lo + s, n)).then_inc(sem("vsh_in"), 16)
            sp.wait_ge(sem("l3_in"), 16)
            sp.wait_ge(sem("x2_ready"), 4)
            for c4 in range(C4):
                sp.dma_start(nat(scratch_x2, c4), quad(xs, c4)).then_inc(sem("x2_out"), 16)
            sp.wait_ge(sem("x2_out"), 64)
            sp.wait_ge(sem("X64_in0"), 16)
            sp.wait_ge(sem("X64_in1"), 16)
            sp.dma_start(x2R, dram(scratch_x2, 0, [(64, P), (8192, 32), (1, 64)])).then_inc(sem("x2R_in"), 16)
            sp.wait_ge(sem("HHMM"), 4)
            for t in (HH, MM):
                sp.dma_start(t[:, 4096:6144], t[:, 0:2048]).then_inc(sem("wrap_in"), 16)
            sp.wait_ge(sem("wraw_zero"), 1)
            for b2 in range(2):
                sp.dma_start(view(wraw, b2 * 64, [(P, TAPS), (1, 64)], 64 * b2, 64),
                             dram(sign_w, 0, [(576, 64), (64, TAPS), (1, 64)])).then_inc(sem("l3_in"), 16)
            for h in (1, 0):
                sp.wait_ge(sem("x3_ready"), 2 - h)
                sp.dma_start(dram(scratch_x3, h * 131072, [(64, P), (8192, 16), (1, 64)]),
                             x3R[:, h * 1024:(h + 1) * 1024]).then_inc(sem(f"x3_out{h}"), 16)
            for i, q in enumerate((2, 3, 0, 1)):
                sp.wait_ge(sem("y_ready"), i + 1)
                sp.dma_start(dram(out, q * 65536, [(PX, P), (32768, 2), (1, PX)]),
                             view(yout, q * 512, [(PX, 2), (1, PX)])).then_inc(sem("y_out"), 16)
            sp.wait_ge(sem("y_out"), 64)

        @block.gpsimd
        def _(pool):
            done = [0]

            def link(ins):
                ins.then_inc(sem("pool_step"), 1)
                done[0] += 1
                pool.wait_ge(sem("pool_step"), done[0])

            def diagonal(t, col, dims, pattern, base, mult, fill):
                v = view(t, col, dims)
                link(pool.affine_select(out=v, in_=v, compare_op=ALU.not_equal, fill=fill, base=base,
                                        pattern=pattern, channel_multiplier=mult))

            link(pool.memset(ident, 0.0))
            v = ident
            pool.affine_select(out=v, in_=v, compare_op=ALU.not_equal, fill=1.0, base=0,
                               pattern=[[-1, P]], channel_multiplier=1).then_inc(sem("ident_ready"), 1)
            pool.memset(wt5, 0.0).then_inc(sem("wt5_zero"), 1)
            pool.memset(wt7, 0.0).then_inc(sem("wt7_zero"), 1)
            pool.iota(iota_x, pattern=[[1, HW]], base=0, channel_multiplier=0,
                      allow_small_or_imprecise_dtypes=True).then_inc(sem("iota_ready"), 1)
            for t, w, value in ((mean256, 16, 1.0 / 256), (pair_mean, 2, 0.5)):
                link(pool.memset(t, value))
                v = view(t, 0, [(w, P // w), (1, w)])
                link(pool.affine_select(out=v, in_=v, compare_op=ALU.is_ge, fill=0.0, base=0,
                                        pattern=[[-w, P // w], [0, w]], channel_multiplier=1))
                last = pool.affine_select(out=v, in_=v, compare_op=ALU.is_ge, fill=0.0, base=w - 1,
                                          pattern=[[w, P // w], [0, w]], channel_multiplier=-1)
                last.then_inc(sem("means_ready"), 1)
                pool.wait_ge(sem("means_ready"), 1 if w == 16 else 2)
            pool.memset(wtd, 0.0).then_inc(sem("wtd_zero"), 1)
            pool.wait_ge(sem("fold_ready"), 3)
            pool.wait_ge(sem("smallx_in"), 16)
            pool.wait_ge(sem("l0_pw"), 6)
            same_x = view(fold16, 0, [(0, 8), (0, 4), (1, HW)])
            pool.tensor_tensor(out=view(kvk, 0, [(P, 8), (HW, 4), (1, HW)]), in0=same_x,
                               in1=view(sX, SX_KEY, [(1, 8), (0, 4), (0, HW)]), op=ALU.mult).then_inc(sem("kvk_ready"), 1)
            pool.tensor_tensor(out=view(kvk, 64, [(P, 8), (HW, 4), (1, HW)]), in0=same_x,
                               in1=view(sX, SX_V1, [(4, 8), (1, 4), (0, HW)]), op=ALU.mult).then_inc(sem("kvk_ready"), 1)
            pool.wait_ge(sem("small_in"), 48)
            pool.wait_ge(sem("g_turned"), 4)
            pool.tensor_copy(view(v2k, 0, [(16, 8), (1, 16)], 0, 32),
                             view(v2raw, 0, [(1, 8), (0, 16)], 0, 32)).then_inc(sem("v2k_ready"), 1)
            pool.wait_ge(sem("raw12_in"), 32)
            pool.tensor_tensor(out=view(k1, 0, [(4, 640), (1, 4)]), in0=view(raw1, 0, [(1, 640), (0, 4)]),
                               in1=view(fold4, 0, [(0, 640), (1, 4)]), op=ALU.mult).then_inc(sem("k1_ready"), 1)
            pool.tensor_tensor(out=view(k2, 0, [(4, 128), (1, 4)]), in0=view(raw2, 0, [(1, 128), (0, 4)]),
                               in1=view(fold4, 0, [(0, 128), (1, 4)]), op=ALU.mult).then_inc(sem("k2_ready"), 1)
            link(pool.memset(rot1, 0.0))
            diagonal(rot1, 0, [(16, 8), (1, 15)], [[-16, 8], [-1, 15]], -1, 1, 1.0)
            diagonal(rot1, 15, [(16, 8)], [[-16, 8]], 0, 1, 1.0)
            pool.iota(ytile, pattern=[[0, 2], [1, HW], [0, HW]], base=0, channel_multiplier=0,
                      allow_small_or_imprecise_dtypes=True).then_inc(sem("iota_ready"), 1)
            link(pool.memset(adj, 0.0))
            for d in (0, 16, -16):
                diagonal(adj, 0, [(1, P)], [[-1, P]], d, 1, SPLIT)
            diagonal(adj, 0, [(16, 8), (1, 15)], [[-16, 8], [-1, 15]], -1, 1, SPLIT)
            diagonal(adj, 1, [(16, 8), (1, 15)], [[-16, 8], [-1, 15]], 0, 1, SPLIT)
            diagonal(adj, P, [(1, P)], [[-1, P]], -112, 1, SPLIT)
            diagonal(adj, 2 * P, [(1, P)], [[-1, P]], 0, 1, SPLIT)
            for t, c, s, n in ((adj16, 0, 0, 3 * P), (adj16, 3 * P, 0, P), (adj16, 5 * P, 2 * P, P),
                               (adj_last, 0, 0, 2 * P), (identS, 0, 2 * P, P)):
                link(pool.tensor_copy(t[:, c:c + n], adj[:, s:s + n]))
            link(pool.memset(adj16[:, 4 * P:5 * P], 0.0))
            pool.tensor_copy(ident16, ident).then_inc(sem("graph_ready"), 1)
            pool.wait_ge(sem("x1_ready"), 8)
            for b in range(5):
                pool.memset(vsh[b], 0.0).then_inc(sem("vsh_zero"), 1)
            pool.wait_ge(sem("window_done"), 1)
            pool.memset(colacc[:, 0:REACH * P], 0.0).then_inc(sem("col_near"), 1)
            pool.memset(colacc[:, REACH * P:48 * P], 0.0).then_inc(sem("col_far"), 1)
            pool.wait_ge(sem("turn_done"), 12)
            pool.memset(wraw, 0.0).then_inc(sem("wraw_zero"), 1)
            pool.wait_ge(sem("l3_in"), 48)
            link(pool.tensor_scalar(wraw, wraw, 0.0, 4.0, ALU.is_gt, ALU.mult))
            for b2 in range(2):
                link(pool.memset(view(wsgn, 64 * (1 - b2), [(P, TAPS), (1, 64)], 64 * b2, 64), 0.0))
                pool.tensor_scalar(view(wsgn, 64 * b2, [(P, TAPS), (1, 64)], 64 * b2, 64),
                                   view(wraw, 64 * b2, [(P, TAPS), (1, 64)], 64 * b2, 64), 2.0, None,
                                   ALU.subtract).then_inc(sem("wsgn"), 1)
            pool.wait_ge(sem("wsgn"), 2)
            pool.memset(apad, 0.0).then_inc(sem("apad_zero"), 1)

        @block.scalar
        def _(act):
            act.dma_start(raw0, dram(pw0, 0, [(192, 32), (0, 4), (1, 192)])).then_inc(sem("raw0_in"), 16)
            def load_table(func):
                act.activation(table_out, eps[:, :], func).then_inc(sem("table"), 1)

            act.wait_ge(sem("ones_ready"), 4)
            load_table(ACT.Sqrt)
            act.dma_start(sX, dram(small_x, 0, [(SX_N, 8), (0, 16), (1, SX_N)])).then_inc(sem("smallx_in"), 16)
            act.wait_ge(sem("keyb_zero"), 1)
            act.dma_start(keyb[0:64, :], dram(key_b, 0, [(0, 64), (1, 1)])).then_inc(sem("small_in"), 16)
            act.dma_start(rowN[0:16, :], dram(row_n, 0, [(0, 16), (1, 12)])).then_inc(sem("small_in"), 16)
            act.dma_start(v2raw[0:32, :], dram(v2_w, 0, [(8, 8), (64, 4), (1, 8)])).then_inc(sem("small_in"), 16)
            act.dma_start(raw1, dram(pw1, 0, [(640, 32), (0, 4), (1, 640)])).then_inc(sem("raw12_in"), 16)
            act.dma_start(raw2, dram(pw2, 0, [(128, 32), (0, 4), (1, 128)])).then_inc(sem("raw12_in"), 16)
            roots = [0]

            def root(dst, src, add_eps=True):
                roots[0] += 1
                act.wait_ge(sem("root_asked"), roots[0])
                act.activation(dst, src, ACT.Sqrt, bias=eps[0:dst.shape[0], :] if add_eps else 0.0).then_inc(sem("root_given"), 1)

            for h in range(2):
                root(rstd[:, 2 * h:2 * h + 2], view(mv, 4 * h + 1, [(2, 2)]))
            act.wait_ge(sem("bias_in"), 16)
            for i, (h, s) in enumerate(pw_order):
                act.wait_ge(sem("l0_pw"), i + 1)
                o = view(tN, h * 1024 + s * PX, [(512, 2), (1, PX)]) if s < 2 else view(gN, h * 512, [(PX, 2), (1, PX)])
                act.activation(o, view(bank(3 * h + s), 0, [(PX, 2), (1, PX)]), ACT.Identity,
                               bias=sN[:, s:s + 1]).then_inc(sem("l0_pw_bias"), 1)
            for m, (l, g) in enumerate(conv_order):
                act.wait_ge(sem("conv_done"), m + 1)
                act.activation(ctxs[l][:, g * PX:(g + 1) * PX], bank(m % CONV_BANKS, PX), ACT.Gelu).then_inc(sem("gelu"), 1)
            act.wait_ge(sem("table"), 1)
            load_table(ACT.Exp)
            act.wait_ge(sem("key_centred"), 1)
            act.activation(kE[64:P, :], kC[0:64, :], ACT.Exp).then_inc(sem("key_exp"), 1)
            act.wait_ge(sem("table"), 2)
            load_table(ACT.Sqrt)
            root(vrs[0:16, :], vmv[0:16, 1:2])

            for h in range(2):
                root(rstd[:, 2 * h:2 * h + 2], view(mv, 4 * h + 1, [(2, 2)]))

            def values(h):
                for s in range(2):
                    act.wait_ge(sem("value_done"), 2 * h + s + 1)
                    act.activation(view(omN[1], h * 1024 + s * PX, [(512, 2), (1, PX)]),
                                   view(bank(4 + 2 * s + h), 0, [(PX, 2), (1, PX)]),
                                   ACT.Identity, bias=sN[:, 11 + s:12 + s]).then_inc(sem("value_bias"), 1)

            values(0)
            for g in range(G):
                act.wait_ge(sem("dw_done"), g - g % 2 + 2)
                act.activation(dwX[:, g * PX:(g + 1) * PX], view(bank(g // 2), (g % 2) * PX, [(1, PX)]),
                               ACT.Identity, bias=sX[:, SX_DWB + g:SX_DWB + g + 1]).then_inc(sem("dw_bias"), 1)
            values(1)

            def evacuate(js, h):
                if js == 1:
                    act.wait_ge(sem("v0_ready"), 4)
                elif js > 1:
                    act.wait_ge(sem("maps_turned"), 4 * (js - 1))
                for s in range(2):
                    act.wait_ge(sem("maps_done"), 4 * js + 2 * h + s + 1)
                    act.activation(view(omN[js % 2], h * 1024 + s * PX, [(512, 2), (1, PX)]),
                                   view(bank(4 * (js % 2) + 2 * s + h), 0, [(PX, 2), (1, PX)]),
                                   ACT.Identity, bias=sN[:, 3 + 2 * js + s:4 + 2 * js + s]).then_inc(sem("maps_bias"), 1)

            W = TAPS * PX

            def sizes(dst, src, n, turned):
                act.wait_ge(sem("maps_turned"), turned)
                act.activation(dst[:, W:W + n], omX[:, src:src + n], ACT.Abs).then_inc(sem("sizes"), 1)

            def go_beyond(col, dst, n):
                act.wait_ge(sem("sizes"), col + 1)
                act.activation(beyond[:, 0:n], dst[:, W:W + n], ACT.Relu, bias=minus_one[:, :],
                               accum_out=over[:, col:col + 1]).then_inc(sem("over"), 1)

            def hats_x(ky, n, sides):
                act.wait_ge(sem("over"), 3 if ky == 0 else 4)
                for dx in range(3):
                    def taps(t, c):
                        return view(t, c + (3 * ky + dx) * PX, [(3 * PX, n), (1, PX)])
                    ins = act.activation(taps(hx, W), taps(hx, W), ACT.Identity, scale=nvalid[:, dx + 1:dx + 2],
                                         bias=valid[:, dx + 1:dx + 2])
                    if sides:
                        act.activation(taps(hx, 0), taps(omX, 2 * W), ACT.Relu, scale=nvalid[:, dx:dx + 1])
                        ins = act.activation(taps(hx, 2 * W), taps(omX, 2 * W), ACT.Relu, scale=valid[:, dx + 2:dx + 3])
                ins.then_inc(sem("hats_x"), 1)

            evacuate(0, 0)
            evacuate(0, 1)
            evacuate(1, 0)
            sizes(hy, 0, 8 * PX, 4)
            evacuate(1, 1)
            go_beyond(0, hy, 8 * PX)
            evacuate(2, 0)
            sizes(hy[:, 8 * PX:], 8 * PX, PX, 8)
            go_beyond(1, hy[:, 8 * PX:], PX)
            evacuate(2, 1)
            evacuate(3, 0)
            sizes(hx, 2 * W, 6 * PX, 12)
            evacuate(3, 1)
            go_beyond(2, hx, 6 * PX)
            hats_x(0, 2, False)
            sizes(hx[:, 6 * PX:], 2 * W + 6 * PX, 3 * PX, 16)
            go_beyond(3, hx[:, 6 * PX:], 3 * PX)
            hats_x(2, 1, True)

            root(rstd[:, 0:4], view(mv, 1, [(2, 4)]))
            act.wait_ge(sem("xhat2"), 4)
            for c4 in range(C4):
                act.dma_start(nat(scratch_hat, c4), quad(xh2, c4)).then_inc(sem("hat_out"), 16)
            act.wait_ge(sem("hat_out"), 64)
            for h in range(2):
                act.dma_start(view(X64, h * 2048, [(1, 2048)], 0, 64),
                              dram(scratch_hat, h * 2048, [(4096, 64), (1, 2048)])).then_inc(sem(f"X64_in{h}"), 16)
            for q in range(4):
                act.wait_ge(sem("xt_done"), q + 1)
                act.activation(sq[:, q * 512:(q + 1) * 512], bank(q), ACT.Square).then_inc(sem("sq"), 1)
            for q in range(4):
                if q == 2:
                    root(rs, n2, add_eps=False)
                act.activation(XT[:, q * 512:(q + 1) * 512], bank(q), ACT.Copy).then_inc(sem("xt"), 1)
            for q in range(5):
                if q < 4:
                    act.wait_ge(sem("xx"), q + 1)
                    act.activation(view(hm, q * 2048, [(256, 8), (64, 2), (1, 64)]), view(xx, q * 512, [(64, 8), (0, 2), (1, 64)]),
                                   ACT.Copy).then_inc(sem("h_half"), 1)
                if q:
                    act.wait_ge(sem("m_half"), q)
                    act.activation(view(hm, q * 2048 - 1856, [(256, 8), (1, 64)]),
                                   view(hm, q * 2048 - 1920, [(256, 8), (1, 64)]), ACT.Copy).then_inc(sem("m_copy"), 1)
            for q in range(4):
                act.wait_ge(sem("turn_done"), 3 * q + 2)
                act.activation(HM[:, q * 1024:(q + 1) * 1024], turned(q, 1), ACT.Copy).then_inc(sem("HM"), 1)
            def span_exp(i, k):
                act.wait_ge(sem("span_done"), i + 1)
                act.activation(E[k], ps[:, (k % 2) * 2048:(k % 2 + 1) * 2048], ACT.Exp, scale=0.5 / SPLIT ** 2,
                               accum_out=rowsum[:, bass.ds(i, 1)]).then_inc(sem("exp_done"), 1)

            for i in range(4):
                span_exp(i, i)
            with act.Fori(1, NODE_BLOCKS // 4) as it:
                for k in range(4):
                    act.wait_ge(sem("col_near"), 4 * it + k - 2)
                    span_exp(4 * it + k, k)
            for t in range(2):
                act.wait_ge(sem("col_near"), NODE_BLOCKS - 2 + t)
                act.wait_ge(sem("far_done"), t + 1)
                for i in range(REACH):
                    c, row = i * P, REACH * (1 - t) + i
                    ins = act.activation(E[t][:, c:c + P], ps[:, t * 2048 + c:t * 2048 + c + P], ACT.Exp,
                                         scale=0.5 / SPLIT ** 2, accum_out=row16[:, row:row + 1])
                ins.then_inc(sem("exp_done"), 1)
                if t == 0:
                    act.wait_ge(sem("simii"), 1)
                    act.activation(dexp, simii, ACT.Exp, scale=0.5, bias=half[:, :]).then_inc(sem("dexp"), 1)
            act.wait_ge(sem("table"), 3)
            load_table(ACT.Sqrt)
            for h in (1, 0):
                act.wait_ge(sem(f"x3_out{h}"), 16)
                act.dma_start(view(x3N, h * 1024, [(PX, 4), (1, PX)]),
                              dram(scratch_x3, h * 131072, [(PX, P), (32768, 4), (1, PX)])).then_inc(sem(f"x3N_in{h}"), 16)
                root(rstd[:, 4 * h:4 * h + 4], pvar[:, 4 * h:4 * h + 4])

        @block.vector
        def _(dve):
            done = [0]

            def link(ins):
                ins.then_inc(sem("dve_step"), 1)
                done[0] += 1
                dve.wait_ge(sem("dve_step"), done[0])

            last, roots = [None], [0]

            def inverse_root(t, least=None, meanwhile=None):
                roots[0] += 1
                last[0].then_inc(sem("root_asked"), 1)
                if meanwhile is not None:
                    meanwhile()
                dve.wait_ge(sem("root_given"), roots[0])
                if least is not None:
                    link(dve.tensor_scalar(t, t, least, None, ALU.max))
                link(dve.reciprocal(t, t))

            def group_norm(dst, ready, before, first=0, n=NQ):
                images = range(first, first + n)
                for q in images:
                    before(q)
                    ins = dve.bn_stats(stats[:, 6 * q:6 * q + 6], xs[:, q * 512:(q + 1) * 512])
                link(ins)
                for q in images:
                    ins = dve.bn_aggr(mv[:, 2 * q:2 * q + 2], stats[:, 6 * q:6 * q + 6])
                last[0] = ins
                inverse_root(rstd[:, first:first + n])
                for q in images:
                    dve.tensor_scalar(dst[:, q * 512:(q + 1) * 512], xs[:, q * 512:(q + 1) * 512], mv[:, 2 * q:2 * q + 1],
                                      rstd[:, q:q + 1], ALU.subtract, ALU.mult).then_inc(sem(ready), 1)

            dve.memset(minus_one, -1.0).then_inc(sem("ones_ready"), 1)
            dve.memset(eps, GN_EPS).then_inc(sem("ones_ready"), 1)
            dve.memset(half, 0.5).then_inc(sem("ones_ready"), 1)
            dve.memset(ones, 1.0).then_inc(sem("ones_ready"), 1)
            dve.memset(keyb, 0.0).then_inc(sem("keyb_zero"), 1)
            dve.memset(wt3, 0.0).then_inc(sem("wt3_zero"), 1)
            dve.wait_ge(sem("ident_ready"), 1)
            dve.tensor_reduce(fold4, view(ident, 0, [(1, 4), (4, 32)]), AX.X, ALU.add).then_inc(sem("fold_ready"), 1)
            dve.tensor_reduce(fold16, view(ident, 0, [(1, 16), (16, 8)]), AX.X, ALU.add).then_inc(sem("fold_ready"), 1)
            dve.tensor_reduce(group_of[0:32, :], view(ident, 0, [(4, 8), (1, 4)], 0, 32), AX.X, ALU.add).then_inc(sem("fold_ready"), 1)
            dve.wait_ge(sem("fold_ready"), 3)
            dve.wait_ge(sem("raw0_in"), 16)
            dve.tensor_tensor(out=view(k0, 0, [(4, 192), (1, 4)]), in0=view(raw0, 0, [(1, 192), (0, 4)]),
                              in1=view(fold4, 0, [(0, 192), (1, 4)]), op=ALU.mult).then_inc(sem("k0_ready"), 1)
            for h in range(2):
                group_norm(xh, "xhat0", lambda q: dve.wait_ge(sem("x_in"), 64), 2 * h, 2)
            dve.wait_ge(sem("iota_ready"), 1)
            link(dve.tensor_tensor(out=scr16, in0=fold16, in1=iota_x, op=ALU.mult))
            link(dve.tensor_reduce(xcol, scr16, AX.X, ALU.add))
            for b in range(5):
                s = b - 2
                dve.tensor_scalar(valid[:, b:b + 1], xcol, float(-s if s < 0 else HW - 1 - s), None,
                                  ALU.is_ge if s < 0 else ALU.is_le)
            link(dve.memset(scr16, 0.0))
            dve.tensor_scalar(nvalid, valid, -1.0, None, ALU.mult).then_inc(sem("valid_ready"), 2)

            for h in range(2):
                dve.wait_ge(sem("l0_pw_bias"), 2 * h + 2)
                for nq in (2 * h, 2 * h + 1):
                    dve.transpose(cols(tX, 0, PX, nq), to_rows_in(tN, nq)).then_inc(sem("t_turned"), 1)
            dve.wait_ge(sem("l0_pw_bias"), 6)
            for nq in range(NQ):
                dve.transpose(cols(gX, 0, PX, nq), view(gN, nq * PX, [(HW, HW), (0, C2), (1, HW)])).then_inc(sem("g_turned"), 1)
            dve.wait_ge(sem("g_turned"), 4)
            dve.wait_ge(sem("t_turned"), 4)
            for m, (l, g) in enumerate(conv_order):
                sl = slice(g * PX, (g + 1) * PX)
                dst = ctx_all[:, g * SLOT:g * SLOT + PX]
                gate = gX[:, l * PX:(l + 1) * PX]
                dve.wait_ge(sem("gelu"), m + 1)
                if l == 0:
                    link(dve.tensor_tensor(out=dst, in0=ctxs[0][:, sl], in1=gate, op=ALU.mult))
                    continue
                if l == 2:
                    dve.tensor_reduce(ctx_all[:, g * SLOT + PX:(g + 1) * SLOT], view(ctxs[2], g * PX, [(1, HW), (HW, HW)]),
                                      AX.X, ALU.add).then_inc(sem("rows3"), 1)
                link(dve.tensor_tensor(out=tmpg[:, 0:PX], in0=ctxs[l][:, sl], in1=gate, op=ALU.mult))
                dve.tensor_tensor(out=dst, in0=dst, in1=tmpg[:, 0:PX], op=ALU.add).then_inc(sem("ctx_summed"), 1)
                dve.wait_ge(sem("ctx_summed"), max(1, ctx_sums(m)))

            def global_gated(h):
                dve.wait_ge(sem("glob_done"), 1)
                link(dve.tensor_tensor(out=view(tmp, h * 1024, [(PX, 4), (HW, HW), (1, HW)]),
                                       in0=view(bank(0), h * 64, [(HW, 4), (0, HW), (1, HW)]),
                                       in1=view(gX, 3 * PX, [(0, 4), (HW, HW), (1, HW)]), op=ALU.mult))

            def global_added(h):
                link(dve.tensor_tensor(out=view(tmp, h * 1024, [(PX, 4), (1, PX)]),
                                       in0=view(ctx_all, 4 * h * SLOT, [(SLOT, 4), (1, PX)]),
                                       in1=view(tmp, h * 1024, [(PX, 4), (1, PX)]), op=ALU.add))

            def turned_back(nq):
                link(dve.transpose(to_rows_in(ctxs[0], nq), cols(tmp, 0, PX, nq)))

            dve.wait_ge(sem("kv_done"), 1)
            dve.tensor_copy(rowsums, bank(7)[:, PX:PX + HW]).then_inc(sem("rowsums"), 1)
            dve.wait_ge(sem("kvg_done"), 1)
            dve.wait_ge(sem("small_in"), 48)
            link(dve.tensor_tensor(out=view(kC, 0, [(HW, HW), (1, HW)]), in0=view(gX, 3 * PX, [(HW, HW), (1, HW)]),
                                   in1=view(bank(1), 0, [(0, HW), (1, HW)]), op=ALU.mult))
            link(dve.scalar_tensor_tensor(out=kS, in0=bank(7, PX), scalar=keyb[:, 0:1], in1=kC, op0=ALU.add, op1=ALU.add))
            dve.tensor_reduce(kmax[0:64, :], view(kS, 0, [(1, HW), (HW, HW)], 0, 64), AX.X, ALU.max).then_inc(sem("kmax"), 1)
            global_gated(0)
            dve.wait_ge(sem("kmax_turned"), 1)
            link(dve.tensor_reduce(gmax[0:16, :], view(bank(2), 0, [(1, 64)], 0, 16), AX.X, ALU.max))
            dve.tensor_scalar(diag[0:16, :], ident[0:16, 0:16], gmax[0:16, 0:1], None, ALU.mult).then_inc(sem("max_diag"), 1)
            global_gated(1)
            dve.wait_ge(sem("max_spread"), 1)
            dve.tensor_tensor(out=view(kC, 0, [(HW, HW), (1, HW)], 0, 64), in0=view(kS, 0, [(HW, HW), (1, HW)], 0, 64),
                              in1=view(bank(3), 0, [(0, HW), (1, HW)], 0, 64), op=ALU.subtract).then_inc(sem("key_centred"), 1)
            global_added(0)
            dve.wait_ge(sem("key_exp"), 1)
            link(dve.tensor_tensor(out=kC[64:P, :], in0=kS[64:P, :], in1=kE[64:P, :], op=ALU.mult))
            dve.tensor_reduce(Ey[64:P, :], view(kE, 0, [(1, HW), (HW, HW)], 64, 64), AX.X, ALU.add).then_inc(sem("v1_rows"), 1)
            dve.tensor_reduce(Fy[64:P, :], view(kC, 0, [(1, HW), (HW, HW)], 64, 64), AX.X, ALU.add).then_inc(sem("v1_rows"), 1)
            global_added(1)
            dve.wait_ge(sem("v1_done"), 1)
            link(dve.reciprocal(rden[0:16, :], view(bank(2), 256, [(1, 1)], 0, 16)))
            link(dve.scalar_tensor_tensor(out=vrow[0:16, :], in0=view(bank(2), 128, [(1, 4)], 0, 16),
                                          scalar=rden[0:16, 0:1], in1=rowN[0:16, 0:4], op0=ALU.mult, op1=ALU.add))
            link(dve.bn_stats(vst[0:16, :], vrow[0:16, :]))
            last[0] = dve.bn_aggr(vmv[0:16, :], vst[0:16, :])
            inverse_root(vrs[0:16, :], meanwhile=lambda: turned_back(0))
            link(dve.tensor_scalar(vrow[0:16, :], vrow[0:16, :], vmv[0:16, 0:1], vrs[0:16, 0:1], ALU.subtract, ALU.mult))
            link(dve.tensor_tensor(out=vrow[0:16, :], in0=vrow[0:16, :], in1=rowN[0:16, 4:8], op=ALU.mult))
            link(dve.tensor_tensor(out=vrow[0:16, :], in0=vrow[0:16, :], in1=rowN[0:16, 8:12], op=ALU.add))
            dve.tensor_scalar(view(vwide, 0, [(4, 8), (1, 4)], 0, 16), view(vrow, 0, [(0, 8), (1, 4)], 0, 16), 0.0, None,
                              ALU.max).then_inc(sem("v1_relu"), 1)
            turned_back(1)
            dve.wait_ge(sem("v1_turned"), 1)
            dve.tensor_tensor(out=view(vdiag, 0, [(HW, 8), (1, HW)], 0, 32), in0=view(group_of, 0, [(1, 8), (0, HW)], 0, 32),
                              in1=view(bank(2), 320, [(0, 8), (1, HW)], 0, 32), op=ALU.mult).then_inc(sem("vdiag"), 1)
            turned_back(2)
            dve.wait_ge(sem("v2_done"), 1)
            link(dve.tensor_tensor(out=view(vadd, 0, [(HW, 8), (1, HW)]), in0=view(bank(3), 128, [(HW, 8), (1, HW)]),
                                   in1=view(sX, SX_V2B, [(1, 8), (0, HW)]), op=ALU.add))
            turned_back(3)
            link(dve.transpose(view(vaddN, 0, [(2 * HW, NQ), (HW, C2), (1, HW)]), view(vadd, 0, [(1, NQ), (HW, 8), (NQ, N4)])))

            def add_context(nq):
                for c2 in range(C2):
                    v = slice(nq * 512 + c2 * PX, nq * 512 + (c2 + 1) * PX)
                    dve.scalar_tensor_tensor(out=xs[:, v], in0=xs[:, v], scalar=vaddN[:, (2 * nq + c2) * HW:(2 * nq + c2) * HW + 1],
                                             in1=ctxs[0][:, v], op0=ALU.add, op1=ALU.add).then_inc(sem("x1_ready"), 1)
                dve.wait_ge(sem("x1_ready"), 2 * nq + 2)


            for h in range(2):
                group_norm(xh1, "xhat1", add_context, 2 * h, 2)
            dve.wait_ge(sem("xhat1"), 4)
            for nq in range(NQ):
                dve.transpose(cols(xX, 0, PX, nq), to_rows_in(xh1, nq)).then_inc(sem("xX_turned"), 1)
            dve.wait_ge(sem("dw_bias"), G)
            for nq in range(NQ):
                dve.transpose(to_rows_in(dN, nq), cols(dwX, 0, PX, nq)).then_inc(sem("dN_ready"), 1)
            dve.wait_ge(sem("vsh_zero"), 5)
            for nq in range(NQ):
                dve.wait_ge(sem("value_bias"), 2 + 2 * (nq // 2))
                dve.transpose(cols(vsh[2], 2 * HW, 20 * HW, nq), to_rows_in(omN[1], nq)).then_inc(sem("v0_ready"), 1)
            W = TAPS * PX
            offy, mask = omX[:, 0:W], omX[:, W:2 * W]

            def turn_maps(js):
                for nq in range(NQ):
                    dve.wait_ge(sem("maps_bias"), 4 * js + 2 + 2 * (nq // 2))
                    dve.transpose(cols(omX, 8 * js * PX, PX, nq), to_rows_in(omN[js % 2], nq)).then_inc(sem("maps_turned"), 1)

            def mask_hats(k, n, distances):
                for a in distances:
                    v = hy[:, a * W + k * PX:a * W + (k + n) * PX]
                    dve.tensor_tensor(out=v, in0=v, in1=mask[:, k * PX:(k + n) * PX], op=ALU.mult).then_inc(sem("masked"), 1)

            def side_hats_y(k, n):
                dve.tensor_scalar(hy[:, 2 * W + k * PX:2 * W + (k + n) * PX], offy[:, k * PX:(k + n) * PX], 0.0, None, ALU.max)
                dve.tensor_scalar(hy[:, k * PX:(k + n) * PX], offy[:, k * PX:(k + n) * PX], 0.0, -1.0, ALU.min,
                                  ALU.mult).then_inc(sem("hats_y"), 1)

            def middle_hats_y(k, n, part):
                dve.wait_ge(sem("over"), part)
                v = hy[:, W + k * PX:W + (k + n) * PX]
                dve.tensor_scalar(v, v, -1.0, 1.0, ALU.mult, ALU.add).then_inc(sem("hats_y"), 1)

            def row_folds(by, bufs):
                first = True
                for dy in range(3):
                    ay = by - dy
                    if not 0 <= ay < 3:
                        continue
                    link(dve.tensor_tensor(out=view(bufs[0 if first else 1], 0, [(3 * PX, 3), (PX, 3), (1, PX)]),
                                           in0=view(hy, ay * W + dy * 3 * PX, [(PX, 3), (0, 3), (1, PX)]),
                                           in1=view(hx, dy * 3 * PX, [(PX, 3), (W, 3), (1, PX)]), op=ALU.mult))
                    if not first:
                        link(dve.tensor_tensor(out=bufs[0], in0=bufs[0], in1=bufs[1], op=ALU.add))
                    first = False

            def row_weights(f):
                link(dve.tensor_tensor(out=A[:, PX:2 * PX], in0=f[:, 2 * PX:3 * PX], in1=f[:, 4 * PX:5 * PX], op=ALU.add))
                dve.tensor_tensor(out=A[:, PX:2 * PX], in0=A[:, PX:2 * PX], in1=f[:, 6 * PX:7 * PX], op=ALU.add)
                link(dve.tensor_tensor(out=view(A, 0, [(2 * PX, 2), (1, PX)]), in0=view(f, PX, [(4 * PX, 2), (1, PX)]),
                                       in1=view(f, 3 * PX, [(4 * PX, 2), (1, PX)]), op=ALU.add))
                return [f[:, 0:PX], A[:, 0:PX], A[:, PX:2 * PX], A[:, 2 * PX:3 * PX], f[:, 8 * PX:9 * PX]]

            turn_maps(0)
            dve.wait_ge(sem("maps_turned"), 4)
            side_hats_y(0, 8)
            turn_maps(1)
            dve.wait_ge(sem("maps_turned"), 8)
            side_hats_y(8, 1)
            dve.wait_ge(sem("hats_y"), 1)
            mask_hats(0, 7, (0, 2))
            middle_hats_y(0, 8, 1)
            dve.wait_ge(sem("hats_y"), 3)
            mask_hats(0, 7, (1,))
            turn_maps(2)
            middle_hats_y(8, 1, 2)
            dve.wait_ge(sem("maps_turned"), 12)
            dve.wait_ge(sem("hats_y"), 4)
            mask_hats(7, 2, (0, 1, 2))
            for a in (0, 2):
                for dx in range(3):
                    ins = dve.tensor_scalar(view(hx, a * W + dx * PX, [(3 * PX, 2), (1, PX)]),
                                            view(omX, 2 * W + dx * PX, [(3 * PX, 2), (1, PX)]), 0.0,
                                            nvalid[:, dx:dx + 1] if a == 0 else valid[:, dx + 2:dx + 3],
                                            ALU.min if a == 0 else ALU.max, ALU.mult)
            ins.then_inc(sem("side_hats_x"), 1)
            turn_maps(3)
            dve.wait_ge(sem("masked"), 6)
            dve.wait_ge(sem("side_hats_x"), 1)
            dve.wait_ge(sem("hats_x"), 1)
            dve.wait_ge(sem("maps_done"), 16)
            dve.wait_ge(sem("maps_turned"), 16)
            row_folds(0, (fold0,))
            dve.wait_ge(sem("over"), 4)
            dve.tensor_reduce(oversum, over, AX.X, ALU.add).then_inc(sem("over_rows"), 1)
            weights = row_weights(fold0)
            dve.wait_ge(sem("over_all"), 1)
            dve.tensor_scalar(flag[0:1, :], bank(4)[0:1, 0:1], 0.0, None, ALU.is_gt).then_inc(sem("flag"), 1)
            dve.wait_ge(sem("flag"), 1)
            far = dve.value_load(flag[0:1, 0:1], min_val=0, max_val=1)
            with dve.If(far == 0):
                dve.wait_ge(sem("vsh_in"), 64)
                m = 0
                for by in range(5):
                    if by:
                        dve.wait_ge(sem("window_prod"), m - 6)
                        row_folds(by, fold)
                        weights = row_weights(fold[0])
                    for bx in (0, 4, 1, 2, 3):
                        for hh in range(2):
                            if m in (3, 5):
                                dve.wait_ge(sem("window_prod"), m - 1)
                            if m == 6:
                                dve.wait_ge(sem("hats_x"), 2)
                            if m >= RING and m < PRODUCTS + 2:
                                dve.wait_ge(sem("window_added"), m - RING + 1)
                            ins = dve.tensor_tensor(out=view(ring[m % RING], 0, [(PX, 4), (1, PX)]),
                                                    in0=view(vsh[bx], hh * 4 * 320 + by * HW, [(320, 4), (1, PX)]),
                                                    in1=view(weights[bx], 0, [(0, 4), (1, PX)]), op=ALU.mult)
                            if m < PRODUCTS:
                                ins.then_inc(sem("window_prod"), 1)
                            else:
                                link(ins)
                                part = ring[(m - 2) % RING]
                                dve.tensor_tensor(out=part, in0=part, in1=ring[m % RING],
                                                  op=ALU.add).then_inc(sem("window_prod"), 1)
                            m += 1
                dve.wait_ge(sem("window_added"), PRODUCTS)
                dve.memset(scr16, 0.0).then_inc(sem("window_sum"), 1)
            with dve.Else():
                dve.wait_ge(sem("maps_turned"), 16)
                dve.wait_ge(sem("hats_x"), 2)
                dve.wait_ge(sem("vsh_in"), 64)
                slow_vector(dve)
            dve.wait_ge(sem("window_sum"), 1)
            for nq in range(NQ):
                dve.transpose(to_rows_in(oN, nq), cols(ps, 0, PX, nq)).then_inc(sem("window_turned"), 1)
            dve.wait_ge(sem("window_turned"), 4)
            dve.memset(scr16, 0.0).then_inc(sem("window_done"), 1)

            def add_output(q):
                if q % 2 == 0:
                    for s in range(2):
                        dve.wait_ge(sem("op_done"), q + s + 1)
                        v = view(xs, q * 512 + s * PX, [(512, 2), (1, PX)])
                        ins = dve.tensor_tensor(out=v, in0=v, in1=view(bank(4 + q + s), 0, [(PX, 2), (1, PX)]), op=ALU.add)
                        ins.then_inc(sem("x2_ready"), 1)
                dve.wait_ge(sem("x2_ready"), 2 * (q // 2) + 2)


            group_norm(xh2, "xhat2", add_output)
            for q in range(4):
                dve.wait_ge(sem("sq"), q + 1)
                last[0] = dve.tensor_reduce(n2[:, 8 * q:8 * q + 8], view(sq, q * 512, [(64, 8), (1, 64)]), AX.X, ALU.add)
            inverse_root(rs, 1e-8)
            link(dve.tensor_scalar(rsS, rs, SPLIT, None, ALU.mult))
            link(dve.tensor_tensor(out=simii, in0=n2, in1=rs, op=ALU.mult))
            dve.tensor_tensor(out=simii, in0=simii, in1=rs, op=ALU.mult).then_inc(sem("simii"), 1)
            for q in range(5):
                if q < 4:
                    dve.wait_ge(sem("xt"), q + 1)
                    dve.tensor_tensor(out=view(xx, q * 512, [(64, 8), (1, 64)]), in0=view(XT, q * 512, [(64, 8), (1, 64)]),
                                      in1=view(rsS, q * 8, [(1, 8), (0, 64)]), op=ALU.mult).then_inc(sem("xx"), 1)
                if q:
                    dve.wait_ge(sem("h_half"), q)
                    dve.tensor_tensor(out=view(hm, q * 2048 - 1920, [(256, 8), (1, 64)]),
                                      in0=view(xx, q * 512 - 512, [(64, 8), (1, 64)]),
                                      in1=view(hm, q * 2048 - 2048, [(256, 8), (1, 64)]), op=ALU.subtract).then_inc(sem("m_half"), 1)
            for q in range(4):
                for t, (dst, which) in enumerate(((HH, 0), (MM, 2))):
                    dve.wait_ge(sem("turn_done"), 3 * q + which + 1)
                    dve.tensor_copy(dst[:, q * 1024:(q + 1) * 1024], turned(q, which)).then_inc(sem("HHMM"), 1)

            def add_span(i, k):
                dve.wait_ge(sem("exp_done"), i + 1)
                for name, lo, hi in (("col_far", 8, REACH), ("col_near", 1, 8)):
                    dve.wait_ge(sem(name), i + 1)
                    cc = colacc[:, bass.ds((i + lo) * P, (hi - lo) * P)]
                    dve.tensor_tensor(out=cc, in0=cc, in1=E[k][:, lo * P:hi * P], op=ALU.add).then_inc(sem(name), 1)

            with dve.Fori(0, NODE_BLOCKS // 4) as it:
                for k in range(4):
                    add_span(4 * it + k, k)
            dve.wait_ge(sem("col_far"), NODE_BLOCKS + 1)
            dve.wait_ge(sem("col_near"), NODE_BLOCKS + 1)
            dve.tensor_tensor(out=colacc[:, 0:2048], in0=colacc[:, 0:2048], in1=colacc[:, 4096:6144],
                              op=ALU.add).then_inc(sem("col_folded"), 1)
            dve.wait_ge(sem("x2R_in"), 16)
            for h in (1, 0):
                n, c = slice(16 * h, 16 * h + 16), h * 1024
                dve.wait_ge(sem("exp_done"), NODE_BLOCKS + 2 - h)
                dve.wait_ge(sem("col_turned"), 2 - h)
                dve.tensor_tensor(out=Ssum[:, n], in0=rowsum[:, n], in1=row16[:, n], op=ALU.add)
                link(dve.tensor_reduce(colsum[:, n], view(ps, (1 - h) * 2048, [(P, 16), (1, P)]), AX.X, ALU.add))
                dve.wait_ge(sem("dexp"), 1)
                link(dve.tensor_tensor(out=Ssum[:, n], in0=Ssum[:, n], in1=colsum[:, n], op=ALU.add))
                link(dve.reciprocal(Ssum[:, n], Ssum[:, n]))
                link(dve.tensor_tensor(out=Ssum[:, n], in0=Ssum[:, n], in1=dexp[:, n], op=ALU.mult))
                link(dve.tensor_tensor(out=view(o2, c, [(64, 16), (1, 64)]), in0=view(XT, c, [(64, 16), (1, 64)]),
                                       in1=view(Ssum, 16 * h, [(1, 16), (0, 64)]), op=ALU.mult))
                dve.scalar_tensor_tensor(out=x3R[:, c:c + 1024], in0=o2[:, c:c + 1024], scalar=0.0, in1=x2R[:, c:c + 1024],
                                         op0=ALU.max, op1=ALU.add).then_inc(sem("x3_ready"), 1)

            dve.wait_ge(sem("apad_zero"), 1)
            for h in (1, 0):
                dve.wait_ge(sem(f"x3N_in{h}"), 16)
                pst, pav, pvr, rsd = (t[:, 8 * h:8 * h + 8] if t is pstat or t is pavg else t[:, 4 * h:4 * h + 4]
                                      for t in (pstat, pavg, pvar, rstd))
                for b in range(4 * h, 4 * h + 4):
                    ins = dve.bn_stats(stats[:, 6 * b:6 * b + 6], x3N[:, b * PX:(b + 1) * PX])
                link(ins)
                for b in range(4 * h, 4 * h + 4):
                    ins = dve.bn_aggr(mv[:, 2 * b:2 * b + 2], stats[:, 6 * b:6 * b + 6])
                link(ins)
                means, variances = view(mv, 8 * h, [(2, 4)]), view(mv, 8 * h + 1, [(2, 4)])
                dve.tensor_copy(pst[:, 0:4], means)
                link(dve.tensor_tensor(out=pst[:, 4:8], in0=means, in1=means, op=ALU.mult))
                dve.tensor_tensor(out=pst[:, 4:8], in0=pst[:, 4:8], in1=variances, op=ALU.add).then_inc(sem("pstat"), 1)
                dve.wait_ge(sem("pair_done"), 2 - h)
                link(dve.tensor_copy(pav, bank(h, 8)))
                link(dve.tensor_tensor(out=pvr, in0=pav[:, 0:4], in1=pav[:, 0:4], op=ALU.mult))
                last[0] = dve.tensor_tensor(out=pvr, in0=pav[:, 4:8], in1=pvr, op=ALU.subtract)
                inverse_root(rsd)
                for b in range(4):
                    v = slice((4 * h + b) * PX, (4 * h + b + 1) * PX)
                    ins = dve.tensor_scalar(sgn[:, v], x3N[:, v], pav[:, b:b + 1], rsd[:, b:b + 1], ALU.subtract, ALU.mult)
                link(ins)
                dve.tensor_scalar(view(apad, h * 4 * 324 + 19, [(324, 4), (18, 16), (1, 16)]),
                                  view(sgn, h * 1024, [(PX, 4), (16, 16), (1, 16)]), alphaT[:, 0:1], 0.5,
                                  ALU.is_gt, ALU.subtract).then_inc(sem("apad"), 1)
            for i, q in enumerate((2, 3, 0, 1)):
                dve.wait_ge(sem("l3_done"), i + 1)
                dve.tensor_tensor(out=yout[:, q * 512:(q + 1) * 512], in0=x3N[:, q * 512:(q + 1) * 512],
                                  in1=bank(2 + q), op=ALU.add).then_inc(sem("y_ready"), 1)

        @block.tensor
        def _(pe):
            def pointwise(dst, w, nset, s, src, h, ready):
                for c2 in range(C2):
                    ins = pe.matmul(dst, w[:, (c2 * nset + s) * P:(c2 * nset + s + 1) * P],
                                    view(src, h * 1024 + c2 * PX, [(512, 2), (1, PX)]), start=(c2 == 0), stop=(c2 == 1))
                ins.then_inc(sem(ready), 1)

            def depthwise(dst, wt, k, src, g, ready):
                r = k // 2
                rows = [0] + [d for d in range(-r, r + 1) if d]
                for n, dy in enumerate(rows):
                    y0, y1 = max(0, -dy), HW - max(0, dy)
                    ins = pe.matmul(view(dst, y0 * HW, [(1, (y1 - y0) * HW)]), view(wt, g * k + dy + r, [(8 * k, P)]),
                                    view(src, g * PX + (y0 + dy) * HW, [(1, (y1 - y0) * HW)]),
                                    start=(n == 0), stop=(n == k - 1))
                ins.then_inc(sem(ready), 1)

            def key_values(g):
                pe.wait_ge(sem("rows3"), g + 1)
                pe.wait_ge(sem("ctx_summed"), ctx_sums(conv_order.index((2, g))))
                pe.wait_ge(sem("kvk_ready"), 2)
                return pe.matmul(bank(7, SLOT), kvk[:, g * P:(g + 1) * P], ctx_all[:, g * SLOT:(g + 1) * SLOT],
                                 start=(g == 0), stop=(g == G - 1))

            def warm_up(n, b=7):
                for _ in range(n):
                    ins = pe.matmul(bank(b, P), ident, ident, start=True, stop=True)
                ins.then_inc(sem("warm"), 1)

            pe.wait_ge(sem("ident_ready"), 1)
            warm_up(20)
            pe.wait_ge(sem("k0_ready"), 1)
            for h, s in pw_order:
                pe.wait_ge(sem("xhat0"), 2 * h + 2)
                pointwise(bank(3 * h + s), k0, 3, s, xh, h, "l0_pw")
            pe.wait_ge(sem("t_turned"), 4)
            for m, (l, g) in enumerate(conv_order):
                k = (3, 5, 7)[l]
                if g == 0:
                    pe.wait_ge(sem(("wt3_in", "wt5_in", "wt7_in")[l]), 128)
                if m == 0:
                    pe.wait_ge(sem("l0_pw_bias"), 4)
                elif m == 2:
                    pe.wait_ge(sem("l0_pw_bias"), 6)
                need = 0 if m < CONV_BANKS else m - CONV_BANKS + 1
                if l:
                    need = max(need, conv_order.index((l - 1, g)) + 1)
                if need:
                    pe.wait_ge(sem("gelu"), need)
                depthwise(bank(m % CONV_BANKS, PX), (wt3, wt5, wt7)[l], k, (tX, ctxs[0], ctxs[1])[l], g, "conv_done")
                if l == 2 and g:
                    key_values(g - 1)
            key_values(G - 1).then_inc(sem("kv_done"), 1)
            pe.wait_ge(sem("gelu"), 24)
            pe.wait_ge(sem("means_ready"), 2)
            pe.matmul(bank(0, P), mean256, view(ctx_all, PX, [(SLOT, G), (1, HW)]), start=True, stop=True).then_inc(sem("glob_done"), 1)
            pe.wait_ge(sem("rowsums"), 1)
            pe.matmul(bank(1, HW), mean256, rowsums, start=True, stop=True).then_inc(sem("kvg_done"), 1)
            pe.wait_ge(sem("kmax"), 1)
            pe.transpose(view(bank(2), 0, [(1, 64)], 0, 16), kmax[0:64, :], ident[0:64, 0:64]).then_inc(sem("kmax_turned"), 1)
            pe.wait_ge(sem("max_diag"), 1)
            pe.wait_ge(sem("ones_ready"), 4)
            pe.matmul(view(bank(3), 0, [(1, 16)], 0, 64), ones[0:16, 0:64], diag[0:16, :], start=True,
                      stop=True).then_inc(sem("max_spread"), 1)
            pe.wait_ge(sem("v1_rows"), 2)
            pe.matmul(view(bank(2), 128, [(1, 4)], 0, 16), Fy[64:P, :], view(mean256, 64, [(HW, 4)], 64, 64), start=True, stop=True)
            pe.matmul(view(bank(2), 256, [(1, 1)], 0, 16), Ey[64:P, :], view(mean256, 64, [(1, 1)], 64, 64), start=True,
                      stop=True).then_inc(sem("v1_done"), 1)
            pe.wait_ge(sem("v1_relu"), 1)
            pe.transpose(view(bank(2), 320, [(1, HW)], 0, 32), vwide[0:16, :], ident[0:16, 0:16]).then_inc(sem("v1_turned"), 1)
            pe.wait_ge(sem("vdiag"), 1)
            pe.wait_ge(sem("v2k_ready"), 1)
            pe.matmul(bank(3)[:, 128:256], v2k[0:32, :], vdiag[0:32, :], start=True, stop=True).then_inc(sem("v2_done"), 1)

            pe.wait_ge(sem("x1_ready"), 4)
            warm_up(8)

            def values(h):
                for s in range(2):
                    pointwise(bank(4 + 2 * s + h), k1, 10, 8 + s, xh1, h, "value_done")

            pe.wait_ge(sem("k1_ready"), 1)
            pe.wait_ge(sem("xhat1"), 2)
            values(0)
            pe.wait_ge(sem("xX_turned"), 4)
            pe.wait_ge(sem("wtd_in"), 128)
            for g in range(G):
                depthwise(view(bank(g // 2), (g % 2) * PX, [(1, PX)]), wtd, 3, xX, g, "dw_done")
            values(1)
            pe.wait_ge(sem("dN_ready"), 4)
            pe.wait_ge(sem("dw_bias"), G)

            def size_of_offsets():
                pe.wait_ge(sem("over_rows"), 1)
                pe.matmul(bank(4)[0:1, 0:1], oversum, ones[:, 0:1], start=True, stop=True).then_inc(sem("over_all"), 1)

            for js in range(4):
                for h in range(2):
                    for s in range(2):
                        if js == 1:
                            pe.wait_ge(sem("value_bias"), 2 * h + s + 1)
                        elif js > 1:
                            pe.wait_ge(sem("maps_bias"), 4 * (js - 2) + 2 * h + s + 1)
                        pointwise(bank(4 * (js % 2) + 2 * s + h), k1, 10, 2 * js + s, dN, h, "maps_done")
            pe.wait_ge(sem("maps_bias"), 13)
            size_of_offsets()
            pe.wait_ge(sem("flag"), 1)
            far = pe.value_load(flag[0:1, 0:1], min_val=0, max_val=1)
            with pe.If(far == 0):
                for m in range(PRODUCTS):
                    pe.wait_ge(sem("window_prod"), m + 1 if m < PRODUCTS - 2 else m + 3)
                    for q in range(2):
                        ins = pe.matmul(bank(2 * (m % 2) + q), ident, view(ring[m % RING], 512 * q, [(1, 512)]),
                                        start=(m < 2), stop=(m >= PRODUCTS - 2))
                    ins.then_inc(sem("window_added"), 1)
            with pe.Else():
                slow_tensor(pe)
            pe.wait_ge(sem("k2_ready"), 1)
            for h in range(2):
                pe.wait_ge(sem("window_turned"), 2 * h + 2)
                for s in range(2):
                    pointwise(bank(4 + 2 * h + s), k2, 2, s, oN, h, "op_done")

            for q in range(4):
                pe.wait_ge(sem(f"X64_in{q // 2}"), 16)
                for j in range(8):
                    i = 8 * q + j
                    ins = pe.transpose(view(bank(q), 64 * j, [(1, 64)]), X64[0:64, i * P:(i + 1) * P], ident[0:64, 0:64])
                ins.then_inc(sem("xt_done"), 1)
            pe.wait_ge(sem("graph_ready"), 1)
            pe.wait_ge(sem("x2_ready"), 4)
            pe.wait_ge(sem("xt"), 4)
            warm_up(10)
            for q in range(4):
                pe.wait_ge(sem("h_half"), q + 1)
                pe.wait_ge(sem("m_half"), q + 1)
                pe.wait_ge(sem("m_copy"), q + 1)
                for which in range(3):
                    t = 3 * q + which
                    if t >= 8:
                        for name, n in free_turned[t - 8]:
                            pe.wait_ge(sem(name), n)
                    for j in range(8):
                        ins = pe.transpose(view(turned(q, which), P * j, [(1, P)]),
                                           view(hm, (8 * q + j) * 256 + 64 * which, [(1, P)]), ident16)
                    ins.then_inc(sem("turn_done"), 1)
            pe.wait_ge(sem("HM"), 4)
            pe.wait_ge(sem("HHMM"), 8)

            def half_products(dst, i, col, n):
                w = HM[:, i * P:(i + 1) * P]
                pe.matmul(dst, w, HH[:, col:col + n], start=True, stop=False)
                return pe.matmul(dst, w, MM[:, col:col + n], start=False, stop=True)

            def span(i, k, edges):
                if not isinstance(i, int) or i >= 2:
                    pe.wait_ge(sem("exp_done"), i - 1)
                b0 = (k % 2) * 4
                w = HM[:, bass.ds(i * P, P)]
                for q in range(4):
                    for t, m in enumerate((HH, MM)):
                        ins = pe.matmul(bank(b0 + q), w, m[:, bass.ds(i * P + 512 * q, 512)], start=(t == 0),
                                        stop=(t == 1 and q > 0))
                    if q == 0:
                        ins = pe.matmul(bank(b0, edges.ap[1][1]), identS, edges, start=False, stop=True)
                ins.then_inc(sem("span_done"), 1)

            even, odd = adj16[:, 0:3 * P], adj16[:, 3 * P:6 * P]
            for k in range(4):
                span(k, k, (even, odd)[k % 2])
            pe.wait_ge(sem("wrap_in"), 32)
            with pe.Fori(1, NODE_BLOCKS // 4 - 1) as it:
                for k in range(4):
                    span(4 * it + k, k, (even, odd)[k % 2])
            for k, edges in enumerate((even, odd, adj_last, adj16[:, 3 * P:4 * P])):
                span(NODE_BLOCKS - 4 + k, k, edges)
            for t in range(2):
                pe.wait_ge(sem("exp_done"), NODE_BLOCKS - 1 + t)
                for i in range(REACH):
                    ins = half_products(view(ps, t * 2048 + i * P, [(1, P)]), i + REACH * (1 - t), (i + REACH * t) * P, P)
                ins.then_inc(sem("far_done"), 1)
            pe.wait_ge(sem("col_far"), NODE_BLOCKS + 1)
            pe.wait_ge(sem("col_near"), NODE_BLOCKS + 1)
            for h in (1, 0):
                pe.wait_ge(sem("exp_done"), NODE_BLOCKS + 2 - h)
                if h == 0:
                    pe.wait_ge(sem("col_folded"), 1)
                for i in range(16):
                    ins = pe.transpose(view(ps, (1 - h) * 2048 + i * P, [(1, P)]), colacc[:, (16 * h + i) * P:(16 * h + i + 1) * P],
                                       ident)
                ins.then_inc(sem("col_turned"), 1)

            def pair_means(h):
                pe.wait_ge(sem("pstat"), 2 - h)
                pe.matmul(bank(h, 8), pair_mean, pstat[:, 8 * h:8 * h + 8], start=True, stop=True).then_inc(sem("pair_done"), 1)

            pair_means(1)
            warm_up(7, 0)
            pe.wait_ge(sem("wsgn"), 2)
            pe.wait_ge(sem("warm"), 4)
            for i, q in enumerate((2, 3, 0, 1)):
                pe.wait_ge(sem("apad"), i // 2 + 1)
                for t in range(TAPS):
                    ky, kx = divmod(t, 3)
                    ins = pe.matmul(bank(2 + q), wsgn[:, t * P:(t + 1) * P],
                                    view(apad, 2 * q * 324 + ky * 18 + kx, [(324, 2), (18, 16), (1, 16)]),
                                    start=(t == 0), stop=(t == TAPS - 1))
                ins.then_inc(sem("l3_done"), 1)
                if i == 0:
                    pair_means(0)


def kernel(**inputs):
    import numpy as np
    import concourse.bacc as bacc
    from concourse.bass_utils import run_bass_kernel_spmd as run

    a = {k: np.asarray(v) for k, v in inputs.items()}
    arrays = lay_out(np, a)
    nc = bacc.Bacc("TRN2", target_bir_lowering=False, num_devices=1)
    args = [nc.dram_tensor(f"in_{n}", v.shape, mybir.dt.from_np(v.dtype), kind="ExternalInput").ap()
            for n, v in arrays.items()]
    args.append(nc.dram_tensor("out_0", (B * C * PX,), F32, kind="ExternalOutput").ap())
    bass_preact_convs(nc, *args)
    r = run(nc, [{f"in_{n}": v for n, v in arrays.items()}], core_ids=[0])
    return r.results[0]["out_0"].reshape(B, C, HW, HW)


def lay_out(np, a):
    f = np.float32

    def toeplitz(ws):
        k = ws.shape[-1]
        r = k // 2
        t = np.zeros((8, HW, HW, 8, k), f)
        w = ws.reshape(8, 8, k, k).transpose(1, 0, 2, 3)
        for x in range(HW):
            for x1 in range(max(0, x - r), min(HW, x + r + 1)):
                t[:, x1, x] = w[..., x1 - x + r]
        return t

    def rows(w):
        return w.reshape(-1, 8, 4, 2).transpose(2, 1, 3, 0).reshape(32, 2, -1)

    def outs(v):
        return v.reshape(v.shape[:-1] + (8, 4, 2)).transpose(tuple(range(v.ndim - 1)) + (v.ndim + 1, v.ndim, v.ndim - 1)) \
                .reshape(v.shape[:-1] + (2, 32))

    def gates(v):
        g = np.zeros(v.shape[:-1] + (4, 8), f)
        g[..., 0:4] = v[..., None, :]
        return g.reshape(v.shape[:-1] + (1, 32))

    def groups(v, n):
        m = -(-n // 8) * 8
        t = np.zeros(v.shape[:-2] + (8, m), f)
        t[..., :n] = v
        t = t.reshape(v.shape[:-2] + (4, 2, m // 8, 8))
        d = v.ndim - 2
        return t.transpose(tuple(range(d)) + (d + 2, d + 1, d, d + 3)).reshape(v.shape[:-2] + (m // 8 * 2, 32))

    def maps(v):
        v = v.reshape(v.shape[:-1] + (8, 27))
        return np.concatenate([v[..., 0:18:2], v[..., 18:27], v[..., 1:18:2]], axis=-1)

    w0, b0 = rows(a["L0_conv_conv_w"]), a["L0_conv_conv_b"]
    pw0 = np.concatenate([outs(w0[..., :64]), gates(w0[..., 64:])], axis=2)
    om, vp = rows(a["L1_conv_om_w"]), rows(a["L1_conv_vp_w"])
    pw1 = np.concatenate([groups(maps(om), 27), groups(vp.reshape(32, 2, 8, 8), 8)], axis=2)
    op = a["L1_conv_op_w"].reshape(64, 4, 2, 8).transpose(1, 3, 2, 0).reshape(32, 2, 64)
    bias = np.concatenate([outs(b0[:64]), gates(b0[64:]), groups(maps(a["L1_conv_om_b"]), 27),
                           groups(a["L1_conv_vp_b"].reshape(8, 8), 8)], axis=0)
    small = np.concatenate([a["L0_conv_v1_w"].reshape(4, 8, 8).transpose(2, 1, 0).reshape(8, 32),
                            a["L0_conv_v2_b"].reshape(8, 8).T, a["L1_conv_dw_b"].reshape(8, 8).T,
                            a["L0_conv_key_w"].reshape(8, 8).T], axis=1)
    out = {
        "x": a["x"].reshape(-1), "toep3": toeplitz(a["L0_conv_fw3"]), "toep5": toeplitz(a["L0_conv_fw5"]),
        "toep7": toeplitz(a["L0_conv_fw7"]), "toepd": toeplitz(a["L1_conv_dw_w"]),
        "pw0": pw0, "pw1": pw1, "pw2": outs(op), "bias_n": bias.T, "small_x": small, "key_b": a["L0_conv_key_b"],
        "row_n": np.concatenate([a["L0_conv_v1_b"], a["L0_conv_ln_w"], a["L0_conv_ln_b"]]),
        "v2_w": a["L0_conv_v2_w"].T, "alpha": a["L3_conv_alpha"].reshape(-1),
        "sign_w": a["L3_conv_weight"].transpose(1, 2, 3, 0),
    }
    return {k: np.ascontiguousarray(v).reshape(-1) for k, v in out.items()}
```
